# Optimizing a Trainium2 kernel written in Bass

```python
import numpy as np
import jax
import jax.numpy as jnp

def _softmax(x, axis=-1):
    return jax.nn.softmax(x, axis=axis)

def _gelu(x):
    return jax.nn.gelu(x, approximate=True)

def _silu(x):
    return jax.nn.silu(x)

def _sigmoid(x):
    return jax.nn.sigmoid(x)

def _layernorm(x, axis=-1, eps=1e-05):
    m = jnp.mean(x, axis=axis, keepdims=True)
    v = jnp.var(x, axis=axis, keepdims=True)
    return (x - m) / jnp.sqrt(v + eps)

def _scatter_add(tgt, idx, src, axis=0):
    return tgt.at[idx].add(src)

def _segment_sum(src, seg, n):
    return jax.ops.segment_sum(src, seg, n)
kernel_name = 'mk_flamingo_gated_d2_seqx_r8_b98d10'

def setup_inputs(seed: int=0):
    np.random.seed(seed)
    _w = jnp.asarray

    def _rec_inputs():
        import jax
        import jax.numpy as jnp
        _rk = jax.random.key(seed)
        x = -0.0002928 + 1 * jax.random.normal(jax.random.fold_in(_rk, 1), (32, 128, 128), jnp.float32)
        _lenS = 128 - jax.random.randint(jax.random.fold_in(_rk, 7), (32,), 0, max(1, 128 // 4) + 1, jnp.int32)
        _lenS2 = 128 - jax.random.randint(jax.random.fold_in(_rk, 8), (32,), 0, max(1, 128 // 4) + 1, jnp.int32)
        _ctx_1024P = jax.random.normal(jax.random.fold_in(_rk, 11), (32, 16, 128), jnp.float32)
        _ctx_1024c = jax.random.dirichlet(jax.random.fold_in(_rk, 511), 0.3 * jnp.ones((16,), jnp.float32), (32, 128))
        _ctx_1024t = jnp.einsum('bsk,bkd->bsd', _ctx_1024c, _ctx_1024P)
        _ctx_1024t = _ctx_1024t * jax.lax.rsqrt(jnp.mean(jnp.square(_ctx_1024t)) + 1e-12) * 0.953939
        ctx_1024 = -1.39393e-06 + 0.999914 * (_ctx_1024t + 0.3 * jax.random.normal(jax.random.fold_in(_rk, 611), (32, 128, 128), jnp.float32))
        _g = jax.random.normal(jax.random.fold_in(_rk, 9001), (2, 2), jnp.float32)
        _g = jnp.sign(_g) * jnp.maximum(jnp.abs(_g), 1.0) + (_g == 0) * 1.0
        g_xattn = _g[0]
        g_ffn = _g[1]
        return (x, ctx_1024, g_xattn, g_ffn)
    x, ctx_1024, g_xattn, g_ffn = _rec_inputs()

    def _L0_xattn_setup():
        import jax, jax.numpy as jnp
        import numpy as np
        D_MODEL = 128
        NUM_HEADS = 16
        HEAD_DIM = D_MODEL // NUM_HEADS
        key = jax.random.key(seed)
        ks = jax.random.split(key, 11)
        B, S, D = (2, 256, D_MODEL)
        s = 1.0 / np.sqrt(D)
        inp = {'query': jax.random.normal(ks[0], (B, S, D), jnp.float32), 'key': jax.random.normal(ks[1], (B, S, D), jnp.float32), 'value': jax.random.normal(ks[2], (B, S, D), jnp.float32), 'Wq': jax.random.normal(ks[3], (D, D), jnp.float32) * s, 'bq': jnp.zeros((D,), jnp.float32), 'Wk': jax.random.normal(ks[4], (D, D), jnp.float32) * s, 'bk': jnp.zeros((D,), jnp.float32), 'Wv': jax.random.normal(ks[5], (D, D), jnp.float32) * s, 'bv': jnp.zeros((D,), jnp.float32), 'Wo': jax.random.normal(ks[6], (D, D), jnp.float32) * s, 'bo': jnp.zeros((D,), jnp.float32)}
        return inp
    _L0_xattn_all = _L0_xattn_setup()
    _L0_xattn_in = {k: v for k, v in _L0_xattn_all.items() if k in ('Wq', 'bq', 'Wk', 'bk', 'Wv', 'bv', 'Wo', 'bo')}
    del _L0_xattn_all

    def _L0_ffn_setup():
        import jax, jax.numpy as jnp
        import numpy as np
        MICRO_BATCHES = 2
        TOP_K = 2
        NUM_EXPERTS = 8
        B, S, D = (4, 512, 128)
        H = 4 * D
        key = jax.random.key(seed)
        ks = jax.random.split(key, 8)
        s = 0.02
        return {'x': jax.random.normal(ks[0], (B, S, D), jnp.float32), 'ln_scale': jnp.ones((D,), jnp.float32), 'ln_bias': jnp.zeros((D,), jnp.float32), 'attn_w': jax.random.normal(ks[1], (D, D), jnp.float32) * s, 'attn_b': jnp.zeros((D,), jnp.float32), 'gate_w': jax.random.normal(ks[2], (NUM_EXPERTS, D), jnp.float32) * s, 'w1': jax.random.normal(ks[3], (NUM_EXPERTS, D, H), jnp.float32) * s, 'b1': jnp.zeros((NUM_EXPERTS, H), jnp.float32), 'w2': jax.random.normal(ks[4], (NUM_EXPERTS, H, D), jnp.float32) * s, 'b2': jnp.zeros((NUM_EXPERTS, D), jnp.float32), 'next_w': jax.random.normal(ks[5], (D, D), jnp.float32) * s, 'next_b': jnp.zeros((D,), jnp.float32)}
    _L0_ffn_all = _L0_ffn_setup()
    _L0_ffn_in = {k: v for k, v in _L0_ffn_all.items() if k in ('ln_scale', 'ln_bias', 'attn_w', 'attn_b', 'gate_w', 'w1', 'b1', 'w2', 'b2', 'next_w', 'next_b')}
    del _L0_ffn_all

    def _L1_xattn_setup():
        import jax, jax.numpy as jnp
        import numpy as np
        B, N, D_MODEL, H, DH = (2, 256, 128, 16, 64)
        SCALE = DH ** (-0.5)
        key = jax.random.key(seed)
        ks = jax.random.split(key, 6)

        def lin(k, fan_in, shape):
            return jax.random.normal(k, shape, dtype=jnp.float32) / np.sqrt(fan_in)
        return {'x': jax.random.normal(ks[0], (B, N, D_MODEL), dtype=jnp.float32), 'context': jax.random.normal(ks[1], (B, N, D_MODEL), dtype=jnp.float32), 'Wq': lin(ks[2], D_MODEL, (D_MODEL, H * DH)), 'Wk': lin(ks[3], D_MODEL, (D_MODEL, H * DH)), 'Wv': lin(ks[4], D_MODEL, (D_MODEL, H * DH)), 'Wo': lin(ks[5], H * DH, (H * DH, D_MODEL)), 'bo': jnp.zeros((D_MODEL,), dtype=jnp.float32)}
    _L1_xattn_all = _L1_xattn_setup()
    _L1_xattn_in = {k: v for k, v in _L1_xattn_all.items() if k in ('Wq', 'Wk', 'Wv', 'Wo', 'bo')}
    del _L1_xattn_all

    def _L1_ffn_setup():
        import jax, jax.numpy as jnp
        import numpy as np
        S, B, H, I, E = (64, 2, 128, 352, 8)
        key = jax.random.key(seed)
        ks = jax.random.split(key, 5)
        return {'hidden_states': jax.random.normal(ks[0], (S, B, H), dtype=jnp.float32), 'router_w': jax.random.normal(ks[1], (E, H), dtype=jnp.float32) * 0.02, 'gate_w': jax.random.normal(ks[2], (E, I, H), dtype=jnp.float32) * 0.02, 'up_w': jax.random.normal(ks[3], (E, I, H), dtype=jnp.float32) * 0.02, 'down_w': jax.random.normal(ks[4], (E, H, I), dtype=jnp.float32) * 0.02}
    _L1_ffn_all = _L1_ffn_setup()
    _L1_ffn_in = {k: v for k, v in _L1_ffn_all.items() if k in ('router_w', 'gate_w', 'up_w', 'down_w')}
    del _L1_ffn_all
    return {'x': x, 'ctx_1024': ctx_1024, 'g_xattn': g_xattn, 'g_ffn': g_ffn, 'L0_xattn_Wq': _L0_xattn_in['Wq'], 'L0_xattn_bq': _L0_xattn_in['bq'], 'L0_xattn_Wk': _L0_xattn_in['Wk'], 'L0_xattn_bk': _L0_xattn_in['bk'], 'L0_xattn_Wv': _L0_xattn_in['Wv'], 'L0_xattn_bv': _L0_xattn_in['bv'], 'L0_xattn_Wo': _L0_xattn_in['Wo'], 'L0_xattn_bo': _L0_xattn_in['bo'], 'L0_ffn_ln_scale': _L0_ffn_in['ln_scale'], 'L0_ffn_ln_bias': _L0_ffn_in['ln_bias'], 'L0_ffn_attn_w': _L0_ffn_in['attn_w'], 'L0_ffn_attn_b': _L0_ffn_in['attn_b'], 'L0_ffn_gate_w': _L0_ffn_in['gate_w'], 'L0_ffn_w1': _L0_ffn_in['w1'], 'L0_ffn_b1': _L0_ffn_in['b1'], 'L0_ffn_w2': _L0_ffn_in['w2'], 'L0_ffn_b2': _L0_ffn_in['b2'], 'L0_ffn_next_w': _L0_ffn_in['next_w'], 'L0_ffn_next_b': _L0_ffn_in['next_b'], 'L1_xattn_Wq': _L1_xattn_in['Wq'], 'L1_xattn_Wk': _L1_xattn_in['Wk'], 'L1_xattn_Wv': _L1_xattn_in['Wv'], 'L1_xattn_Wo': _L1_xattn_in['Wo'], 'L1_xattn_bo': _L1_xattn_in['bo'], 'L1_ffn_router_w': _L1_ffn_in['router_w'], 'L1_ffn_gate_w': _L1_ffn_in['gate_w'], 'L1_ffn_up_w': _L1_ffn_in['up_w'], 'L1_ffn_down_w': _L1_ffn_in['down_w']}

def reference(x, ctx_1024, g_xattn, g_ffn, L0_xattn_Wq, L0_xattn_bq, L0_xattn_Wk, L0_xattn_bk, L0_xattn_Wv, L0_xattn_bv, L0_xattn_Wo, L0_xattn_bo, L0_ffn_ln_scale, L0_ffn_ln_bias, L0_ffn_attn_w, L0_ffn_attn_b, L0_ffn_gate_w, L0_ffn_w1, L0_ffn_b1, L0_ffn_w2, L0_ffn_b2, L0_ffn_next_w, L0_ffn_next_b, L1_xattn_Wq, L1_xattn_Wk, L1_xattn_Wv, L1_xattn_Wo, L1_xattn_bo, L1_ffn_router_w, L1_ffn_gate_w, L1_ffn_up_w, L1_ffn_down_w):
    import jax
    import jax.numpy as jnp

    def _L0_xattn_ref(query, key, value, Wq, bq, Wk, bk, Wv, bv, Wo, bo):
        import jax, jax.numpy as jnp
        import numpy as np
        D_MODEL = 128
        NUM_HEADS = 16
        HEAD_DIM = D_MODEL // NUM_HEADS
        B, S, D = query.shape
        H, Hd = (NUM_HEADS, HEAD_DIM)
        Q = (query @ Wq.T + bq).reshape(B, S, H, Hd).transpose(0, 2, 1, 3)
        K = (key @ Wk.T + bk).reshape(B, S, H, Hd).transpose(0, 2, 1, 3)
        V = (value @ Wv.T + bv).reshape(B, S, H, Hd).transpose(0, 2, 1, 3)
        scale = 1.0 / jnp.sqrt(jnp.asarray(Hd, Q.dtype))
        scores = jnp.einsum('bhqd,bhkd->bhqk', Q, K) * scale
        attn = jax.nn.softmax(scores, axis=-1)
        out = jnp.einsum('bhqk,bhkd->bhqd', attn, V)
        out = out.transpose(0, 2, 1, 3).reshape(B, S, D)
        return out @ Wo.T + bo

    def _L0_ffn_ref(x, ln_scale, ln_bias, attn_w, attn_b, gate_w, w1, b1, w2, b2, next_w, next_b):
        import jax, jax.numpy as jnp
        import numpy as np
        MICRO_BATCHES = 2
        TOP_K = 2
        NUM_EXPERTS = 8
        B, S, D = (4, 512, 128)
        H = 4 * D
        b, s, d = x.shape
        flat = x.reshape(b * s, d)
        mu = jnp.mean(flat, axis=-1, keepdims=True)
        var = jnp.mean((flat - mu) ** 2, axis=-1, keepdims=True)
        xn = (flat - mu) * jax.lax.rsqrt(var + 1e-05) * ln_scale + ln_bias
        x_attn = xn @ attn_w.T + attn_b + flat
        logits = x_attn @ gate_w.T
        _vals, _idx = jax.lax.top_k(logits, TOP_K)
        e = w1.shape[0]
        n = b * s // (MICRO_BATCHES * e)
        xe = x_attn.reshape(MICRO_BATCHES, e, n, d)
        h = jax.nn.gelu(jnp.einsum('mend,edh->menh', xe, w1) + b1[None, :, None, :], approximate=False)
        eo = jnp.einsum('menh,ehd->mend', h, w2) + b2[None, :, None, :]
        eo = eo.reshape(b * s, d)
        out = jax.nn.gelu(eo @ next_w.T + next_b, approximate=False)
        return out.reshape(b, s, d)

    def _L1_xattn_ref(x, context, Wq, Wk, Wv, Wo, bo):
        import jax, jax.numpy as jnp
        import numpy as np
        B, N, D_MODEL, H, DH = (2, 256, 128, 16, 64)
        SCALE = DH ** (-0.5)
        b, n, _ = x.shape
        m = context.shape[1]
        q = (x @ Wq).reshape(b, n, H, DH)
        k = (context @ Wk * SCALE).reshape(b, m, H, DH)
        v = (context @ Wv).reshape(b, m, H, DH)
        scores = jnp.einsum('bihd,bjhd->bhij', q, k)
        attn = jax.nn.softmax(scores, axis=-1)
        out = jnp.einsum('bhij,bjhd->bihd', attn, v)
        out = out.reshape(b, n, H * DH)
        return out @ Wo + bo

    def _L1_ffn_ref(hidden_states, router_w, gate_w, up_w, down_w):
        import jax, jax.numpy as jnp
        import numpy as np
        S, B, H, I, E = (64, 2, 128, 352, 8)
        router_logits = jnp.einsum('sbh,eh->sbe', hidden_states, router_w)
        routing_indices = jnp.argmax(router_logits, axis=-1)
        out = jnp.zeros_like(hidden_states)
        for e in range(E):
            mask = (routing_indices == e)[..., None]
            xe = jnp.where(mask, hidden_states, 0.0)
            g = jnp.einsum('sbh,ih->sbi', xe, gate_w[e])
            u = jnp.einsum('sbh,ih->sbi', xe, up_w[e])
            ye = jnp.einsum('sbi,hi->sbh', jax.nn.silu(g) * u, down_w[e])
            out = out + jnp.where(mask, ye, 0.0)
        return out
    x = x + jnp.tanh(g_xattn[0]) * _L0_xattn_ref(_layernorm(x, axis=-1), ctx_1024, ctx_1024, L0_xattn_Wq, L0_xattn_bq, L0_xattn_Wk, L0_xattn_bk, L0_xattn_Wv, L0_xattn_bv, L0_xattn_Wo, L0_xattn_bo)
    x = x + jnp.tanh(g_ffn[0]) * _L0_ffn_ref(_layernorm(x, axis=-1), L0_ffn_ln_scale, L0_ffn_ln_bias, L0_ffn_attn_w, L0_ffn_attn_b, L0_ffn_gate_w, L0_ffn_w1, L0_ffn_b1, L0_ffn_w2, L0_ffn_b2, L0_ffn_next_w, L0_ffn_next_b)
    x = x + jnp.tanh(g_xattn[1]) * _L1_xattn_ref(_layernorm(x, axis=-1), ctx_1024, L1_xattn_Wq, L1_xattn_Wk, L1_xattn_Wv, L1_xattn_Wo, L1_xattn_bo)
    x = x + jnp.tanh(g_ffn[1]) * _L1_ffn_ref(_layernorm(x, axis=-1), L1_ffn_router_w, L1_ffn_gate_w, L1_ffn_up_w, L1_ffn_down_w)
    return x

_drawn_inputs = setup_inputs


def setup_inputs(seed=0):
    import zlib

    import numpy as np

    out = dict(_drawn_inputs(seed))
    spreads = {'g_ffn': (-1.0, 0.6),
     'L0_xattn_bq': (0.0, 0.509),
     'L0_xattn_bk': (0.0, 0.8),
     'L0_xattn_bv': (0.0, 0.1),
     'L0_xattn_bo': (0.0, 0.1),
     'L0_ffn_ln_scale': (1.0, 0.6),
     'L0_ffn_ln_bias': (0.0, 0.8),
     'L0_ffn_attn_b': (0.0, 0.8),
     'L0_ffn_b1': (0.0, 0.8),
     'L0_ffn_b2': (0.0, 0.8),
     'L0_ffn_next_b': (0.0, 0.1),
     'L1_xattn_bo': (0.0, 0.1)}
    factors = {'L0_ffn_attn_w': 8.0,
     'L0_ffn_w1': 8.0,
     'L0_ffn_w2': 8.0,
     'L0_ffn_next_w': 6.797,
     'L1_ffn_router_w': 8.0,
     'L1_ffn_gate_w': 8.0,
     'L1_ffn_up_w': 8.0,
     'L1_ffn_down_w': 8.0}
    for name, (base, spread) in spreads.items():
        noise = np.random.default_rng([zlib.crc32(name.encode()), seed]).standard_normal(out[name].shape)
        drawn = base * np.exp(spread * noise) if base else spread * noise
        out[name] = jnp.asarray(drawn.astype(out[name].dtype))
    for name, factor in factors.items():
        out[name] = (out[name] * factor).astype(out[name].dtype)
    return out
```

```python
from contextlib import ExitStack
import numpy as np
import concourse.bass as bass
from concourse import mybir

ALU = mybir.AluOpType
ACT = mybir.ActivationFunctionType
F32 = mybir.dt.float32
F16 = mybir.dt.float16
BF16 = mybir.dt.bfloat16
AX = mybir.AxisListType

P = 128
B = 32
PAIRS = B // 2
H = 16
D0 = P // H
G = 32
HD1 = 64
E = 8
H0 = 4
I1 = 352
CHUNKS = ((0, 128), (128, 128), (256, 96))
EPS = 1e-5


def both_products(nc, out, pairs, start=True, stop=True):
    last = None
    for n, (lhsT, rhs) in enumerate(pairs):
        last = nc.tensor.matmul(out, lhsT, rhs, start=start and n == 0, stop=stop and n == len(pairs) - 1,
                                skip_group_check=True)
    return last


class Setup:
    pass


def load_and_prepare(nc, ctx, A, k):
    def sb(name, shape, dt=F32):
        return ctx.enter_context(nc.sbuf_tensor(name, shape, dt))

    k.x_sb = sb("x_sb", [P, B + 2, P])
    k.ctx_sb = sb("ctx_sb", [P, B + 2, P])
    k.cT = sb("cT", [P, 2, B, P], F16)
    k.cT_hi, k.cT_lo = k.cT[:, 0], k.cT[:, 1]
    k.ident = sb("ident", [P, P])
    k.gates = sb("gates", [P, 4])
    k.tg = sb("tg", [P, 4])
    k.pick_head = sb("pick_head", [P, H, P], BF16)
    k.stack_sel = sb("stack_sel", [P, 4, H, 4, D0], F16)
    k.ones32 = sb("ones32", [P, G])
    k.w0T_hi = sb("w0T_hi", [P, 3, P], F16)
    k.w0T_lo = sb("w0T_lo", [P, 3, P], F16)
    k.wo0 = sb("wo0", [P, 4, P])
    k.bias0 = sb("bias0", [P, 3])
    k.bv0 = sb("bv0", [P, P])
    k.bo = sb("bo", [P, 2, P])
    k.attn_wT = sb("attn_wT", [P, P])
    k.next_wT = sb("next_wT", [P, P])
    k.ffn_cols = sb("ffn_cols", [P, 4])
    k.b1 = sb("b1", [P, E, H0])
    k.b2 = sb("b2", [P, E])
    k.w1 = sb("w1", [P, E, H0 * P])
    k.w2 = sb("w2", [P, E, H0, P])
    k.A_hi = sb("A_hi", [P, H, P], F16)
    k.A_lo = sb("A_lo", [P, H, P], F16)
    k.M_hi = sb("M_hi", [P, H, P], F16)
    k.M_lo = sb("M_lo", [P, H, P], F16)
    k.gateT = sb("gateT", [P, E, I1])
    k.upT = sb("upT", [P, E, I1])
    k.downT = sb("downT", [P, 3, E, P])
    k.routerT = sb("routerT", [P, E])
    k.x_landed = ctx.enter_context(nc.semaphore("x_landed"))
    k.ffn0_landed = ctx.enter_context(nc.semaphore("ffn0_landed"))

    with ExitStack() as tmp:
        def tb(name, shape, dt=F32):
            return tmp.enter_context(nc.sbuf_tensor(name, shape, dt))

        def sem(name):
            return tmp.enter_context(nc.semaphore(name))

        small = tb("small", [P, 6, P])
        wo_spread = tb("wo_spread", [P, 4, 4, G])
        big = tb("big", [P, 3, H * HD1])
        bigT = tb("bigT", [P, 3, 8, P])
        wo1 = tb("wo1", [P, 8, P])
        router = tb("router", [E, P])
        gu = tb("gu", [P, 2, 3, E, P])
        down = k.cT[:, :, :, :].rearrange("p a b n -> p (a b n)").bitcast(F32)[:, 0:E * I1].rearrange("p (e i) -> p e i", e=E)
        banks = [tmp.enter_context(nc.psum_tensor(f"setup_bank{n}", [P, 512], F32)) for n in range(8)]

        small_landed, big_landed, gu_landed = sem("small_landed"), sem("big_landed"), sem("gu_landed")
        g_landed, tg_ready, zeroed, const_ready = sem("g_landed"), sem("tg_ready"), sem("zeroed"), sem("const_ready")
        spread_ready, moved_ready, evacuated = sem("spread_ready"), sem("moved_ready"), sem("evacuated")
        split_hi = sem("split_hi")

        jobs = []
        for n in range(3):
            jobs.append(("t", small_landed, [(small[:, n, :], P, P)], ("split", k.w0T_hi[:, n, :], k.w0T_lo[:, n, :])))
        jobs.append(("t", spread_ready, [(wo_spread[:, j].rearrange("p c g -> p (c g)"), P, P) for j in range(4)],
                     ("gate", k.wo0[:, :, :].rearrange("p j n -> p (j n)"), 0)))
        for n, dst in ((4, k.attn_wT), (5, k.next_wT)):
            jobs.append(("t", small_landed, [(small[:, n, :], P, P)], ("copy", dst[:, :])))
        jobs.append(("t", small_landed, [(router[:, :], P, E)], ("copy", k.routerT[:, :])))
        for w in range(3):
            for q in range(2):
                jobs.append(("t", big_landed, [(big[:, w, (4 * q + n) * P:(4 * q + n + 1) * P], P, P) for n in range(4)],
                             ("copy", bigT[:, w, 4 * q:4 * q + 4, :].rearrange("p a n -> p (a n)"))))
        bigT_jobs = len(jobs)
        for w, dst in ((0, k.gateT), (1, k.upT)):
            for e in range(E):
                jobs.append(("t", gu_landed, [(gu[0:rows, w, c, e, :], P, rows) for c, (_, rows) in enumerate(CHUNKS)],
                             ("copy", dst[:, e, :])))
        for c, (c0, rows) in enumerate(CHUNKS):
            for q in range(2):
                jobs.append(("t", gu_landed, [(down[:, 4 * q + n, c0:c0 + rows], rows, P) for n in range(4)],
                             ("copy", k.downT[0:rows, c, 4 * q:4 * q + 4, :].rearrange("p a n -> p (a n)"))))
        for q in range(4):
            heads = range(8 * (q // 2) + q % 2, 8 * (q // 2) + 8, 2)
            half = lambda t, w, h: t[HD1 * (h % 2):HD1 * (h % 2) + HD1, w, h // 2, :]
            there = slice(heads[0], heads[0] + 7, 2)
            jobs.append(("m", evacuated, [(half(bigT, 0, h), half(bigT, 1, h)) for h in heads],
                         ("scaled", k.A_hi[:, there, :], k.A_lo[:, there, :])))
            jobs.append(("m", evacuated, [(half(bigT, 2, h), wo1[HD1 * (h % 2):HD1 * (h % 2) + HD1, h // 2, :]) for h in heads],
                         ("gated", k.M_hi[:, there, :], k.M_lo[:, there, :])))

        total = {}

        with nc.Block() as block:
            @block.sync
            def _(sp):
                def load(dst, src, landed):
                    sp.dma_start(dst, src).then_inc(landed, 16)
                    total[landed.name] = total.get(landed.name, 0) + 16

                def on_all(v):
                    return v.rearrange("(a n) -> a n", a=1).broadcast_to([P, v.shape[0]])

                load(k.gates[:, 0:2], on_all(A["g_xattn"]), g_landed)
                load(k.gates[:, 2:4], on_all(A["g_ffn"]), g_landed)
                for n, name in enumerate(("L0_xattn_Wq", "L0_xattn_Wk", "L0_xattn_Wv", "L0_xattn_Wo",
                                          "L0_ffn_attn_w", "L0_ffn_next_w")):
                    load(small[:, n, :], A[name], small_landed)
                load(router[:, :], A["L1_ffn_router_w"], small_landed)
                for b0 in range(0, B, 8):
                    load(k.x_sb[:, b0:b0 + 8, :], A["x"][b0:b0 + 8].rearrange("b t d -> t b d"), k.x_landed)
                    load(k.ctx_sb[:, b0:b0 + 8, :], A["ctx_1024"][b0:b0 + 8].rearrange("b t d -> t b d"), k.x_landed)
                for n, name in enumerate(("L1_xattn_Wq", "L1_xattn_Wk", "L1_xattn_Wv")):
                    load(big[:, n, :], A[name], big_landed)
                load(wo1[:, :, :], A["L1_xattn_Wo"].rearrange("(j p) n -> p j n", p=P), big_landed)
                for w, name in enumerate(("L1_ffn_gate_w", "L1_ffn_up_w")):
                    for c, (c0, rows) in enumerate(CHUNKS):
                        load(gu[0:rows, w, c, :, :], A[name][:, c0:c0 + rows, :].rearrange("e i h -> i e h"), gu_landed)
                load(down, A["L1_ffn_down_w"].rearrange("e h i -> h e i"), gu_landed)

                def column(v):
                    return v.rearrange("(p a) -> p a", a=1)

                load(k.bias0[:, 0:1], column(A["L0_xattn_bq"]), k.x_landed)
                load(k.bias0[:, 1:2], column(A["L0_xattn_bk"]), k.x_landed)
                load(k.bv0[:, :], on_all(A["L0_xattn_bv"]), k.x_landed)
                load(k.bo[:, 0, :], on_all(A["L0_xattn_bo"]), k.x_landed)
                load(k.bo[:, 1, :], on_all(A["L1_xattn_bo"]), k.x_landed)
                for n, name in enumerate(("L0_ffn_ln_scale", "L0_ffn_ln_bias", "L0_ffn_attn_b", "L0_ffn_next_b")):
                    load(k.ffn_cols[:, n:n + 1], column(A[name]), k.ffn0_landed)
                load(k.w1[:, :, :], A["L0_ffn_w1"].rearrange("e d h -> d e h"), k.ffn0_landed)
                load(k.w2[:, :, :, :].rearrange("p e c n -> p (e c) n"),
                     A["L0_ffn_w2"].rearrange("e (c p) n -> p (e c) n", p=P), k.ffn0_landed)
                with nc.allow_non_contiguous_dma(reason="small bias columns"):
                    load(k.b1[:, :, :].rearrange("p e c -> p (e c)"),
                         A["L0_ffn_b1"].rearrange("e (c p) -> p (e c)", p=P), k.ffn0_landed)
                    load(k.b2[:, :], A["L0_ffn_b2"].rearrange("e p -> p e"), k.ffn0_landed)

            k.x_total, k.ffn0_total = total[k.x_landed.name], total[k.ffn0_landed.name]

            @block.gpsimd
            def _(pool):
                nc.gpsimd.memset(k.ident[:, :], 0.0).then_inc(zeroed, 1)
                nc.gpsimd.memset(wo_spread[:, :, :, :], 0.0).then_inc(zeroed, 1)
                nc.gpsimd.memset(k.stack_sel[:, :, :, :, :], 0.0).then_inc(zeroed, 1)
                nc.gpsimd.memset(k.pick_head[:, :, :], 0.0).then_inc(zeroed, 1)
                nc.gpsimd.memset(k.ones32[:, :], 1.0).then_inc(zeroed, 1)
                nc.gpsimd.memset(k.x_sb[:, B:B + 2, :], 0.0).then_inc(zeroed, 1)
                nc.gpsimd.memset(k.ctx_sb[:, B:B + 2, :], 0.0).then_inc(zeroed, 1)
                pool.wait_ge(zeroed, 7)
                nc.gpsimd.affine_select(out=k.ident[:, :], in_=k.ident[:, :], compare_op=ALU.not_equal, fill=1.0,
                                        base=0, pattern=[[-1, P]], channel_multiplier=1).then_inc(const_ready, 1)
                nc.gpsimd.affine_select(out=k.pick_head[:, :, :], in_=k.pick_head[:, :, :], compare_op=ALU.not_equal,
                                        fill=1.0, base=0, pattern=[[-1, H], [0, P]], channel_multiplier=1)\
                    .then_inc(const_ready, 1)
                for n, copies in enumerate((slice(0, 4, 2), slice(1, 4, 2), slice(0, 2), slice(2, 4))):
                    part = k.stack_sel[:, n, :, copies, :]
                    nc.gpsimd.affine_select(out=part, in_=part, compare_op=ALU.not_equal, fill=1.0, base=0,
                                            pattern=[[-D0, H], [0, 2], [-1, D0]], channel_multiplier=1)\
                        .then_inc(const_ready, 1)

            @block.scalar
            def _(act):
                act.wait_ge(g_landed, 32)
                nc.scalar.activation(k.tg[:, :], k.gates[:, :], ACT.Tanh).then_inc(tg_ready, 1)

            @block.tensor
            def _(pe):
                pe.wait_ge(const_ready, 6)
                seen = set()
                for n, (kind, need, parts, target) in enumerate(jobs):
                    if need.name not in seen:
                        seen.add(need.name)
                        pe.wait_ge(need, {spread_ready.name: 1, evacuated.name: bigT_jobs}.get(need.name, total.get(need.name)))
                    if n >= 8:
                        pe.wait_ge(evacuated, n - 7)
                    at = 0
                    for a, b, *c in parts:
                        if kind == "t":
                            rows, width = b, c[0]
                            last = nc.tensor.transpose(banks[n % 8][0:rows, at:at + width], a, k.ident[0:width, 0:width])
                            at += width
                        else:
                            last = nc.tensor.matmul(banks[n % 8][:, at:at + P], a, b, start=True, stop=True)
                            at += P
                    last.then_inc(moved_ready, 1)

            @block.vector
            def _(dve):
                dve.wait_ge(small_landed, total[small_landed.name])
                dve.wait_ge(zeroed, 7)
                nc.vector.tensor_copy(wo_spread[:, :, :, 0:D0],
                                      small[:, 3, :].rearrange("p (j c d) -> p j c d", j=4, c=4)).then_inc(spread_ready, 1)
                dve.wait_ge(tg_ready, 1)
                splits = 0
                for n, (kind, need, parts, target) in enumerate(jobs):
                    dve.wait_ge(moved_ready, n + 1)
                    what, dst = target[0], target[1]
                    width = sum(c[0] if c else P for _, _, *c in parts)
                    src = banks[n % 8][0:dst.shape[0], 0:width]
                    if kind == "m":
                        src = src.rearrange("p (a n) -> p a n", n=P)
                    if what == "copy":
                        nc.vector.tensor_copy(dst, src).then_inc(evacuated, 1)
                    elif what == "gate":
                        nc.vector.tensor_scalar(dst, src, k.tg[:, 0:1], None, ALU.mult).then_inc(evacuated, 1)
                    else:
                        factor = {"split": 1.0, "scaled": float(HD1) ** -0.5, "gated": k.tg[:, 1:2]}[what]
                        nc.vector.tensor_scalar(dst, src, factor, None, ALU.mult).then_inc(split_hi, 1)
                        splits += 1
                        dve.wait_ge(split_hi, splits)
                        nc.vector.scalar_tensor_tensor(out=target[2], in0=src, scalar=factor, in1=dst,
                                                       op0=ALU.mult, op1=ALU.subtract).then_inc(evacuated, 1)
                dve.wait_ge(evacuated, len(jobs))
                dve.wait_ge(const_ready, 6)


def alone(nc, dve, carrier, semaphore, value):
    dve.wait_ge(semaphore, value)
    nc.vector.tensor_copy(carrier[:, 1:2], carrier[:, 0:1])


def normalise(nc, pool, stats, x_b, out, work, s, count):
    nc.gpsimd.tensor_tensor(work[:, 0:1], stats[:, 1:2], work[:, 3:4], ALU.add).then_inc(s, 1)
    nc.gpsimd.tensor_tensor(out, x_b, stats[:, 0:1].broadcast_to([P, P]), ALU.subtract).then_inc(s, 1)
    pool.wait_ge(s, count + 2)
    nc.gpsimd.tensor_tensor(work[:, 1:2], work[:, 0:1], work[:, 2:3], ALU.pow).then_inc(s, 1)
    pool.wait_ge(s, count + 3)
    return nc.gpsimd.tensor_tensor(out, out, work[:, 1:2].broadcast_to([P, P]), ALU.mult)


def first_attention(nc, k):
    with ExitStack() as ctx:
        def sb(name, shape, dt=F32):
            return ctx.enter_context(nc.sbuf_tensor("l0_" + name, shape, dt))

        def sem(name):
            return ctx.enter_context(nc.semaphore("l0_" + name))

        carrier = sb("carrier", [P, 3])
        bn = sb("bn", [P, 2, 6])
        stats = sb("stats", [P, 2, 2])
        work = sb("work", [P, 2, 4])
        xn = sb("xn", [P, 2, 2, P])
        bias_row = sb("bias_row", [P, P])
        T_hi = sb("T_hi", [P, 4, P], F16)
        T_lo = sb("T_lo", [P, 4, P], F16)
        qk_hi = sb("qk_hi", [P, 2, 2 * P], F16)
        qk_lo = sb("qk_lo", [P, 2, 2 * P], F16)
        stack = sb("stack", [P, 2, 4, 2, P], F16)
        V = sb("V", [P, 2, H, G])
        neg_max = sb("neg_max", [P, 2, H])
        neg_maxT = sb("neg_maxT", [P, 2, P], BF16)
        probs = sb("probs", [P, 2, 4, 4, P])
        inv = sb("inv", [P, 2, 4 * P])
        heads_out = sb("heads_out", [P, 2, 4 * P])
        bank = [ctx.enter_context(nc.psum_tensor(f"l0_bank{n}", [P, 4, 512], F32)) for n in range(2)]

        primed, bn_done, stats_ready = sem("primed"), sem("bn_done"), sem("stats_ready")
        norm_step, xn_ready, bias_added = sem("norm_step"), sem("xn_ready"), sem("bias_added")
        T_moved, T_hi_ready, T_lo_ready, kept = sem("T_moved"), sem("T_hi_ready"), sem("T_lo_ready"), sem("kept")
        qk_done, qk_hi_ready, qk_lo_ready = sem("qk_done"), sem("qk_hi_ready"), sem("qk_lo_ready")
        v_done, V_ready = sem("v_done"), sem("V_ready")
        stacked, stack_q, stack_k = sem("stacked"), sem("stack_q"), sem("stack_k")
        scored, max_ready, maxT_moved, maxT_ready = sem("scored"), sem("max_ready"), sem("maxT_moved"), sem("maxT_ready")
        shifted, exp_done = sem("shifted"), sem("exp_done")
        pv_done, inv_ready, heads_ready = sem("pv_done"), sem("inv_ready"), sem("heads_ready")
        projected, x_done = sem("projected"), sem("x_done")

        with nc.Block() as block:
            @block.vector
            def _(dve):
                nc.vector.memset(carrier[:, 2:3], 0.0).then_inc(kept, 1)
                nc.vector.memset(V[:, :, :, :], 1.0).then_inc(primed, 1)
                nc.vector.memset(neg_maxT[:, :, :], 0.0).then_inc(primed, 1)
                nc.vector.memset(work[:, :, 2:3], -0.5).then_inc(primed, 1)
                nc.vector.memset(carrier[:, 0:2], 0.0).then_inc(primed, 1)
                nc.vector.memset(work[:, :, 3:4], EPS).then_inc(primed, 1)
                dve.wait_ge(k.x_landed, k.x_total)
                nc.vector.tensor_scalar(bias_row[:, :], k.bo[:, 0, :], k.tg[:, 0:1], None, ALU.mult).then_inc(primed, 1)
                dve.wait_ge(primed, 6)

                def statistics(i, done):
                    for u in range(2):
                        nc.vector.bn_stats(bn[:, u, :], k.x_sb[:, bass.ds(2 * i + u, 1), :]).then_inc(bn_done, 1)
                    alone(nc, dve, carrier, bn_done, 2 * done + 2)
                    for u in range(2):
                        nc.vector.bn_aggr(stats[:, u, :], bn[:, u, :]).then_inc(stats_ready, 1)

                statistics(0, 0)
                with dve.Fori(0, PAIRS) as i:
                    dve.wait_ge(T_hi_ready, i + 1)
                    nc.vector.tensor_tensor(T_lo[:, :, :].rearrange("p a n -> p (a n)"), bank[0][:, 0, :],
                                            T_hi[:, :, :].rearrange("p a n -> p (a n)"), ALU.subtract).then_inc(T_lo_ready, 1)
                    dve.wait_ge(qk_hi_ready, 2 * i + 2)
                    for n in range(2):
                        nc.vector.scalar_tensor_tensor(out=qk_lo[:, n, :], in0=bank[0][:, 1, n * 256:n * 256 + 256],
                                                       scalar=k.bias0[:, n:n + 1], in1=qk_hi[:, n, :],
                                                       op0=ALU.add, op1=ALU.subtract).then_inc(qk_lo_ready, 1)
                    dve.wait_ge(v_done, i + 1)
                    for u in range(2):
                        nc.vector.tensor_tensor(V[:, u, :, 0:D0], bank[0][:, 2, u * P:u * P + P].rearrange("p (h d) -> p h d", h=H),
                                                k.bv0[:, :].rearrange("p (h d) -> p h d", h=H), ALU.add).then_inc(V_ready, 1)
                    dve.wait_ge(stacked, i + 1)
                    nc.vector.tensor_copy(stack[:, 0].rearrange("p j u n -> p (j u n)"),
                                          bank[1][:, 0:2, :].rearrange("p a n -> p (a n)")).then_inc(stack_q, 1)
                    dve.wait_ge(xn_ready, 4 * i + 4)
                    statistics(i + 1, i + 1)
                    for u in range(2):
                        dve.wait_ge(scored, 2 * i + u + 1)
                        nc.vector.tensor_reduce(neg_max[:, u, :], bank[u][:, :, :].rearrange("p r (j n) -> p r j n", j=4),
                                                AX.X, ALU.max, negate=True).then_inc(max_ready, 1)
                        dve.wait_ge(maxT_moved, 2 * i + u + 1)
                        nc.vector.tensor_copy(neg_maxT[0:H, u, :], bank[u][0:H, 0, 0:P]).then_inc(maxT_ready, 1)
                    for u in range(2):
                        dve.wait_ge(pv_done, 2 * i + u + 1)
                        nc.vector.reciprocal(inv[:, u, :], bank[u][:, 1, :]).then_inc(inv_ready, 1)
                        dve.wait_ge(inv_ready, 2 * i + u + 1)
                        nc.vector.tensor_tensor(heads_out[:, u, :], bank[u][:, 0, :], inv[:, u, :], ALU.mult).then_inc(heads_ready, 1)
                    for u in range(2):
                        dve.wait_ge(projected, 2 * i + u + 1)
                        dve.wait_ge(bias_added, 2 * i + u + 1)
                        x_b = k.x_sb[:, bass.ds(2 * i + u, 1), :]
                        nc.vector.tensor_tensor(x_b.rearrange("p a n -> p (a n)"), bank[u][:, 2, 0:P],
                                                x_b.rearrange("p a n -> p (a n)"), ALU.add).then_inc(x_done, 1)

            @block.gpsimd
            def _(pool):
                pool.wait_ge(primed, 6)

                def one_pair(i, done):
                    for u in range(2):
                        pool.wait_ge(stats_ready, 2 * done + u + 1)
                        x_b = k.x_sb[:, bass.ds(2 * i + u, 1), :].rearrange("p a n -> p (a n)")
                        c_b = k.ctx_sb[:, bass.ds(2 * i + u, 1), :].rearrange("p a n -> p (a n)")
                        normalise(nc, pool, stats[:, u, :], x_b, xn[:, u, 0, :], work[:, u, :], norm_step,
                                  6 * done + 3 * u).then_inc(xn_ready, 1)
                        nc.gpsimd.tensor_copy(xn[:, u, 1, :], c_b).then_inc(xn_ready, 1)

                one_pair(0, 0)
                with pool.Fori(0, PAIRS) as i:
                    pool.wait_ge(xn_ready, 4 * i + 4)
                    pool.wait_ge(T_lo_ready, i + 1)
                    for u in range(2):
                        x_b = k.x_sb[:, bass.ds(2 * i + u, 1), :].rearrange("p a n -> p (a n)")
                        nc.gpsimd.tensor_tensor(x_b, x_b, bias_row[:, :], ALU.add).then_inc(bias_added, 1)
                    for dst, src in ((k.cT_hi, T_hi), (k.cT_lo, T_lo)):
                        nc.gpsimd.tensor_copy(dst[:, bass.ts(i, 2), :], src[:, 1:4:2, :]).then_inc(kept, 1)
                    one_pair(i + 1, i + 1)

            @block.scalar
            def _(act):
                with act.Fori(0, PAIRS) as i:
                    act.wait_ge(T_moved, i + 1)
                    act.wait_ge(kept, 2 * i + 1)
                    nc.scalar.activation(T_hi[:, :, :].rearrange("p a n -> p (a n)"), bank[0][:, 0, :], ACT.Copy).then_inc(T_hi_ready, 1)
                    act.wait_ge(qk_done, i + 1)
                    for n in range(2):
                        nc.scalar.activation(qk_hi[:, n, :], bank[0][:, 1, n * 256:n * 256 + 256], ACT.Identity,
                                             bias=k.bias0[:, n:n + 1]).then_inc(qk_hi_ready, 1)
                    act.wait_ge(stacked, i + 1)
                    nc.scalar.activation(stack[:, 1].rearrange("p j u n -> p (j u n)"),
                                         bank[1][:, 2:4, :].rearrange("p a n -> p (a n)"), ACT.Copy).then_inc(stack_k, 1)
                    for u in range(2):
                        for r in range(4):
                            act.wait_ge(shifted, 8 * i + 4 * u + r + 1)
                            nc.scalar.activation(probs[:, u, r].rearrange("p j n -> p (j n)"), bank[u][:, r, :], ACT.Exp,
                                                 scale=float(D0) ** -0.5).then_inc(exp_done, 1)

            @block.tensor
            def _(pe):
                pe.wait_ge(primed, 6)
                with pe.Fori(0, PAIRS) as i:
                    for u in range(2):
                        pe.wait_ge(xn_ready, 4 * i + 2 * u + 2)
                        for n in range(2):
                            last = nc.tensor.transpose(bank[0][:, 0, (2 * u + n) * P:(2 * u + n + 1) * P], xn[:, u, n, :], k.ident[:, :])
                    last.then_inc(T_moved, 1)
                    pe.wait_ge(T_lo_ready, i + 1)
                    for n in range(2):
                        last = both_products(nc, bank[0][:, 1, n * 256:n * 256 + 256].rearrange("p (u n) -> p u n", u=2),
                                             [(w[:, n, :], t[:, n:4:2, :]) for w, t in ((k.w0T_hi, T_hi), (k.w0T_lo, T_hi), (k.w0T_hi, T_lo))])
                    last.then_inc(qk_done, 1)
                    for u in range(2):
                        last = both_products(nc, bank[0][:, 2, u * P:u * P + P],
                                             [(t[:, 2 * u + 1, :], w[:, 2, :]) for w, t in ((k.w0T_hi, T_hi), (k.w0T_lo, T_hi), (k.w0T_hi, T_lo))])
                    last.then_inc(v_done, 1)
                    pe.wait_ge(qk_lo_ready, 2 * i + 2)
                    for n in range(2):
                        for j in range(4):
                            sel = [k.stack_sel[:, 2 * n + part, 4 * j:4 * j + 4].rearrange("p h c d -> p (h c d)") for part in range(2)]
                            last = both_products(nc, bank[1][:, 2 * n + j // 2, (j % 2) * 256:(j % 2) * 256 + 256],
                                                 [(sel[0], qk_hi[:, n, :]), (sel[1], qk_lo[:, n, :])])
                    last.then_inc(stacked, 1)
                    pe.wait_ge(stack_q, i + 1)
                    pe.wait_ge(stack_k, i + 1)
                    pe.wait_ge(V_ready, 2 * i + 2)
                    for u in range(2):
                        for j in range(4):
                            for r in range(4):
                                rows = slice(G * r, G * r + G)
                                last = nc.tensor.matmul(bank[u][:, r, j * P:j * P + P], stack[rows, 0, j, u, :], stack[rows, 1, j, u, :],
                                                        start=True, stop=True, tile_position=(G * r, 0))
                        last.then_inc(scored, 1)
                    for u in range(2):
                        pe.wait_ge(max_ready, 2 * i + u + 1)
                        nc.tensor.transpose(bank[u][0:H, 0, 0:P], neg_max[:, u, :], k.ident[:, :]).then_inc(maxT_moved, 1)
                        pe.wait_ge(maxT_ready, 2 * i + u + 1)
                        for r in range(4):
                            rows = slice(G * r, G * r + G)
                            for j in range(4):
                                nc.tensor.matmul(bank[u][:, r, j * P:j * P + P], k.pick_head[:, 4 * r + j, :], neg_maxT[:, u, :],
                                                 start=j == 0, stop=False, skip_group_check=True)
                            for j in range(4):
                                last = nc.tensor.matmul(bank[u][:, r, j * P:j * P + P], stack[rows, 1, j, u, :], stack[rows, 0, j, u, :],
                                                        start=False, stop=j == 3, tile_position=(G * r, 0), skip_group_check=True)
                            last.then_inc(shifted, 1)
                    for u in range(2):
                        pe.wait_ge(exp_done, 8 * i + 4 * u + 4)
                        for r in range(4):
                            for j in range(4):
                                nc.tensor.matmul(bank[u][G * r:G * r + G, 0, j * P:j * P + P], V[:, u, 4 * j + r, :], probs[:, u, r, j, :],
                                                 start=True, stop=True, tile_position=(0, G * r))
                        for r in range(4):
                            last = nc.tensor.matmul(bank[u][G * r:G * r + G, 1, :], k.ones32[:, :], probs[:, u, r].rearrange("p j n -> p (j n)"),
                                                    start=True, stop=True, tile_position=(0, G * r))
                        last.then_inc(pv_done, 1)
                    for u in range(2):
                        pe.wait_ge(heads_ready, 2 * i + u + 1)
                        last = both_products(nc, bank[u][:, 2, 0:P],
                                             [(heads_out[:, u, j * P:j * P + P], k.wo0[:, j, :]) for j in range(4)])
                        last.then_inc(projected, 1)
                    pe.wait_ge(x_done, 2 * i + 2)


def first_ffn(nc, k):
    with ExitStack() as ctx:
        def sb(name, shape, dt=F32):
            return ctx.enter_context(nc.sbuf_tensor("f0_" + name, shape, dt))

        def sem(name):
            return ctx.enter_context(nc.semaphore("f0_" + name))

        carrier = sb("carrier", [P, 3])
        bn = sb("bn", [P, 2, 2, 6])
        stats = sb("stats", [P, 2, 2, 2])
        work = sb("work", [P, 2, 2, 4])
        xn = sb("xn", [P, 2, 2, P])
        znT = sb("znT", [P, 2, 2, P])
        xaT = sb("xaT", [P, 2 * P])
        hid = sb("hid", [P, H0, 2 * P])
        eoT = sb("eoT", [P, 2 * P])
        outT = sb("outT", [P, 2 * P])
        bank = [ctx.enter_context(nc.psum_tensor(f"f0_bank{n}", [P, 512], F32)) for n in range(8)]
        names = ("primed bn_done stats_ready norm_step once_ready twice_ready T_moved T_ready attn_done xa_ready "
                 "hid_done hid_ready eo_done eo_ready next_done outT_ready back_done x_done").split()
        (primed, bn_done, stats_ready, norm_step, once_ready, twice_ready, T_moved, T_ready, attn_done, xa_ready,
         hid_done, hid_ready, eo_done, eo_ready, next_done, outT_ready, back_done, x_done) = map(sem, names)
        GROUPS = E

        with nc.Block() as block:
            @block.vector
            def _(dve):
                nc.vector.memset(work[:, :, :, 2:3], -0.5).then_inc(primed, 1)
                nc.vector.memset(carrier[:, 0:2], 0.0).then_inc(primed, 1)
                nc.vector.memset(work[:, :, :, 3:4], EPS).then_inc(primed, 1)
                dve.wait_ge(k.ffn0_landed, k.ffn0_total)
                dve.wait_ge(primed, 3)
                with dve.Fori(0, 2) as m:
                    for e in range(E):
                        g = m * GROUPS + e
                        for u in range(2):
                            x_b = k.x_sb[:, bass.ds(2 * g + u, 1), :]
                            nc.vector.bn_stats(bn[:, u, 0, :], x_b).then_inc(bn_done, 1)
                        alone(nc, dve, carrier, bn_done, 4 * g + 2)
                        for u in range(2):
                            nc.vector.bn_aggr(stats[:, u, 0, :], bn[:, u, 0, :]).then_inc(stats_ready, 1)
                        for u in range(2):
                            dve.wait_ge(once_ready, 2 * g + u + 1)
                            nc.vector.bn_stats(bn[:, u, 1, :], xn[:, u, 0, :]).then_inc(bn_done, 1)
                        alone(nc, dve, carrier, bn_done, 4 * g + 4)
                        for u in range(2):
                            nc.vector.bn_aggr(stats[:, u, 1, :], bn[:, u, 1, :]).then_inc(stats_ready, 1)
                        dve.wait_ge(T_moved, g + 1)
                        T = bank[0][:, :].rearrange("p (w n) -> p w n", w=2)
                        nc.vector.tensor_copy(znT[:, 0].rearrange("p u n -> p (u n)"), T[:, 0, :]).then_inc(T_ready, 1)
                        nc.vector.tensor_scalar(znT[:, 1].rearrange("p u n -> p (u n)"), T[:, 1, :], k.ffn_cols[:, 0:1],
                                                k.ffn_cols[:, 1:2], ALU.mult, ALU.add).then_inc(T_ready, 1)
                        dve.wait_ge(attn_done, g + 1)
                        dve.wait_ge(T_ready, 2 * g + 2)
                        nc.vector.scalar_tensor_tensor(out=xaT[:, :], in0=bank[1][:, 0:2 * P], scalar=k.ffn_cols[:, 2:3],
                                                       in1=znT[:, 0].rearrange("p u n -> p (u n)"), op0=ALU.add,
                                                       op1=ALU.add).then_inc(xa_ready, 1)
                        dve.wait_ge(eo_done, g + 1)
                        nc.vector.tensor_scalar(eoT[:, :], bank[6][:, 0:2 * P], k.b2[:, e:e + 1], None, ALU.add).then_inc(eo_ready, 1)
                        dve.wait_ge(back_done, g + 1)
                        for u in range(2):
                            x_b = k.x_sb[:, bass.ds(2 * g + u, 1), :].rearrange("p a n -> p (a n)")
                            nc.vector.scalar_tensor_tensor(out=x_b, in0=bank[0][:, u * P:u * P + P], scalar=k.tg[:, 2:3],
                                                           in1=x_b, op0=ALU.mult, op1=ALU.add).then_inc(x_done, 1)

            @block.gpsimd
            def _(pool):
                pool.wait_ge(primed, 3)
                with pool.Fori(0, 2) as m:
                    for e in range(E):
                        g = m * GROUPS + e
                        for u in range(2):
                            x_b = k.x_sb[:, bass.ds(2 * g + u, 1), :].rearrange("p a n -> p (a n)")
                            pool.wait_ge(stats_ready, 4 * g + u + 1)
                            normalise(nc, pool, stats[:, u, 0, :], x_b, xn[:, u, 0, :], work[:, u, 0, :], norm_step,
                                      12 * g + 3 * u).then_inc(once_ready, 1)
                        for u in range(2):
                            pool.wait_ge(stats_ready, 4 * g + u + 3)
                            normalise(nc, pool, stats[:, u, 1, :], xn[:, u, 0, :], xn[:, u, 1, :], work[:, u, 1, :], norm_step,
                                      12 * g + 3 * u + 6).then_inc(twice_ready, 1)

            @block.scalar
            def _(act):
                act.wait_ge(k.ffn0_landed, k.ffn0_total)
                with act.Fori(0, 2) as m:
                    for e in range(E):
                        g = m * GROUPS + e
                        for c in range(H0):
                            act.wait_ge(hid_done, 4 * g + c + 1)
                            nc.scalar.activation(hid[:, c, :], bank[2 + c][:, 0:2 * P], ACT.Gelu, bias=k.b1[:, e, c:c + 1])\
                                .then_inc(hid_ready, 1)
                        act.wait_ge(next_done, g + 1)
                        nc.scalar.activation(outT[:, :], bank[7][:, 0:2 * P], ACT.Gelu, bias=k.ffn_cols[:, 3:4]).then_inc(outT_ready, 1)

            @block.tensor
            def _(pe):
                pe.wait_ge(k.ffn0_landed, k.ffn0_total)
                with pe.Fori(0, 2) as m:
                    for e in range(E):
                        g = m * GROUPS + e
                        pe.wait_ge(twice_ready, 2 * g + 2)
                        for w in range(2):
                            for u in range(2):
                                last = nc.tensor.transpose(bank[0][:, w * 256 + u * P:w * 256 + u * P + P], xn[:, u, w, :], k.ident[:, :])
                        last.then_inc(T_moved, 1)
                        pe.wait_ge(T_ready, 2 * g + 2)
                        nc.tensor.matmul(bank[1][:, 0:2 * P], k.attn_wT[:, :], znT[:, 1].rearrange("p u n -> p (u n)"),
                                         start=True, stop=True).then_inc(attn_done, 1)
                        pe.wait_ge(xa_ready, g + 1)
                        for c in range(H0):
                            nc.tensor.matmul(bank[2 + c][:, 0:2 * P], k.w1[:, e, c * P:c * P + P], xaT[:, :],
                                             start=True, stop=True).then_inc(hid_done, 1)
                        for c in range(H0):
                            pe.wait_ge(hid_ready, 4 * g + c + 1)
                            last = nc.tensor.matmul(bank[6][:, 0:2 * P], k.w2[:, e, c, :], hid[:, c, :],
                                                    start=c == 0, stop=c == H0 - 1)
                        last.then_inc(eo_done, 1)
                        pe.wait_ge(eo_ready, g + 1)
                        nc.tensor.matmul(bank[7][:, 0:2 * P], k.next_wT[:, :], eoT[:, :], start=True, stop=True).then_inc(next_done, 1)
                        pe.wait_ge(outT_ready, g + 1)
                        for u in range(2):
                            last = nc.tensor.transpose(bank[0][:, u * P:u * P + P], outT[:, u * P:u * P + P], k.ident[:, :])
                        last.then_inc(back_done, 1)
                        pe.wait_ge(x_done, 2 * g + 2)


def second_attention(nc, k):
    with ExitStack() as ctx:
        def sb(name, shape, dt=F32):
            return ctx.enter_context(nc.sbuf_tensor("l1_" + name, shape, dt))

        def sem(name):
            return ctx.enter_context(nc.semaphore("l1_" + name))

        carrier = sb("carrier", [P, 3])
        bn = sb("bn", [P, 2, 6])
        stats = sb("stats", [P, 2, 2])
        work = sb("work", [P, 2, 4])
        xn = sb("xn", [P, 2, P])
        bias_row = sb("bias_row", [P, P])
        T_hi = sb("T_hi", [P, 2, P], F16)
        T_lo = sb("T_lo", [P, 2, P], F16)
        Y_hi = sb("Y_hi", [P, H, 2, P], F16)
        Y_lo = sb("Y_lo", [P, H, 2, P], F16)
        Z = sb("Z", [P, 2, H, P + 1])
        neg_max = sb("neg_max", [P, 2, H])
        neg_maxT = sb("neg_maxT", [P, 2, P], BF16)
        probs = sb("probs", [P, 2, H, P])
        inv = sb("inv", [P, 2, H])
        acc = sb("acc", [P, 2, P])
        bank = [ctx.enter_context(nc.psum_tensor(f"l1_bank{n}", [P, 4, 512], F32)) for n in range(2)]
        names = ("primed bn_done stats_ready norm_step xn_ready bias_added T_moved T_hi_ready T_lo_ready y_done Y_hi_ready "
                 "Y_lo_ready z_done Z_ready scored max_ready maxT_moved maxT_ready shifted exp_done pv_done inv_ready "
                 "summed x_done").split()
        (primed, bn_done, stats_ready, norm_step, xn_ready, bias_added, T_moved, T_hi_ready, T_lo_ready, y_done, Y_hi_ready,
         Y_lo_ready, z_done, Z_ready, scored, max_ready, maxT_moved, maxT_ready, shifted, exp_done, pv_done, inv_ready,
         summed, x_done) = map(sem, names)

        with nc.Block() as block:
            @block.vector
            def _(dve):
                nc.vector.memset(Z[:, :, :, P:P + 1], 1.0).then_inc(primed, 1)
                nc.vector.memset(neg_maxT[:, :, :], 0.0).then_inc(primed, 1)
                nc.vector.memset(work[:, :, 2:3], -0.5).then_inc(primed, 1)
                nc.vector.memset(carrier[:, 0:2], 0.0).then_inc(primed, 1)
                nc.vector.memset(work[:, :, 3:4], EPS).then_inc(primed, 1)
                nc.vector.tensor_scalar(bias_row[:, :], k.bo[:, 1, :], k.tg[:, 1:2], None, ALU.mult).then_inc(primed, 1)
                dve.wait_ge(primed, 6)

                def statistics(i, done):
                    for u in range(2):
                        nc.vector.bn_stats(bn[:, u, :], k.x_sb[:, bass.ds(2 * i + u, 1), :]).then_inc(bn_done, 1)
                    alone(nc, dve, carrier, bn_done, 2 * done + 2)
                    for u in range(2):
                        nc.vector.bn_aggr(stats[:, u, :], bn[:, u, :]).then_inc(stats_ready, 1)

                statistics(0, 0)
                with dve.Fori(0, PAIRS) as i:
                    dve.wait_ge(T_hi_ready, i + 1)
                    nc.vector.tensor_tensor(T_lo[:, :, :].rearrange("p a n -> p (a n)"), bank[0][:, 0, 0:2 * P],
                                            T_hi[:, :, :].rearrange("p a n -> p (a n)"), ALU.subtract).then_inc(T_lo_ready, 1)
                    for n in range(8):
                        dve.wait_ge(Y_hi_ready, 8 * i + n + 1)
                        nc.vector.tensor_tensor(Y_lo[:, 2 * n:2 * n + 2].rearrange("p h u n -> p (h u n)"), bank[1 - n // 4][:, n % 4, :],
                                                Y_hi[:, 2 * n:2 * n + 2].rearrange("p h u n -> p (h u n)"),
                                                ALU.subtract).then_inc(Y_lo_ready, 1)
                    dve.wait_ge(xn_ready, 2 * i + 2)
                    statistics(i + 1, i + 1)
                    for u in range(2):
                        dve.wait_ge(scored, 2 * i + u + 1)
                        nc.vector.tensor_reduce(neg_max[:, u, :], bank[u][:, :, :].rearrange("p r (j n) -> p r j n", j=4),
                                                AX.X, ALU.max, negate=True).then_inc(max_ready, 1)
                        dve.wait_ge(maxT_moved, 2 * i + u + 1)
                        nc.vector.tensor_copy(neg_maxT[0:H, u, :], bank[u][0:H, 0, 0:P]).then_inc(maxT_ready, 1)
                    for u in range(2):
                        x_b = k.x_sb[:, bass.ds(2 * i + u, 1), :].rearrange("p a n -> p (a n)")
                        for n in range(8):
                            O = bank[u][:, n % 4, 0:2 * (P + 1)].rearrange("p (h n) -> p h n", h=2)
                            dve.wait_ge(pv_done, 16 * i + 8 * u + n + 1)
                            nc.vector.reciprocal(inv[:, u, 2 * n:2 * n + 2], O[:, :, P]).then_inc(inv_ready, 1)
                            dve.wait_ge(inv_ready, 16 * i + 8 * u + n + 1)
                            if n == 0:
                                dve.wait_ge(bias_added, 2 * i + u + 1)
                            for h in range(2):
                                first, last = n + h == 0, n == 7 and h == 1
                                if not first:
                                    dve.wait_ge(summed, 30 * i + 15 * u + 2 * n + h)
                                nc.vector.scalar_tensor_tensor(
                                    out=x_b if last else acc[:, u, :], in0=O[:, h, 0:P], scalar=inv[:, u, 2 * n + h:2 * n + h + 1],
                                    in1=x_b if first else acc[:, u, :], op0=ALU.mult, op1=ALU.add)\
                                    .then_inc(x_done if last else summed, 1)

            @block.gpsimd
            def _(pool):
                pool.wait_ge(primed, 6)

                def one_pair(i, done):
                    for u in range(2):
                        pool.wait_ge(stats_ready, 2 * done + u + 1)
                        x_b = k.x_sb[:, bass.ds(2 * i + u, 1), :].rearrange("p a n -> p (a n)")
                        normalise(nc, pool, stats[:, u, :], x_b, xn[:, u, :], work[:, u, :], norm_step,
                                  6 * done + 3 * u).then_inc(xn_ready, 1)

                one_pair(0, 0)
                with pool.Fori(0, PAIRS) as i:
                    pool.wait_ge(xn_ready, 2 * i + 2)
                    for u in range(2):
                        x_b = k.x_sb[:, bass.ds(2 * i + u, 1), :].rearrange("p a n -> p (a n)")
                        nc.gpsimd.tensor_tensor(x_b, x_b, bias_row[:, :], ALU.add).then_inc(bias_added, 1)
                    pool.wait_ge(T_moved, i + 1)
                    one_pair(i + 1, i + 1)

            @block.scalar
            def _(act):
                act.wait_ge(primed, 6)
                with act.Fori(0, PAIRS) as i:
                    act.wait_ge(T_moved, i + 1)
                    nc.scalar.activation(T_hi[:, :, :].rearrange("p a n -> p (a n)"), bank[0][:, 0, 0:2 * P], ACT.Copy).then_inc(T_hi_ready, 1)
                    for n in range(8):
                        act.wait_ge(y_done, 8 * i + n + 1)
                        nc.scalar.activation(Y_hi[:, 2 * n:2 * n + 2].rearrange("p h u n -> p (h u n)"), bank[1 - n // 4][:, n % 4, :],
                                             ACT.Copy).then_inc(Y_hi_ready, 1)
                    for u in range(2):
                        for q in range(4):
                            act.wait_ge(z_done, 8 * i + 4 * u + q + 1)
                            nc.scalar.activation(Z[:, u, 4 * q:4 * q + 4, 0:P], bank[1 - u][:, q, :].rearrange("p (h n) -> p h n", h=4),
                                                 ACT.Copy).then_inc(Z_ready, 1)
                    for u in range(2):
                        for q in range(4):
                            act.wait_ge(shifted, 8 * i + 4 * u + q + 1)
                            nc.scalar.activation(probs[:, u, 4 * q:4 * q + 4, :].rearrange("p h n -> p (h n)"), bank[u][:, q, :],
                                                 ACT.Exp).then_inc(exp_done, 1)

            @block.tensor
            def _(pe):
                pe.wait_ge(primed, 6)
                with pe.Fori(0, PAIRS) as i:
                    for u in range(2):
                        pe.wait_ge(xn_ready, 2 * i + u + 1)
                        last = nc.tensor.transpose(bank[0][:, 0, u * P:u * P + P], xn[:, u, :], k.ident[:, :])
                    last.then_inc(T_moved, 1)
                    pe.wait_ge(T_lo_ready, i + 1)
                    for n in range(8):
                        for h in range(2):
                            last = both_products(nc, bank[1 - n // 4][:, n % 4, h * 256:h * 256 + 256],
                                                 [(w[:, 2 * n + h, :], t[:, :, :].rearrange("p u n -> p (u n)"))
                                                  for w, t in ((k.A_hi, T_hi), (k.A_lo, T_hi), (k.A_hi, T_lo))])
                        last.then_inc(y_done, 1)
                    for u in range(2):
                        c_hi, c_lo = (c[:, bass.ds(2 * i + u, 1), :].rearrange("p a n -> p (a n)") for c in (k.cT_hi, k.cT_lo))
                        for q in range(4):
                            pe.wait_ge(Y_lo_ready, 8 * i + 4 * u + q + 1)
                            last = both_products(nc, bank[1 - u][:, q, :],
                                                 [(c, w[:, 4 * q:4 * q + 4, :].rearrange("p h n -> p (h n)"))
                                                  for c, w in ((c_hi, k.M_hi), (c_hi, k.M_lo), (c_lo, k.M_hi))])
                            last.then_inc(z_done, 1)
                    pe.wait_ge(Z_ready, 8 * i + 8)
                    for u in range(2):
                        c_hi = k.cT_hi[:, bass.ds(2 * i + u, 1), :].rearrange("p a n -> p (a n)")
                        for h in range(H):
                            last = nc.tensor.matmul(bank[u][:, h // 4, (h % 4) * P:(h % 4) * P + P], Y_hi[:, h, u, :], c_hi,
                                                    start=True, stop=True)
                        last.then_inc(scored, 1)
                    for u in range(2):
                        c_hi, c_lo = (c[:, bass.ds(2 * i + u, 1), :].rearrange("p a n -> p (a n)") for c in (k.cT_hi, k.cT_lo))
                        pe.wait_ge(max_ready, 2 * i + u + 1)
                        nc.tensor.transpose(bank[u][0:H, 0, 0:P], neg_max[:, u, :], k.ident[:, :]).then_inc(maxT_moved, 1)
                        pe.wait_ge(maxT_ready, 2 * i + u + 1)
                        for q in range(4):
                            out = bank[u][:, q, :]
                            for h in range(4):
                                nc.tensor.matmul(out[:, h * P:h * P + P], k.pick_head[:, 4 * q + h, :], neg_maxT[:, u, :],
                                                 start=h == 0, stop=False, skip_group_check=True)
                            last = both_products(nc, out.rearrange("p (h n) -> p h n", h=4),
                                                 [(c, y[:, 4 * q:4 * q + 4, u, :]) for c, y in ((c_hi, Y_hi), (c_hi, Y_lo), (c_lo, Y_hi))],
                                                 start=False)
                            last.then_inc(shifted, 1)
                    for u in range(2):
                        for n in range(8):
                            if n < 4:
                                pe.wait_ge(exp_done, 8 * i + 4 * u + 4)
                            else:
                                pe.wait_ge(summed, 30 * i + 15 * u + 2 * (n - 4) + 2)
                            for h in range(2):
                                last = nc.tensor.matmul(bank[u][:, n % 4, h * (P + 1):(h + 1) * (P + 1)], probs[:, u, 2 * n + h, :],
                                                        Z[:, u, 2 * n + h, :], start=True, stop=True)
                            last.then_inc(pv_done, 1)
                    pe.wait_ge(x_done, 2 * i + 2)


def second_ffn(nc, k, out):
    N = 4
    W = N * P
    with ExitStack() as ctx:
        def sb(name, shape, dt=F32):
            return ctx.enter_context(nc.sbuf_tensor("f1_" + name, shape, dt))

        def sem(name):
            return ctx.enter_context(nc.semaphore("f1_" + name))

        carrier = sb("carrier", [P, 3])
        bn = sb("bn", [P, N, 6])
        stats = sb("stats", [P, N, 2])
        work = sb("work", [P, N, 4])
        xn = sb("xn", [P, N, P])
        hT = sb("hT", [P, W])
        logits = sb("logits", [P, N, E])
        best = sb("best", [P, N])
        less8 = sb("less8", [P, E])
        place = sb("place", [P, N, E])
        first = sb("first", [P, N])
        chosen = sb("chosen", [P, N, E])
        silu = sb("silu", [P, 3, W])
        act_in = sb("act_in", [P, 3, W])
        bank = [ctx.enter_context(nc.psum_tensor(f"f1_bank{n}", [P, 512], F32)) for n in range(8)]
        names = ("primed bn_done stats_ready norm_step xn_ready T_moved hT_ready routed logits_ready step chosen_ready "
                 "gate_done silu_ready up_done act_ready down_done x_done stored").split()
        (primed, bn_done, stats_ready, norm_step, xn_ready, T_moved, hT_ready, routed, logits_ready, step, chosen_ready,
         gate_done, silu_ready, up_done, act_ready, down_done, x_done, stored) = map(sem, names)
        STEPS = B // N

        with nc.Block() as block:
            @block.sync
            def _(sp):
                with sp.Fori(0, STEPS) as i:
                    sp.wait_ge(x_done, N * E * (i + 1))
                    sp.dma_start(out[bass.ts(i, N)].rearrange("b t d -> t b d"), k.x_sb[:, bass.ts(i, N), :]).then_inc(stored, 16)
                sp.wait_ge(stored, 16 * STEPS)

            @block.vector
            def _(dve):
                nc.vector.memset(work[:, :, 2:3], -0.5).then_inc(primed, 1)
                nc.vector.memset(carrier[:, 0:2], 0.0).then_inc(primed, 1)
                nc.vector.memset(work[:, :, 3:4], EPS).then_inc(primed, 1)
                for e in range(E):
                    nc.vector.memset(less8[:, e:e + 1], float(e - E)).then_inc(primed, 1)
                dve.wait_ge(primed, E + 3)
                with dve.Fori(0, STEPS) as i:
                    for u in range(N):
                        nc.vector.bn_stats(bn[:, u, :], k.x_sb[:, bass.ds(N * i + u, 1), :]).then_inc(bn_done, 1)
                    alone(nc, dve, carrier, bn_done, N * i + N)
                    for u in range(N):
                        nc.vector.bn_aggr(stats[:, u, :], bn[:, u, :]).then_inc(stats_ready, 1)
                    dve.wait_ge(T_moved, i + 1)
                    nc.vector.tensor_copy(hT[:, :], bank[6][:, :]).then_inc(hT_ready, 1)
                    dve.wait_ge(routed, i + 1)
                    L = bank[7][:, 0:N * E].rearrange("p (u e) -> p u e", u=N)
                    nc.vector.tensor_copy(logits[:, :, :], L).then_inc(logits_ready, 1)
                    dve.wait_ge(logits_ready, i + 1)
                    nc.vector.tensor_reduce(best[:, :], logits[:, :, :], AX.X, ALU.max).then_inc(step, 1)
                    dve.wait_ge(step, 11 * i + 1)
                    for u in range(N):
                        nc.vector.scalar_tensor_tensor(out=place[:, u, :], in0=logits[:, u, :], scalar=best[:, u:u + 1], in1=less8[:, :],
                                                       op0=ALU.is_equal, op1=ALU.mult).then_inc(step, 1)
                    dve.wait_ge(step, 11 * i + 5)
                    nc.vector.tensor_reduce(first[:, :], place[:, :, :], AX.X, ALU.min).then_inc(step, 1)
                    dve.wait_ge(step, 11 * i + 6)
                    for u in range(N):
                        nc.vector.tensor_scalar(chosen[:, u, :], less8[:, :], first[:, u:u + 1], k.tg[:, 3:4],
                                                ALU.is_equal, ALU.mult).then_inc(step, 1)
                    dve.wait_ge(step, 11 * i + 10)
                    nc.vector.tensor_copy(best[:, :], first[:, :]).then_inc(step, 1)
                    for e in range(E):
                        for c, (c0, rows) in enumerate(CHUNKS):
                            n = e * 3 + c
                            dve.wait_ge(silu_ready, 24 * i + n + 1)
                            dve.wait_ge(up_done, 24 * i + n + 1)
                            nc.vector.tensor_tensor(act_in[0:rows, c, :], bank[2 + n % 2][0:rows, :], silu[0:rows, c, :], ALU.mult)\
                                .then_inc(act_ready, 1)
                        dve.wait_ge(down_done, 8 * i + e + 1)
                        for u in range(N):
                            x_b = k.x_sb[:, bass.ds(N * i + u, 1), :].rearrange("p a n -> p (a n)")
                            if e:
                                dve.wait_ge(x_done, N * E * i + N * (e - 1) + u + 1)
                            nc.vector.scalar_tensor_tensor(out=x_b, in0=bank[4 + e % 2][:, u * P:u * P + P], scalar=chosen[:, u, e:e + 1],
                                                           in1=x_b, op0=ALU.mult, op1=ALU.add).then_inc(x_done, 1)

            @block.gpsimd
            def _(pool):
                pool.wait_ge(primed, E + 3)
                with pool.Fori(0, STEPS) as i:
                    for u in range(N):
                        x_b = k.x_sb[:, bass.ds(N * i + u, 1), :].rearrange("p a n -> p (a n)")
                        pool.wait_ge(stats_ready, N * i + u + 1)
                        normalise(nc, pool, stats[:, u, :], x_b, xn[:, u, :], work[:, u, :], norm_step,
                                  3 * N * i + 3 * u).then_inc(xn_ready, 1)

            @block.scalar
            def _(act):
                act.wait_ge(primed, E + 3)
                with act.Fori(0, STEPS) as i:
                    for e in range(E):
                        for c, (c0, rows) in enumerate(CHUNKS):
                            n = e * 3 + c
                            act.wait_ge(gate_done, 24 * i + n + 1)
                            if e:
                                act.wait_ge(act_ready, 24 * i + n - 2)
                            nc.scalar.activation(silu[0:rows, c, :], bank[n % 2][0:rows, :], ACT.Silu).then_inc(silu_ready, 1)

            @block.tensor
            def _(pe):
                pe.wait_ge(primed, E + 3)
                with pe.Fori(0, STEPS) as i:
                    for u in range(N):
                        pe.wait_ge(xn_ready, N * i + u + 1)
                        last = nc.tensor.transpose(bank[6][:, u * P:u * P + P], xn[:, u, :], k.ident[:, :])
                    last.then_inc(T_moved, 1)
                    pe.wait_ge(hT_ready, i + 1)
                    for u in range(N):
                        last = nc.tensor.matmul(bank[7][:, u * E:u * E + E], hT[:, u * P:u * P + P], k.routerT[:, :], start=True, stop=True)
                    last.then_inc(routed, 1)

                    def up(e):
                        for c, (c0, rows) in enumerate(CHUNKS):
                            n = e * 3 + c
                            if n >= 2:
                                pe.wait_ge(act_ready, 24 * i + n - 1)
                            nc.tensor.matmul(bank[n % 2][0:rows, :], k.gateT[:, e, c0:c0 + rows], hT[:, :], start=True, stop=True).then_inc(gate_done, 1)
                            nc.tensor.matmul(bank[2 + n % 2][0:rows, :], k.upT[:, e, c0:c0 + rows], hT[:, :], start=True, stop=True).then_inc(up_done, 1)

                    for e in range(E):
                        up(e)
                        pe.wait_ge(act_ready, 24 * i + 3 * e + 3)
                        if e >= 2:
                            pe.wait_ge(x_done, N * E * i + N * (e - 1))
                        for u in range(N):
                            for c, (c0, rows) in enumerate(CHUNKS):
                                last = nc.tensor.matmul(bank[4 + e % 2][:, u * P:u * P + P], act_in[0:rows, c, u * P:u * P + P],
                                                        k.downT[0:rows, c, e, :], start=c == 0, stop=c == 2)
                        last.then_inc(down_done, 1)
                    pe.wait_ge(x_done, N * E * i + N * E)


def build(nc, A, out):
    with ExitStack() as ctx:
        k = Setup()
        load_and_prepare(nc, ctx, A, k)
        first_attention(nc, k)
        first_ffn(nc, k)
        second_attention(nc, k)
        second_ffn(nc, k, out)


_NAMES = ['x', 'ctx_1024', 'g_xattn', 'g_ffn', 'L0_xattn_Wq', 'L0_xattn_bq', 'L0_xattn_Wk', 'L0_xattn_bk', 'L0_xattn_Wv',
          'L0_xattn_bv', 'L0_xattn_Wo', 'L0_xattn_bo', 'L0_ffn_ln_scale', 'L0_ffn_ln_bias', 'L0_ffn_attn_w', 'L0_ffn_attn_b',
          'L0_ffn_w1', 'L0_ffn_b1', 'L0_ffn_w2', 'L0_ffn_b2', 'L0_ffn_next_w', 'L0_ffn_next_b', 'L1_xattn_Wq', 'L1_xattn_Wk',
          'L1_xattn_Wv', 'L1_xattn_Wo', 'L1_xattn_bo', 'L1_ffn_router_w', 'L1_ffn_gate_w', 'L1_ffn_up_w', 'L1_ffn_down_w']


def kernel(**inputs):
    import concourse.bacc as bacc
    from concourse.bass_utils import run_bass_kernel_spmd

    nc = bacc.Bacc("TRN2", target_bir_lowering=False, num_devices=1)
    arrays, A = {}, {}
    for name in _NAMES:
        a = np.ascontiguousarray(inputs[name])
        arrays["in_" + name] = a
        A[name] = nc.dram_tensor("in_" + name, a.shape, mybir.dt.from_np(a.dtype), kind="ExternalInput").ap()
    out = nc.dram_tensor("out", (B, P, P), F32, kind="ExternalOutput").ap()
    build(nc, A, out)
    r = run_bass_kernel_spmd(nc, [arrays], core_ids=[0])
    return r.results[0]["out"]
```

```python
from contextlib import ExitStack
import numpy as np
import concourse.bass as bass
from concourse import mybir

ALU = mybir.AluOpType
ACT = mybir.ActivationFunctionType
F32 = mybir.dt.float32
F16 = mybir.dt.float16
BF16 = mybir.dt.bfloat16
AX = mybir.AxisListType

P = 128
B = 32
PAIRS = B // 2
H = 16
D0 = P // H
G = 32
HD1 = 64
E = 8
H0 = 4
I1 = 352
CHUNKS = ((0, 128), (128, 128), (256, 96))
EPS = 1e-5
TILES = B + E - 1
AHEAD = 8
ROW = P + 4


def both_products(nc, out, pairs, start=True, stop=True):
    last = None
    for n, (lhsT, rhs) in enumerate(pairs):
        last = nc.tensor.matmul(out, lhsT, rhs, start=start and n == 0, stop=stop and n == len(pairs) - 1,
                                skip_group_check=True)
    return last


class Setup:
    pass


def load_and_prepare(nc, ctx, A, k):
    def sb(name, shape, dt=F32):
        return ctx.enter_context(nc.sbuf_tensor(name, shape, dt))

    k.x_sb = sb("x_sb", [P, B + AHEAD, ROW])
    k.ctx_sb = sb("ctx_sb", [P, B + 3, P])
    k.cT = sb("cT", [P, 2, B + 2, P], F16)
    k.cT_hi, k.cT_lo = k.cT[:, 0], k.cT[:, 1]
    k.ident = sb("ident", [P, P])
    k.gates = sb("gates", [P, 4])
    k.tg = sb("tg", [P, 4])
    k.pick_head = sb("pick_head", [P, H, P], BF16)
    k.stack_sel = sb("stack_sel", [P, 4, H, 4, D0], F16)
    k.w0T_hi = sb("w0T_hi", [P, 3, P], F16)
    k.w0T_lo = sb("w0T_lo", [P, 3, P], F16)
    k.wo0 = sb("wo0", [P, P])
    k.bias0 = sb("bias0", [P, 3])
    k.bv0 = sb("bv0", [P, P])
    k.bo = sb("bo", [P, 2, P])
    k.attn_wT = sb("attn_wT", [P, P])
    k.next_wT = sb("next_wT", [P, P])
    k.ffn_cols = sb("ffn_cols", [P, 4])
    k.b1 = sb("b1", [P, E, H0])
    k.b2 = sb("b2", [P, E])
    k.w1 = sb("w1", [P, E, H0 * P])
    k.w2 = sb("w2", [P, E, H0, P])
    k.A_hi = sb("A_hi", [P, H, P], F16)
    k.A_lo = sb("A_lo", [P, H, P], F16)
    k.M_hi = sb("M_hi", [P, H, P], F16)
    k.M_lo = sb("M_lo", [P, H, P], F16)
    k.gateT = sb("gateT", [P, E, I1])
    k.upT = sb("upT", [P, E, I1])
    k.downT = sb("downT", [P, 3, E, P])
    k.routerT = sb("routerT", [P, E])
    k.tile_expert = sb("tile_expert", [1, TILES], mybir.dt.int32)
    k.sorted_rows = nc.dram_tensor("sorted_rows", ((TILES + 3) * P, ROW), F32, kind="Internal").ap()
    k.rows_cleared = ctx.enter_context(nc.semaphore("rows_cleared"))
    k.x_landed = ctx.enter_context(nc.semaphore("x_landed"))
    k.ffn0_landed = ctx.enter_context(nc.semaphore("ffn0_landed"))

    with ExitStack() as tmp:
        def tb(name, shape, dt=F32):
            return tmp.enter_context(nc.sbuf_tensor(name, shape, dt))

        def sem(name):
            return tmp.enter_context(nc.semaphore(name))

        small = tb("small", [P, 6, P])
        big = tb("big", [P, 3, H * HD1])
        bigT = tb("bigT", [P, 3, 8, P])
        wo1 = tb("wo1", [P, 8, P])
        numbers = tb("numbers", [P, B], mybir.dt.int32)
        empty_row = tb("empty_row", [P, ROW])
        router = tb("router", [E, P])
        router_c = tb("router_c", [E, P])
        router_bn = tb("router_bn", [E, 8])
        gu = tb("gu", [P, 2, 3, E, P])
        down = k.cT[:, :, :, :].rearrange("p a b n -> p (a b n)").bitcast(F32)[:, 0:E * I1].rearrange("p (e i) -> p e i", e=E)
        banks = [tmp.enter_context(nc.psum_tensor(f"setup_bank{n}", [P, 512], F32)) for n in range(8)]

        small_landed, big_landed, gu_landed = sem("small_landed"), sem("big_landed"), sem("gu_landed")
        g_landed, tg_ready, zeroed, const_ready = sem("g_landed"), sem("tg_ready"), sem("zeroed"), sem("const_ready")
        moved_ready, evacuated = sem("moved_ready"), sem("evacuated")
        split_hi, numbered, centred = sem("split_hi"), sem("numbered"), sem("centred")

        jobs = []
        for n in range(3):
            jobs.append(("t", small_landed, [(small[:, n, :], P, P)], ("split", k.w0T_hi[:, n, :], k.w0T_lo[:, n, :])))
        jobs.append(("t", small_landed, [(small[:, 3, :], P, P)], ("gate", k.wo0[:, :])))
        for n, dst in ((4, k.attn_wT), (5, k.next_wT)):
            jobs.append(("t", small_landed, [(small[:, n, :], P, P)], ("copy", dst[:, :])))
        jobs.append(("t", centred, [(router_c[:, :], P, E)], ("copy", k.routerT[:, :])))
        for w in range(3):
            for q in range(2):
                jobs.append(("t", big_landed, [(big[:, w, (4 * q + n) * P:(4 * q + n + 1) * P], P, P) for n in range(4)],
                             ("copy", bigT[:, w, 4 * q:4 * q + 4, :].rearrange("p a n -> p (a n)"))))
        bigT_jobs = len(jobs)
        for w, dst in ((0, k.gateT), (1, k.upT)):
            for e in range(E):
                jobs.append(("t", gu_landed, [(gu[0:rows, w, c, e, :], P, rows) for c, (_, rows) in enumerate(CHUNKS)],
                             ("copy", dst[:, e, :])))
        for c, (c0, rows) in enumerate(CHUNKS):
            for q in range(2):
                jobs.append(("t", gu_landed, [(down[:, 4 * q + n, c0:c0 + rows], rows, P) for n in range(4)],
                             ("copy", k.downT[0:rows, c, 4 * q:4 * q + 4, :].rearrange("p a n -> p (a n)"))))
        for q in range(4):
            heads = range(8 * (q // 2) + q % 2, 8 * (q // 2) + 8, 2)
            half = lambda t, w, h: t[HD1 * (h % 2):HD1 * (h % 2) + HD1, w, h // 2, :]
            there = slice(heads[0], heads[0] + 7, 2)
            jobs.append(("m", evacuated, [(half(bigT, 0, h), half(bigT, 1, h)) for h in heads],
                         ("scaled", k.A_hi[:, there, :], k.A_lo[:, there, :])))
            jobs.append(("m", evacuated, [(half(bigT, 2, h), wo1[HD1 * (h % 2):HD1 * (h % 2) + HD1, h // 2, :]) for h in heads],
                         ("gated", k.M_hi[:, there, :], k.M_lo[:, there, :])))

        total = {}

        with nc.Block() as block:
            @block.sync
            def _(sp):
                def load(dst, src, landed):
                    sp.dma_start(dst, src).then_inc(landed, 16)
                    total[landed.name] = total.get(landed.name, 0) + 16

                def on_all(v):
                    return v.rearrange("(a n) -> a n", a=1).broadcast_to([P, v.shape[0]])

                load(k.gates[:, 0:2], on_all(A["g_xattn"]), g_landed)
                load(k.gates[:, 2:4], on_all(A["g_ffn"]), g_landed)
                for n, name in enumerate(("L0_xattn_Wq", "L0_xattn_Wk", "L0_xattn_Wv", "L0_xattn_Wo",
                                          "L0_ffn_attn_w", "L0_ffn_next_w")):
                    load(small[:, n, :], A[name], small_landed)
                load(router[:, :], A["L1_ffn_router_w"], small_landed)
                sp.wait_ge(zeroed, 9)
                sp.dma_start(k.sorted_rows.rearrange("(j p) w -> p j w", p=P),
                             empty_row[:, :].rearrange("p (a w) -> p a w", a=1).broadcast_to([P, TILES + 3, ROW])).then_inc(k.rows_cleared, 16)
                for b0 in range(0, B, 8):
                    load(k.x_sb[:, b0:b0 + 8, 0:P], A["x"][b0:b0 + 8].rearrange("b t d -> t b d"), k.x_landed)
                    load(k.ctx_sb[:, b0:b0 + 8, :], A["ctx_1024"][b0:b0 + 8].rearrange("b t d -> t b d"), k.x_landed)
                for n, name in enumerate(("L1_xattn_Wq", "L1_xattn_Wk", "L1_xattn_Wv")):
                    load(big[:, n, :], A[name], big_landed)
                load(wo1[:, :, :], A["L1_xattn_Wo"].rearrange("(j p) n -> p j n", p=P), big_landed)
                for w, name in enumerate(("L1_ffn_gate_w", "L1_ffn_up_w")):
                    for c, (c0, rows) in enumerate(CHUNKS):
                        load(gu[0:rows, w, c, :, :], A[name][:, c0:c0 + rows, :].rearrange("e i h -> i e h"), gu_landed)
                load(down, A["L1_ffn_down_w"].rearrange("e h i -> h e i"), gu_landed)

                def column(v):
                    return v.rearrange("(p a) -> p a", a=1)

                load(k.bias0[:, 0:1], column(A["L0_xattn_bq"]), k.x_landed)
                load(k.bias0[:, 1:2], column(A["L0_xattn_bk"]), k.x_landed)
                load(k.bv0[:, :], on_all(A["L0_xattn_bv"]), k.x_landed)
                load(k.bo[:, 0, :], on_all(A["L0_xattn_bo"]), k.x_landed)
                load(k.bo[:, 1, :], on_all(A["L1_xattn_bo"]), k.x_landed)
                for n, name in enumerate(("L0_ffn_ln_scale", "L0_ffn_ln_bias", "L0_ffn_attn_b", "L0_ffn_next_b")):
                    load(k.ffn_cols[:, n:n + 1], column(A[name]), k.ffn0_landed)
                load(k.w1[:, :, :], A["L0_ffn_w1"].rearrange("e d h -> d e h"), k.ffn0_landed)
                load(k.w2[:, :, :, :].rearrange("p e c n -> p (e c) n"),
                     A["L0_ffn_w2"].rearrange("e (c p) n -> p (e c) n", p=P), k.ffn0_landed)
                with nc.allow_non_contiguous_dma(reason="small bias columns"):
                    load(k.b1[:, :, :].rearrange("p e c -> p (e c)"),
                         A["L0_ffn_b1"].rearrange("e (c p) -> p (e c)", p=P), k.ffn0_landed)
                    load(k.b2[:, :], A["L0_ffn_b2"].rearrange("e p -> p e"), k.ffn0_landed)

            k.x_total, k.ffn0_total = total[k.x_landed.name], total[k.ffn0_landed.name]

            @block.gpsimd
            def _(pool):
                nc.gpsimd.memset(k.ident[:, :], 0.0).then_inc(zeroed, 1)
                nc.gpsimd.memset(k.stack_sel[:, :, :, :, :], 0.0).then_inc(zeroed, 1)
                nc.gpsimd.memset(k.pick_head[:, :, :], 0.0).then_inc(zeroed, 1)
                nc.gpsimd.memset(k.x_sb[:, B:B + AHEAD, :], 0.0).then_inc(zeroed, 1)
                nc.gpsimd.memset(k.x_sb[:, 0:B, P:ROW], 0.0).then_inc(zeroed, 1)
                nc.gpsimd.memset(empty_row[:, 0:P], 0.0).then_inc(zeroed, 1)
                nc.gpsimd.memset(empty_row[:, P:ROW], float(B * P)).then_inc(zeroed, 1)
                nc.gpsimd.iota(numbers[:, :], pattern=[[P, B]], base=0, channel_multiplier=1).then_inc(zeroed, 1)
                nc.gpsimd.memset(k.ctx_sb[:, B:B + 3, :], 0.0).then_inc(zeroed, 1)
                pool.wait_ge(zeroed, 9)
                nc.gpsimd.affine_select(out=k.ident[:, :], in_=k.ident[:, :], compare_op=ALU.not_equal, fill=1.0,
                                        base=0, pattern=[[-1, P]], channel_multiplier=1).then_inc(const_ready, 1)
                nc.gpsimd.affine_select(out=k.pick_head[:, :, :], in_=k.pick_head[:, :, :], compare_op=ALU.not_equal,
                                        fill=1.0, base=0, pattern=[[-1, H], [0, P]], channel_multiplier=1)\
                    .then_inc(const_ready, 1)
                for n, copies in enumerate((slice(0, 4, 2), slice(1, 4, 2), slice(0, 2), slice(2, 4))):
                    part = k.stack_sel[:, n, :, copies, :]
                    nc.gpsimd.affine_select(out=part, in_=part, compare_op=ALU.not_equal, fill=1.0, base=0,
                                            pattern=[[-D0, H], [0, 2], [-1, D0]], channel_multiplier=1)\
                        .then_inc(const_ready, 1)

            @block.scalar
            def _(act):
                act.wait_ge(g_landed, 32)
                nc.scalar.activation(k.tg[:, :], k.gates[:, :], ACT.Tanh).then_inc(tg_ready, 1)

            @block.tensor
            def _(pe):
                pe.wait_ge(const_ready, 6)
                seen = set()
                for n, (kind, need, parts, target) in enumerate(jobs):
                    if need.name not in seen:
                        seen.add(need.name)
                        pe.wait_ge(need, {centred.name: 3, evacuated.name: bigT_jobs}.get(need.name, total.get(need.name)))
                    if n >= 8:
                        pe.wait_ge(evacuated, n - 7)
                    at = 0
                    for a, b, *c in parts:
                        if kind == "t":
                            rows, width = b, c[0]
                            last = nc.tensor.transpose(banks[n % 8][0:rows, at:at + width], a, k.ident[0:width, 0:width])
                            at += width
                        else:
                            last = nc.tensor.matmul(banks[n % 8][:, at:at + P], a, b, start=True, stop=True)
                            at += P
                    last.then_inc(moved_ready, 1)

            @block.vector
            def _(dve):
                nc.vector.memset(k.downT[CHUNKS[2][1]:P, 2, :, :], 0.0).then_inc(numbered, 1)
                dve.wait_ge(small_landed, total[small_landed.name])
                dve.wait_ge(zeroed, 9)
                nc.vector.tensor_copy(k.x_sb[:, 0:B, P], numbers[:, :]).then_inc(numbered, 1)
                nc.vector.bn_stats(router_bn[:, 0:6], router[:, :]).then_inc(centred, 1)
                dve.wait_ge(centred, 1)
                nc.vector.bn_aggr(router_bn[:, 6:8], router_bn[:, 0:6]).then_inc(centred, 1)
                dve.wait_ge(centred, 2)
                nc.vector.tensor_scalar(router_c[:, :], router[:, :], router_bn[:, 6:7], None, ALU.subtract).then_inc(centred, 1)
                dve.wait_ge(tg_ready, 1)
                splits = 0
                for n, (kind, need, parts, target) in enumerate(jobs):
                    dve.wait_ge(moved_ready, n + 1)
                    what, dst = target[0], target[1]
                    width = sum(c[0] if c else P for _, _, *c in parts)
                    src = banks[n % 8][0:dst.shape[0], 0:width]
                    if kind == "m":
                        src = src.rearrange("p (a n) -> p a n", n=P)
                    if what == "copy":
                        nc.vector.tensor_copy(dst, src).then_inc(evacuated, 1)
                    elif what == "gate":
                        nc.vector.tensor_scalar(dst, src, k.tg[:, 0:1], None, ALU.mult).then_inc(evacuated, 1)
                    else:
                        factor = {"split": 1.0, "scaled": float(HD1) ** -0.5, "gated": k.tg[:, 1:2]}[what]
                        nc.vector.tensor_scalar(dst, src, factor, None, ALU.mult).then_inc(split_hi, 1)
                        splits += 1
                        dve.wait_ge(split_hi, splits)
                        nc.vector.scalar_tensor_tensor(out=target[2], in0=src, scalar=factor, in1=dst,
                                                       op0=ALU.mult, op1=ALU.subtract).then_inc(evacuated, 1)
                dve.wait_ge(evacuated, len(jobs))
                dve.wait_ge(numbered, 2)
                dve.wait_ge(const_ready, 6)


def alone(nc, dve, carrier, semaphore, value):
    dve.wait_ge(semaphore, value)
    nc.vector.tensor_copy(carrier[:, 1:2], carrier[:, 0:1])


def normalise(nc, pool, stats, x_b, out, work, s, count):
    nc.gpsimd.tensor_tensor(work[:, 0:1], stats[:, 1:2], work[:, 3:4], ALU.add).then_inc(s, 1)
    nc.gpsimd.tensor_tensor(out, x_b, stats[:, 0:1].broadcast_to([P, P]), ALU.subtract).then_inc(s, 1)
    pool.wait_ge(s, count + 2)
    nc.gpsimd.tensor_tensor(work[:, 1:2], work[:, 0:1], work[:, 2:3], ALU.pow).then_inc(s, 1)
    pool.wait_ge(s, count + 3)
    return nc.gpsimd.tensor_tensor(out, out, work[:, 1:2].broadcast_to([P, P]), ALU.mult)


def first_attention(nc, k):
    R = 4
    with ExitStack() as ctx:
        def sb(name, shape, dt=F32):
            return ctx.enter_context(nc.sbuf_tensor("l0_" + name, shape, dt))

        def sem(name):
            return ctx.enter_context(nc.semaphore("l0_" + name))

        carrier = sb("carrier", [P, 3])
        taker = sb("taker", [P, 2])
        bn = sb("bn", [P, 2, 6])
        stats = sb("stats", [P, 2, 2])
        work = sb("work", [P, 2, 4])
        xn = sb("xn", [P, 2, 2, P])
        bias_row = sb("bias_row", [P, P])
        T_hi = sb("T_hi", [P, P], F16)
        T_lo = sb("T_lo", [P, P], F16)
        qk_hi = sb("qk_hi", [P, 2, P], F16)
        qk_lo = sb("qk_lo", [P, 2, P], F16)
        stack = sb("stack", [P, 2, 2, 4, P], F16)
        V = sb("V", [P, 2, H, G])
        neg_max = sb("neg_max", [P, H])
        neg_maxT = sb("neg_maxT", [P, P], BF16)
        probs = sb("probs", [P, R, 4 * P])
        sums = sb("sums", [P, 4 * P])
        inv = sb("inv", [P, H])
        heads_out = sb("heads_out", [P, P])
        headsT = sb("headsT", [P, P])
        score_bank = [ctx.enter_context(nc.psum_tensor(f"l0_score{n}", [P, 512], F32)) for n in range(R)]
        front_bank, stack_bank, misc_bank, sum_bank = (
            ctx.enter_context(nc.psum_tensor(f"l0_{name}", [P, 512], F32)) for name in ("front", "stack_bank", "misc", "sum_bank"))
        names = ("primed bn_done stats_ready norm_step xn_ready bias_added T_moved T_hi_ready T_lo_ready qk_done qk_hi_ready "
                 "qk_lo_ready v_done V_ready q_stacked k_stacked stack_q stack_k scored max_ready maxT_moved maxT_ready shifted "
                 "exp_done pv_done sums_ready sums_moved inv_ready heads_ready heads_moved headsT_ready projected x_done").split()
        (primed, bn_done, stats_ready, norm_step, xn_ready, bias_added, T_moved, T_hi_ready, T_lo_ready, qk_done, qk_hi_ready,
         qk_lo_ready, v_done, V_ready, q_stacked, k_stacked, stack_q, stack_k, scored, max_ready, maxT_moved, maxT_ready, shifted,
         exp_done, pv_done, sums_ready, sums_moved, inv_ready, heads_ready, heads_moved, headsT_ready, projected, x_done) = map(sem, names)

        def row(t, n):
            return t[:, bass.ds(n, 1), 0:P].rearrange("p a n -> p (a n)")

        with nc.Block() as block:
            @block.vector
            def _(dve):
                nc.vector.memset(V[:, :, :, :], 1.0).then_inc(primed, 1)
                nc.vector.memset(neg_maxT[:, :], 0.0).then_inc(primed, 1)
                nc.vector.memset(taker[:, :], 0.0).then_inc(primed, 1)
                nc.vector.memset(work[:, :, 2:3], -0.5).then_inc(primed, 1)
                nc.vector.memset(carrier[:, 0:2], 0.0).then_inc(primed, 1)
                nc.vector.memset(work[:, :, 3:4], EPS).then_inc(primed, 1)
                dve.wait_ge(k.x_landed, k.x_total)
                nc.vector.tensor_scalar(bias_row[:, :], k.bo[:, 0, :], k.tg[:, 0:1], None, ALU.mult).then_inc(primed, 1)
                dve.wait_ge(primed, 7)

                def statistics(n, w):
                    nc.vector.bn_stats(bn[:, w, :], row(k.x_sb, n)).then_inc(bn_done, 1)
                    alone(nc, dve, carrier, bn_done, n + 1)
                    nc.vector.bn_aggr(stats[:, w, :], bn[:, w, :]).then_inc(stats_ready, 1)

                def transposed_lo(n):
                    dve.wait_ge(T_hi_ready, 2 * n + 2)
                    nc.vector.tensor_tensor(T_lo[:, :], front_bank[:, 0:P], T_hi[:, :], ALU.subtract).then_inc(T_lo_ready, 1)
                    nc.vector.tensor_tensor(row(k.cT_lo, n), front_bank[:, P:2 * P], row(k.cT_hi, n), ALU.subtract).then_inc(T_lo_ready, 1)

                def projected_lo(n):
                    dve.wait_ge(qk_hi_ready, 2 * n + 2)
                    for m in range(2):
                        nc.vector.scalar_tensor_tensor(out=qk_lo[:, m, :], in0=front_bank[:, (2 + m) * P:(3 + m) * P],
                                                       scalar=k.bias0[:, m:m + 1], in1=qk_hi[:, m, :],
                                                       op0=ALU.add, op1=ALU.subtract).then_inc(qk_lo_ready, 1)

                def values(n, w):
                    dve.wait_ge(v_done, n + 1)
                    nc.vector.tensor_tensor(V[:, w, :, 0:D0], misc_bank[:, 0:P].rearrange("p (h d) -> p h d", h=H),
                                            k.bv0[:, :].rearrange("p (h d) -> p h d", h=H), ALU.add).then_inc(V_ready, 1)

                def stacked_q(n, w):
                    dve.wait_ge(q_stacked, n + 1)
                    nc.vector.tensor_copy(stack[:, w, 0].rearrange("p j n -> p (j n)"), stack_bank[:, :]).then_inc(stack_q, 1)

                def maxima(n, r):
                    dve.wait_ge(scored, R * n + r + 1)
                    nc.vector.tensor_reduce(neg_max[:, 4 * r:4 * r + 4], score_bank[r][:, :].rearrange("p (j n) -> p j n", j=4),
                                            AX.X, ALU.max, negate=True).then_inc(max_ready, 1)

                def maxima_out(n):
                    dve.wait_ge(maxT_moved, n + 1)
                    nc.vector.tensor_copy(neg_maxT[0:H, :], misc_bank[0:H, P:2 * P]).then_inc(maxT_ready, 1)

                def divide(n):
                    O = sum_bank[:, :].rearrange("p (h g) -> p h g", g=G)
                    dve.wait_ge(sums_moved, n + 1)
                    nc.vector.reciprocal(inv[:, :], O[:, :, D0]).then_inc(inv_ready, 1)
                    dve.wait_ge(inv_ready, n + 1)
                    nc.vector.tensor_tensor(heads_out[:, :].rearrange("p (h d) -> p h d", h=H), O[:, :, 0:D0],
                                            inv[:, :].rearrange("p (h a) -> p h a", a=1).broadcast_to([P, H, D0]), ALU.mult)\
                        .then_inc(heads_ready, 1)

                def heads_transposed(n):
                    dve.wait_ge(heads_moved, n + 1)
                    nc.vector.tensor_copy(headsT[:, :], misc_bank[:, 2 * P:3 * P]).then_inc(headsT_ready, 1)

                def add_to_x(n):
                    dve.wait_ge(projected, n + 1)
                    dve.wait_ge(bias_added, n + 1)
                    nc.vector.tensor_tensor(row(k.x_sb, n), misc_bank[:, 3 * P:4 * P], row(k.x_sb, n), ALU.add).then_inc(x_done, 1)

                def step(n, w, first=False):
                    maxima_out(n)
                    stacked_q(n + 1, 1 - w)
                    transposed_lo(n + 2)
                    if not first:
                        divide(n - 1)
                    values(n + 1, 1 - w)
                    dve.wait_ge(xn_ready, 2 * n + 4)
                    statistics(n + 3, 1 - w)
                    if not first:
                        heads_transposed(n - 1)
                    projected_lo(n + 2)
                    if not first:
                        add_to_x(n - 1)
                    for r in range(R):
                        maxima(n + 1, r)

                for n in range(3):
                    if n == 2:
                        dve.wait_ge(xn_ready, 2)
                    statistics(n, n % 2)
                transposed_lo(0)
                projected_lo(0)
                values(0, 0)
                transposed_lo(1)
                stacked_q(0, 0)
                projected_lo(1)
                for r in range(R):
                    maxima(0, r)
                step(0, 0, first=True)
                step(1, 1)
                with dve.Fori(1, PAIRS) as i:
                    for w in range(2):
                        step(2 * i + w, w)
                divide(B - 1)
                heads_transposed(B - 1)
                add_to_x(B - 1)

            @block.gpsimd
            def _(pool):
                pool.wait_ge(primed, 7)

                def normal(n, w, free=True):
                    pool.wait_ge(stats_ready, n + 1)
                    if free:
                        pool.wait_ge(T_moved, n - 1)
                    normalise(nc, pool, stats[:, w, :], row(k.x_sb, n), xn[:, w, 0, :], work[:, w, :], norm_step, 3 * n).then_inc(xn_ready, 1)
                    nc.gpsimd.tensor_copy(xn[:, w, 1, :], row(k.ctx_sb, n)).then_inc(xn_ready, 1)
                    pool.wait_ge(xn_ready, 2 * n + 2)
                    nc.gpsimd.tensor_tensor(taker[:, 1:2], taker[:, 0:1], taker[:, 0:1], ALU.add)
                    nc.gpsimd.tensor_tensor(row(k.x_sb, n), row(k.x_sb, n), bias_row[:, :], ALU.add).then_inc(bias_added, 1)

                normal(0, 0, free=False)
                normal(1, 1, free=False)
                normal(2, 0)
                normal(3, 1)
                normal(4, 0)
                with pool.Fori(1, PAIRS) as i:
                    for w in range(2):
                        normal(2 * i + w + 3, 1 - w)

            @block.scalar
            def _(act):
                act.wait_ge(primed, 7)
                nc.scalar.activation(carrier[:, 2:3], carrier[:, 0:1], ACT.Exp).then_inc(exp_done, R)

                def transposed_hi(n):
                    act.wait_ge(T_moved, n + 1)
                    nc.scalar.activation(T_hi[:, :], front_bank[:, 0:P], ACT.Copy).then_inc(T_hi_ready, 1)
                    nc.scalar.activation(row(k.cT_hi, n), front_bank[:, P:2 * P], ACT.Copy).then_inc(T_hi_ready, 1)

                def projected_hi(n):
                    act.wait_ge(qk_done, n + 1)
                    for m in range(2):
                        nc.scalar.activation(qk_hi[:, m, :], front_bank[:, (2 + m) * P:(3 + m) * P], ACT.Identity,
                                             bias=k.bias0[:, m:m + 1]).then_inc(qk_hi_ready, 1)

                def stacked_k(n, w):
                    act.wait_ge(k_stacked, n + 1)
                    nc.scalar.activation(stack[:, w, 1].rearrange("p j n -> p (j n)"), stack_bank[:, :], ACT.Copy).then_inc(stack_k, 1)

                def exponentials(n, r):
                    act.wait_ge(shifted, R * n + r + 1)
                    nc.scalar.activation(probs[:, r, :], score_bank[r][:, :], ACT.Exp, scale=float(D0) ** -0.5).then_inc(exp_done, 1)

                def sums_out(n):
                    act.wait_ge(pv_done, n + 1)
                    nc.scalar.activation(sums[:, :], sum_bank[:, :], ACT.Copy).then_inc(sums_ready, 1)

                def step(n, w, first=False):
                    if not first:
                        sums_out(n - 1)
                    transposed_hi(n + 2)
                    exponentials(n, 0)
                    stacked_k(n + 1, 1 - w)
                    projected_hi(n + 2)
                    exponentials(n, 1)
                    exponentials(n, 2)
                    exponentials(n, 3)

                transposed_hi(0)
                projected_hi(0)
                transposed_hi(1)
                stacked_k(0, 0)
                projected_hi(1)
                step(0, 0, first=True)
                step(1, 1)
                with act.Fori(1, PAIRS) as i:
                    for w in range(2):
                        step(2 * i + w, w)
                sums_out(B - 1)

            @block.tensor
            def _(pe):
                pe.wait_ge(primed, 7)

                def transpose(n, w, first=False):
                    pe.wait_ge(xn_ready, 2 * n + 2)
                    if not first:
                        pe.wait_ge(qk_lo_ready, 2 * n)
                    for m in range(2):
                        last = nc.tensor.transpose(front_bank[:, m * P:m * P + P], xn[:, w, m, :], k.ident[:, :])
                    last.then_inc(T_moved, 1)

                def project(n, first=False):
                    pe.wait_ge(T_lo_ready, 2 * n + 2)
                    for m, (hi, lo) in enumerate(((T_hi[:, :], T_lo[:, :]), (row(k.cT_hi, n), row(k.cT_lo, n)))):
                        last = both_products(nc, front_bank[:, (2 + m) * P:(3 + m) * P],
                                             [(v[:, m, :], t) for v, t in ((k.w0T_hi, hi), (k.w0T_lo, hi), (k.w0T_hi, lo))])
                    last.then_inc(qk_done, 1)

                def project_values(n, first=False):
                    if not first:
                        pe.wait_ge(maxT_ready, n)
                    last = both_products(nc, misc_bank[:, 0:P], [(row(t, n), v[:, 2, :]) for v, t in
                                                                 ((k.w0T_hi, k.cT_hi), (k.w0T_lo, k.cT_hi), (k.w0T_hi, k.cT_lo))])
                    last.then_inc(v_done, 1)

                def stack_up(n, m, done, first=False):
                    if m == 0:
                        pe.wait_ge(qk_lo_ready, 2 * n + 2)
                        if not first:
                            pe.wait_ge(stack_k, n)
                    else:
                        pe.wait_ge(stack_q, n + 1)
                    for j in range(4):
                        sel = [k.stack_sel[:, 2 * m + part, 4 * j:4 * j + 4].rearrange("p h c d -> p (h c d)") for part in range(2)]
                        last = both_products(nc, stack_bank[:, j * P:j * P + P], [(sel[0], qk_hi[:, m, :]), (sel[1], qk_lo[:, m, :])])
                    last.then_inc(done, 1)

                def score_by_query(n, w, r):
                    pe.wait_ge(stack_k, n + 1)
                    pe.wait_ge(exp_done, R * n + r + 1)
                    rows = slice(G * r, G * r + G)
                    for j in range(4):
                        last = nc.tensor.matmul(score_bank[r][:, j * P:j * P + P], stack[rows, w, 0, j, :], stack[rows, w, 1, j, :],
                                                start=True, stop=True, tile_position=(G * r, 0))
                    last.then_inc(scored, 1)

                def transpose_maxima(n, back=True):
                    pe.wait_ge(max_ready, R * n + R)
                    pe.wait_ge(V_ready, n + 1)
                    if back:
                        pe.wait_ge(x_done, n - 1)
                    nc.tensor.transpose(misc_bank[0:H, P:2 * P], neg_max[:, :], k.ident[:, :]).then_inc(maxT_moved, 1)

                def score_by_key(n, w, r):
                    if r == 0:
                        pe.wait_ge(maxT_ready, n + 1)
                    rows = slice(G * r, G * r + G)
                    for j in range(4):
                        nc.tensor.matmul(score_bank[r][:, j * P:j * P + P], k.pick_head[:, 4 * r + j, :], neg_maxT[:, :],
                                         start=j == 0, stop=False, skip_group_check=True)
                    for j in range(4):
                        last = nc.tensor.matmul(score_bank[r][:, j * P:j * P + P], stack[rows, w, 1, j, :], stack[rows, w, 0, j, :],
                                                start=False, stop=j == 3, tile_position=(G * r, 0), skip_group_check=True)
                    last.then_inc(shifted, 1)

                def weigh(n, w, r, first=False):
                    pe.wait_ge(exp_done, R * n + r + R + 1)
                    if r == 0:
                        pe.wait_ge(V_ready, n + 1)
                        if not first:
                            pe.wait_ge(heads_ready, n)
                    for j in range(4):
                        last = nc.tensor.matmul(sum_bank[G * r:G * r + G, j * P:j * P + P], V[:, w, 4 * j + r, :],
                                                probs[:, r, j * P:j * P + P], start=True, stop=True, tile_position=(0, G * r))
                    if r == R - 1:
                        last.then_inc(pv_done, 1)

                def transpose_sums(n):
                    pe.wait_ge(sums_ready, n + 1)
                    for j in range(4):
                        last = nc.tensor.transpose(sum_bank[:, j * P:j * P + P], sums[:, j * P:j * P + P], k.ident[:, :])
                    last.then_inc(sums_moved, 1)

                def transpose_heads(n, values=None):
                    pe.wait_ge(heads_ready, n + 1)
                    if values is not None:
                        pe.wait_ge(V_ready, values + 1)
                    nc.tensor.transpose(misc_bank[:, 2 * P:3 * P], heads_out[:, :], k.ident[:, :]).then_inc(heads_moved, 1)

                def project_heads(n):
                    pe.wait_ge(headsT_ready, n + 1)
                    nc.tensor.matmul(misc_bank[:, 3 * P:4 * P], headsT[:, :], k.wo0[:, :], start=True, stop=True).then_inc(projected, 1)

                def step(n, w, first=False, back=True):
                    transpose(n + 2, w)
                    stack_up(n + 1, 0, q_stacked)
                    transpose_maxima(n, back)
                    if not first:
                        transpose_sums(n - 1)
                    score_by_key(n, w, 0)
                    stack_up(n + 1, 1, k_stacked)
                    project(n + 2)
                    project_values(n + 1)
                    score_by_key(n, w, 1)
                    if not first:
                        transpose_heads(n - 1, n + 1)
                    score_by_key(n, w, 2)
                    if not first:
                        project_heads(n - 1)
                    score_by_query(n + 1, 1 - w, 0)
                    score_by_key(n, w, 3)
                    score_by_query(n + 1, 1 - w, 1)
                    weigh(n, w, 0, first)
                    score_by_query(n + 1, 1 - w, 2)
                    weigh(n, w, 1)
                    score_by_query(n + 1, 1 - w, 3)
                    weigh(n, w, 2)
                    weigh(n, w, 3)

                transpose(0, 0, first=True)
                project(0)
                project_values(0, first=True)
                transpose(1, 1)
                stack_up(0, 0, q_stacked, first=True)
                stack_up(0, 1, k_stacked)
                project(1)
                for r in range(R):
                    score_by_query(0, 0, r)
                step(0, 0, first=True, back=False)
                step(1, 1, back=False)
                with pe.Fori(1, PAIRS) as i:
                    for w in range(2):
                        step(2 * i + w, w)
                transpose_sums(B - 1)
                transpose_heads(B - 1)
                project_heads(B - 1)


def first_ffn(nc, k):
    with ExitStack() as ctx:
        def sb(name, shape, dt=F32):
            return ctx.enter_context(nc.sbuf_tensor("f0_" + name, shape, dt))

        def sem(name):
            return ctx.enter_context(nc.semaphore("f0_" + name))

        carrier = sb("carrier", [P, 3])
        half = sb("half", [P, 2])
        bn = sb("bn", [P, 2, 2, 6])
        stats = sb("stats", [P, 2, 2, 2])
        var = sb("var", [P, 2, 2])
        rstd = sb("rstd", [P, 2, 2])
        xn = sb("xn", [P, 2, 2, 2, P])
        znT = sb("znT", [P, 2, 2, 2 * P])
        xaT = sb("xaT", [P, 2 * P])
        hid = sb("hid", [P, H0, 2 * P])
        eoT = sb("eoT", [P, 2 * P])
        outT = sb("outT", [P, 2 * P])
        t_bank, attn_bank, *hid_bank, eo_bank, next_bank = (
            ctx.enter_context(nc.psum_tensor(f"f0_bank{n}", [P, 512], F32)) for n in range(8))
        names = ("primed bn_done stats_ready var_ready rstd_ready once_ready twice_ready T_moved T_ready attn_done xa_ready "
                 "hid_done hid_ready eo_done eo_ready next_done outT_ready back_done x_done").split()
        (primed, bn_done, stats_ready, var_ready, rstd_ready, once_ready, twice_ready, T_moved, T_ready, attn_done, xa_ready,
         hid_done, hid_ready, eo_done, eo_ready, next_done, outT_ready, back_done, x_done) = map(sem, names)

        def row(n):
            return k.x_sb[:, bass.ds(n, 1), 0:P].rearrange("p a n -> p (a n)")

        with nc.Block() as block:
            @block.vector
            def _(dve):
                nc.vector.memset(half[:, :], -0.5).then_inc(primed, 1)
                nc.vector.memset(carrier[:, 0:2], 0.0).then_inc(primed, 1)
                nc.vector.memset(var[:, :, :], 1.0).then_inc(x_done, 2)
                dve.wait_ge(k.ffn0_landed, k.ffn0_total)
                dve.wait_ge(primed, 2)
                dve.wait_ge(x_done, 2)

                def statistics(g, w, s):
                    if s == 1:
                        dve.wait_ge(once_ready, 2 * g + 2)
                    for u in range(2):
                        nc.vector.bn_stats(bn[:, s, u, :], xn[:, w, 0, u, :] if s else row(2 * g + u)).then_inc(bn_done, 1)
                    alone(nc, dve, carrier, bn_done, 4 * g + 2 * s + 2)
                    for u in range(2):
                        nc.vector.bn_aggr(stats[:, s, u, :], bn[:, s, u, :]).then_inc(stats_ready, 1)
                    dve.wait_ge(stats_ready, 4 * g + 2 * s + 2)
                    nc.vector.tensor_scalar(var[:, s, :], stats[:, s, :, 1], EPS, None, ALU.add).then_inc(var_ready, 1)

                def normalised(g, w, s):
                    dve.wait_ge(rstd_ready, 2 * g + s + 1)
                    for u in range(2):
                        nc.vector.tensor_scalar(xn[:, w, s, u, :], xn[:, w, 0, u, :] if s else row(2 * g + u), stats[:, s, u, 0:1],
                                                rstd[:, s, u:u + 1], ALU.subtract, ALU.mult).then_inc(twice_ready if s else once_ready, 1)

                def transposed(g, w):
                    dve.wait_ge(T_moved, g + 1)
                    nc.vector.tensor_copy(znT[:, w, 0, :], t_bank[:, 0:2 * P]).then_inc(T_ready, 1)
                    nc.vector.tensor_scalar(znT[:, w, 1, :], t_bank[:, 2 * P:4 * P], k.ffn_cols[:, 0:1], k.ffn_cols[:, 1:2],
                                            ALU.mult, ALU.add).then_inc(T_ready, 1)

                def attended(g, w):
                    dve.wait_ge(T_ready, 2 * g + 1)
                    dve.wait_ge(attn_done, g + 1)
                    nc.vector.scalar_tensor_tensor(out=xaT[:, :], in0=attn_bank[:, 0:2 * P], scalar=k.ffn_cols[:, 2:3],
                                                   in1=znT[:, w, 0, :], op0=ALU.add, op1=ALU.add).then_inc(xa_ready, 1)

                def add_to_x(g):
                    dve.wait_ge(back_done, g + 1)
                    for u in range(2):
                        nc.vector.scalar_tensor_tensor(out=row(2 * g + u), in0=attn_bank[:, (2 + u) * P:(3 + u) * P], scalar=k.tg[:, 2:3],
                                                       in1=row(2 * g + u), op0=ALU.mult, op1=ALU.add).then_inc(x_done, 1)

                for g in range(2):
                    for s in range(2):
                        statistics(g, g, s)
                        normalised(g, g, s)
                    if g == 0:
                        transposed(0, 0)
                        attended(0, 0)
                transposed(1, 1)
                for s in range(2):
                    statistics(2, 0, s)
                    normalised(2, 0, s)
                statistics(3, 1, 0)
                with dve.Fori(0, 2) as m:
                    for e in range(E):
                        g, w = m * E + e, 1 - e % 2
                        normalised(g + 3, w, 0)
                        statistics(g + 3, w, 1)
                        attended(g + 1, w)
                        transposed(g + 2, 1 - w)
                        normalised(g + 3, w, 1)
                        statistics(g + 4, 1 - w, 0)
                        add_to_x(g)

            @block.gpsimd
            def _(pool):
                pool.wait_ge(primed, 2)

                def deviations(g, s):
                    pool.wait_ge(var_ready, 2 * g + s + 1)
                    nc.gpsimd.tensor_tensor(rstd[:, s, :], var[:, s, :], half[:, :], ALU.pow).then_inc(rstd_ready, 1)

                for g in range(3):
                    for s in range(2):
                        deviations(g, s)
                deviations(3, 0)
                with pool.Fori(0, 2) as m:
                    for e in range(E):
                        g = m * E + e
                        deviations(g + 3, 1)
                        deviations(g + 4, 0)

            @block.scalar
            def _(act):
                act.wait_ge(primed, 2)
                nc.scalar.activation(carrier[:, 2:3], carrier[:, 0:1], ACT.Gelu)
                act.wait_ge(k.ffn0_landed, k.ffn0_total)

                def hidden(g, e):
                    for c in range(H0):
                        act.wait_ge(hid_done, H0 * g + c + 1)
                        nc.scalar.activation(hid[:, c, :], hid_bank[c][:, 0:2 * P], ACT.Gelu, bias=k.b1[:, e, c:c + 1])\
                            .then_inc(hid_ready, 1)

                hidden(0, 0)
                with act.Fori(0, 2) as m:
                    for e in range(E):
                        g = m * E + e
                        act.wait_ge(eo_done, g + 1)
                        nc.scalar.activation(eoT[:, :], eo_bank[:, 0:2 * P], ACT.Identity, bias=k.b2[:, e:e + 1]).then_inc(eo_ready, 1)
                        act.wait_ge(next_done, g + 1)
                        nc.scalar.activation(outT[:, :], next_bank[:, 0:2 * P], ACT.Gelu, bias=k.ffn_cols[:, 3:4]).then_inc(outT_ready, 1)
                        hidden(g + 1, (e + 1) % E)

            @block.tensor
            def _(pe):
                pe.wait_ge(k.ffn0_landed, k.ffn0_total)

                def transpose(g, w):
                    pe.wait_ge(twice_ready, 2 * g + 2)
                    for s in range(2):
                        for u in range(2):
                            last = nc.tensor.transpose(t_bank[:, (2 * s + u) * P:(2 * s + u + 1) * P], xn[:, w, s, u, :], k.ident[:, :])
                    last.then_inc(T_moved, 1)

                def attend(g, w, back=True):
                    pe.wait_ge(T_ready, 2 * g + 2)
                    if back:
                        pe.wait_ge(x_done, 2 * g)
                    nc.tensor.matmul(attn_bank[:, 0:2 * P], k.attn_wT[:, :], znT[:, w, 1, :], start=True, stop=True).then_inc(attn_done, 1)

                def first_product(g, e):
                    pe.wait_ge(xa_ready, g + 1)
                    for c in range(H0):
                        nc.tensor.matmul(hid_bank[c][:, 0:2 * P], k.w1[:, e, c * P:c * P + P], xaT[:, :],
                                         start=True, stop=True).then_inc(hid_done, 1)

                transpose(0, 0)
                attend(0, 0, back=False)
                transpose(1, 1)
                first_product(0, 0)
                with pe.Fori(0, 2) as m:
                    for e in range(E):
                        g = m * E + e
                        for c in range(H0):
                            pe.wait_ge(hid_ready, H0 * g + c + 1)
                            last = nc.tensor.matmul(eo_bank[:, 0:2 * P], k.w2[:, e, c, :], hid[:, c, :], start=c == 0, stop=c == H0 - 1)
                        last.then_inc(eo_done, 1)
                        attend(g + 1, 1 - e % 2)
                        transpose(g + 2, e % 2)
                        pe.wait_ge(eo_ready, g + 1)
                        nc.tensor.matmul(next_bank[:, 0:2 * P], k.next_wT[:, :], eoT[:, :], start=True, stop=True).then_inc(next_done, 1)
                        first_product(g + 1, (e + 1) % E)
                        pe.wait_ge(outT_ready, g + 1)
                        for u in range(2):
                            last = nc.tensor.transpose(attn_bank[:, (2 + u) * P:(3 + u) * P], outT[:, u * P:u * P + P], k.ident[:, :])
                        last.then_inc(back_done, 1)


def second_attention(nc, k):
    Q = 4
    with ExitStack() as ctx:
        def sb(name, shape, dt=F32):
            return ctx.enter_context(nc.sbuf_tensor("l1_" + name, shape, dt))

        def sem(name):
            return ctx.enter_context(nc.semaphore("l1_" + name))

        carrier = sb("carrier", [P, 3])
        taker = sb("taker", [P, 2])
        bn = sb("bn", [P, 2, 6])
        stats = sb("stats", [P, 2, 2])
        work = sb("work", [P, 2, 4])
        xn = sb("xn", [P, 2, P])
        bias_row = sb("bias_row", [P, P])
        T_hi = sb("T_hi", [P, P], F16)
        T_lo = sb("T_lo", [P, P], F16)
        Y_hi = sb("Y_hi", [P, 2, H, P], F16)
        Y_lo = sb("Y_lo", [P, 2, H, P], F16)
        Z = sb("Z", [P, 2, H, P + 1])
        neg_max = sb("neg_max", [P, H])
        neg_maxT = sb("neg_maxT", [P, P], BF16)
        probs = sb("probs", [P, H, P])
        inv = sb("inv", [P, H])
        acc = sb("acc", [P, 2, P])
        tz_bank, y_bank = (ctx.enter_context(nc.psum_tensor(f"l1_{name}", [P, 512], F32)) for name in ("tz", "y"))
        a_bank, b_bank, pv_bank = (
            [ctx.enter_context(nc.psum_tensor(f"l1_{name}{n}", [P, 512], F32)) for n in range(2)]
            for name in ("a", "b", "pv"))
        names = ("primed bn_done stats_ready norm_step xn_ready bias_added T_moved T_hi_ready T_lo_ready y_done Y_hi_ready "
                 "Y_lo_ready z_done Z_ready scored max_ready maxT_moved maxT_ready shifted exp_done pv_done inv_ready "
                 "summed x_done").split()
        (primed, bn_done, stats_ready, norm_step, xn_ready, bias_added, T_moved, T_hi_ready, T_lo_ready, y_done, Y_hi_ready,
         Y_lo_ready, z_done, Z_ready, scored, max_ready, maxT_moved, maxT_ready, shifted, exp_done, pv_done, inv_ready,
         summed, x_done) = map(sem, names)
        def a_ring(w, unit):
            return a_bank[(w * (Q + 1) + unit) % 2]

        def row(t, n):
            return t[:, bass.ds(n, 1), 0:P].rearrange("p a n -> p (a n)")

        with nc.Block() as block:
            @block.vector
            def _(dve):
                nc.vector.memset(Z[:, :, :, P:P + 1], 1.0).then_inc(primed, 1)
                nc.vector.memset(neg_maxT[:, :], 0.0).then_inc(primed, 1)
                nc.vector.memset(work[:, :, 2:3], -0.5).then_inc(primed, 1)
                nc.vector.memset(carrier[:, 0:2], 0.0).then_inc(primed, 1)
                nc.vector.memset(work[:, :, 3:4], EPS).then_inc(primed, 1)
                nc.vector.tensor_scalar(bias_row[:, :], k.bo[:, 1, :], k.tg[:, 1:2], None, ALU.mult).then_inc(primed, 1)
                nc.vector.memset(taker[:, :], 0.0).then_inc(summed, 4)
                nc.vector.memset(acc[:, :, :], 0.0).then_inc(x_done, 2)
                dve.wait_ge(primed, 6)
                dve.wait_ge(summed, 4)
                dve.wait_ge(x_done, 2)

                def statistics(n, w):
                    nc.vector.bn_stats(bn[:, w, :], row(k.x_sb, n)).then_inc(bn_done, 1)
                    alone(nc, dve, carrier, bn_done, n + 1)
                    nc.vector.bn_aggr(stats[:, w, :], bn[:, w, :]).then_inc(stats_ready, 1)

                def transposed_lo(n):
                    dve.wait_ge(T_hi_ready, n + 1)
                    nc.vector.tensor_tensor(T_lo[:, :], tz_bank[:, 0:P], T_hi[:, :], ALU.subtract).then_inc(T_lo_ready, 1)

                def y_lo(n, w, q):
                    dve.wait_ge(Y_hi_ready, Q * n + q + 1)
                    nc.vector.tensor_tensor(Y_lo[:, w, Q * q:Q * q + Q].rearrange("p h n -> p (h n)"), y_bank[:, :],
                                            Y_hi[:, w, Q * q:Q * q + Q].rearrange("p h n -> p (h n)"), ALU.subtract)\
                        .then_inc(Y_lo_ready, 1)

                def maxima(n, w, q):
                    dve.wait_ge(scored, Q * n + q + 1)
                    nc.vector.tensor_reduce(neg_max[:, Q * q:Q * q + Q], a_ring(w, q)[:, :].rearrange("p (h n) -> p h n", h=Q),
                                            AX.X, ALU.max, negate=True).then_inc(max_ready, 1)

                def maxima_out(n, w):
                    dve.wait_ge(maxT_moved, n + 1)
                    nc.vector.tensor_copy(neg_maxT[0:H, :], a_ring(w, Q)[0:H, 0:P]).then_inc(maxT_ready, 1)

                def sums(n, w, m):
                    O = pv_bank[m % 2][:, 0:2 * (P + 1)].rearrange("p (h n) -> p h n", h=2)
                    dve.wait_ge(pv_done, 8 * n + m + 1)
                    nc.vector.reciprocal(inv[:, 2 * m:2 * m + 2], O[:, :, P]).then_inc(inv_ready, 1)
                    if m == 0:
                        dve.wait_ge(bias_added, n + 1)
                    dve.wait_ge(inv_ready, 8 * n + m + 1)
                    for h, total in enumerate((row(k.x_sb, n), acc[:, w, :])):
                        j = 2 * m + h
                        if m == 0 and h == 1:
                            dve.wait_ge(x_done, n + 1)
                            nc.vector.tensor_scalar(total, O[:, h, 0:P], inv[:, j:j + 1], None, ALU.mult).then_inc(summed, 1)
                            continue
                        if m:
                            dve.wait_ge(summed, 16 * n + j + 3)
                        nc.vector.scalar_tensor_tensor(out=total, in0=O[:, h, 0:P], scalar=inv[:, j:j + 1], in1=total,
                                                       op0=ALU.mult, op1=ALU.add).then_inc(summed, 1)

                statistics(0, 0)
                statistics(1, 1)
                transposed_lo(0)
                for q in range(Q):
                    y_lo(0, 0, q)
                    maxima(0, 0, q)
                maxima_out(0, 0)
                transposed_lo(1)
                with dve.Fori(0, PAIRS) as i:
                    for u in range(2):
                        n, f, w = 2 * i + u, 2 * i + u + 1, 1 - u
                        for q in range(Q):
                            y_lo(f, w, q)
                            if q:
                                sums(n, u, 2 * q - 2)
                                sums(n, u, 2 * q - 1)
                            else:
                                dve.wait_ge(xn_ready, n + 1)
                                statistics(n + 2, u)
                            maxima(f, w, q)
                        transposed_lo(f + 1)
                        maxima_out(f, w)
                        sums(n, u, 2 * Q - 2)
                        sums(n, u, 2 * Q - 1)

            @block.gpsimd
            def _(pool):
                pool.wait_ge(primed, 6)
                pool.wait_ge(summed, 4)

                def normal(n, w):
                    pool.wait_ge(stats_ready, n + 1)
                    normalise(nc, pool, stats[:, w, :], row(k.x_sb, n), xn[:, w, :], work[:, w, :], norm_step, 3 * n).then_inc(xn_ready, 1)

                normal(0, 0)
                normal(1, 1)
                with pool.Fori(0, PAIRS) as i:
                    for u in range(2):
                        n = 2 * i + u
                        pool.wait_ge(xn_ready, n + 1)
                        nc.gpsimd.tensor_tensor(row(k.x_sb, n), row(k.x_sb, n), bias_row[:, :], ALU.add).then_inc(bias_added, 1)
                        pool.wait_ge(T_moved, n + 1)
                        normal(n + 2, u)
                        pool.wait_ge(summed, 16 * n + 20)
                        nc.gpsimd.tensor_tensor(taker[:, 1:2], taker[:, 0:1], taker[:, 0:1], ALU.add)
                        nc.gpsimd.tensor_tensor(row(k.x_sb, n), row(k.x_sb, n), acc[:, u, :], ALU.add).then_inc(x_done, 1)

            @block.scalar
            def _(act):
                act.wait_ge(primed, 6)
                nc.scalar.activation(carrier[:, 2:3], carrier[:, 0:1], ACT.Exp).then_inc(exp_done, 2)

                def transposed_hi(n):
                    act.wait_ge(T_moved, n + 1)
                    nc.scalar.activation(T_hi[:, :], tz_bank[:, 0:P], ACT.Copy).then_inc(T_hi_ready, 1)

                def y_hi(n, w, q):
                    act.wait_ge(y_done, Q * n + q + 1)
                    nc.scalar.activation(Y_hi[:, w, Q * q:Q * q + Q].rearrange("p h n -> p (h n)"), y_bank[:, :], ACT.Copy)\
                        .then_inc(Y_hi_ready, 1)

                def z_out(n, w, q):
                    act.wait_ge(z_done, Q * n + q + 1)
                    nc.scalar.activation(Z[:, w, Q * q:Q * q + Q, 0:P], tz_bank[:, :].rearrange("p (h n) -> p h n", h=Q), ACT.Copy)\
                        .then_inc(Z_ready, 1)

                transposed_hi(0)
                for q in range(Q):
                    y_hi(0, 0, q)
                    z_out(0, 0, q)
                transposed_hi(1)
                with act.Fori(0, PAIRS) as i:
                    for u in range(2):
                        n, f, w = 2 * i + u, 2 * i + u + 1, 1 - u
                        for q in range(Q):
                            y_hi(f, w, q)
                            act.wait_ge(shifted, Q * n + q + 1)
                            nc.scalar.activation(probs[:, Q * q:Q * q + Q, :].rearrange("p h n -> p (h n)"), b_bank[q % 2][:, :], ACT.Exp)\
                                .then_inc(exp_done, 1)
                            z_out(f, w, q)
                        transposed_hi(f + 1)

            @block.tensor
            def _(pe):
                pe.wait_ge(primed, 6)

                def transpose(n, w, wait=True):
                    pe.wait_ge(xn_ready, n + 1)
                    if wait:
                        pe.wait_ge(Z_ready, Q * n)
                    nc.tensor.transpose(tz_bank[:, 0:P], xn[:, w, :], k.ident[:, :]).then_inc(T_moved, 1)

                def project_x(n, w, q, wait=True):
                    if q == 0:
                        pe.wait_ge(T_lo_ready, n + 1)
                    if q or wait:
                        pe.wait_ge(Y_lo_ready, Q * n + q)
                    for h in range(Q):
                        last = both_products(nc, y_bank[:, h * P:h * P + P],
                                             [(m[:, Q * q + h, :], t[:, :]) for m, t in ((k.A_hi, T_hi), (k.A_lo, T_hi), (k.A_hi, T_lo))])
                    last.then_inc(y_done, 1)

                def project_context(n, w, q):
                    if q:
                        pe.wait_ge(Z_ready, Q * n + q)
                    else:
                        pe.wait_ge(T_lo_ready, n + 1)
                    last = both_products(nc, tz_bank[:, :],
                                         [(row(c, n), m[:, Q * q:Q * q + Q, :].rearrange("p h n -> p (h n)"))
                                          for c, m in ((k.cT_hi, k.M_hi), (k.cT_hi, k.M_lo), (k.cT_lo, k.M_hi))])
                    last.then_inc(z_done, 1)

                def score_by_query(n, w, q, wait=True):
                    pe.wait_ge(Y_hi_ready, Q * n + q + 1)
                    if q == 1 and wait:
                        pe.wait_ge(maxT_ready, n)
                    elif q >= 2:
                        pe.wait_ge(max_ready, Q * n + q - 1)
                    for h in range(Q):
                        last = nc.tensor.matmul(a_ring(w, q)[:, h * P:h * P + P], Y_hi[:, w, Q * q + h, :], row(k.cT_hi, n),
                                                start=True, stop=True)
                    last.then_inc(scored, 1)

                def transpose_maxima(n, w):
                    pe.wait_ge(max_ready, Q * n + Q)
                    nc.tensor.transpose(a_ring(w, Q)[0:H, 0:P], neg_max[:, :], k.ident[:, :]).then_inc(maxT_moved, 1)

                def score_by_key(n, w, q):
                    out = b_bank[q % 2]
                    if q == 0:
                        pe.wait_ge(maxT_ready, n + 1)
                    pe.wait_ge(exp_done, Q * n + q + 1)
                    for h in range(Q):
                        nc.tensor.matmul(out[:, h * P:h * P + P], k.pick_head[:, Q * q + h, :], neg_maxT[:, :],
                                         start=h == 0, stop=False, skip_group_check=True)
                    last = both_products(nc, out[:, :], [(row(c, n), y[:, w, Q * q:Q * q + Q, :].rearrange("p h n -> p (h n)"))
                                                         for c, y in ((k.cT_hi, Y_hi), (k.cT_hi, Y_lo), (k.cT_lo, Y_hi))], start=False)
                    last.then_inc(shifted, 1)

                def weigh(n, w, m):
                    if m % 2 == 0:
                        pe.wait_ge(exp_done, Q * n + m // 2 + 3)
                    pe.wait_ge(summed, 16 * n + 2 * m + 2)
                    for h in range(2):
                        last = nc.tensor.matmul(pv_bank[m % 2][:, h * (P + 1):(h + 1) * (P + 1)], probs[:, 2 * m + h, :],
                                                Z[:, w, 2 * m + h, :], start=True, stop=True)
                    last.then_inc(pv_done, 1)

                transpose(0, 0, wait=False)
                for q in range(Q):
                    project_x(0, 0, q, wait=False)
                    project_context(0, 0, q)
                    score_by_query(0, 0, q, wait=False)
                transpose_maxima(0, 0)
                transpose(1, 1)
                with pe.Fori(0, PAIRS) as i:
                    for u in range(2):
                        n, f, w = 2 * i + u, 2 * i + u + 1, 1 - u
                        for q in range(Q):
                            project_x(f, w, q)
                            score_by_key(n, u, q)
                            if q == 1:
                                pe.wait_ge(Z_ready, Q * n + Q)
                            if q:
                                weigh(n, u, 2 * q - 2)
                            project_context(f, w, q)
                            if q:
                                weigh(n, u, 2 * q - 1)
                            score_by_query(f, w, q)
                        transpose(f + 1, u)
                        weigh(n, u, 2 * Q - 2)
                        weigh(n, u, 2 * Q - 1)
                        transpose_maxima(f, w)


def route(nc, k):
    N = 4
    STEPS = B // N
    BE = B * E
    with ExitStack() as ctx:
        def sb(name, shape, dt=F32):
            return ctx.enter_context(nc.sbuf_tensor("r_" + name, shape, dt))

        def sem(name):
            return ctx.enter_context(nc.semaphore("r_" + name))

        xs = sb("xs", [P, 2, N, P])
        xT = sb("xT", [P, 2, N * P])
        best = sb("best", [P, B])
        equal = sb("equal", [P, B, E])
        less8 = sb("less8", [P, E])
        first = sb("first", [P, B])
        onehot = sb("onehot", [P, B, E], BF16)
        before = sb("before", [P, P], BF16)
        ones = sb("ones", [P, P], BF16)
        totals = sb("totals", [P, B, E])
        runs = sb("runs", [P, 2, 16 + B, E])
        tiles_i = sb("tiles_i", [P, E], mybir.dt.int32)
        tiles = sb("tiles", [P, E])
        ends = sb("ends", [P, 2, 4 + E])
        place = sb("place", [P, B, E])
        slot = sb("slot", [P, B])
        slot_i = sb("slot_i", [P, B], mybir.dt.uint32)
        tile_no = sb("tile_no", [1, TILES, E])
        tile_no_i = sb("tile_no_i", [1, TILES, E], mybir.dt.int32)
        passed = sb("passed", [1, TILES, E])
        owner = sb("owner", [1, TILES])
        bank = [ctx.enter_context(nc.psum_tensor(f"r_bank{n}", [P, 512], F32)) for n in range(5)]
        names = "primed ones_ready copied T_moved xT_ready routed chose ranked step slots_ready scattered".split()
        primed, ones_ready, copied, T_moved, xT_ready, routed, chose, ranked, step, slots_ready, scattered = map(sem, names)

        with nc.Block() as block:
            @block.scalar
            def _(act):
                with act.Fori(0, STEPS // 2) as i:
                    for w in range(2):
                        act.wait_ge(T_moved, 2 * i + w + 1)
                        nc.scalar.activation(xs[:, w, :, :], k.x_sb[:, bass.ds(2 * N * i + N * w, N), 0:P], ACT.Copy).then_inc(copied, 1)

            @block.tensor
            def _(pe):
                pe.wait_ge(primed, 10)
                logits = bank[4][:, 0:BE]
                with pe.Fori(0, STEPS // 2) as i:
                    for w in range(2):
                        pe.wait_ge(copied, 2 * i + w + 1)
                        pe.wait_ge(xT_ready, 2 * i + w + 1)
                        for u in range(N):
                            last = nc.tensor.transpose(bank[w][:, u * P:u * P + P], xs[:, w, u, :], k.ident[:, :])
                        last.then_inc(T_moved, 1)
                    for w in range(2):
                        pe.wait_ge(xT_ready, 2 * i + w + 3)
                        for u in range(N):
                            last = nc.tensor.matmul(bank[4][:, bass.ds((2 * N * i + N * w + u) * E, E)], xT[:, w, u * P:u * P + P],
                                                    k.routerT[:, :], start=True, stop=True)
                        last.then_inc(routed, 1)
                pe.wait_ge(chose, 1)
                pe.wait_ge(ones_ready, 2)
                oh = onehot[:, :, :].rearrange("p b e -> p (b e)")
                nc.tensor.matmul(bank[2][:, 0:BE], before[:, :], oh, start=True, stop=True).then_inc(ranked, 1)
                nc.tensor.matmul(bank[3][:, 0:BE], ones[:, :], oh, start=True, stop=True).then_inc(ranked, 1)

            @block.gpsimd
            def _(pool):
                nc.gpsimd.memset(before[:, :], 1.0).then_inc(ones_ready, 1)
                nc.gpsimd.iota(tile_no_i[:, :, :], pattern=[[1, TILES], [0, E]], base=0, channel_multiplier=0).then_inc(primed, 1)
                pool.wait_ge(ones_ready, 1)
                nc.gpsimd.affine_select(out=before[:, :], in_=before[:, :], compare_op=ALU.is_gt, fill=0.0, base=0,
                                        pattern=[[1, P]], channel_multiplier=-1).then_inc(ones_ready, 1)
                pool.wait_ge(slots_ready, 1)
                pool.wait_ge(k.rows_cleared, 16)
                for b in range(B):
                    nc.gpsimd.indirect_dma_start(k.sorted_rows[:, :], bass.IndirectOffsetOnAxis(slot_i[:, b:b + 1], 0),
                                                 k.x_sb[:, b, :], None).then_inc(scattered, 16)
                pool.wait_ge(scattered, 16 * B)

            @block.vector
            def _(dve):
                nc.vector.memset(ones[:, :], 1.0).then_inc(primed, 1)
                for e in range(E):
                    nc.vector.memset(less8[:, e:e + 1], float(e - E)).then_inc(primed, 1)
                nc.vector.memset(runs[:, :, 0:16, :], 0.0).then_inc(T_moved, 1)
                nc.vector.memset(ends[:, :, 0:4], 0.0).then_inc(T_moved, 1)
                nc.vector.memset(first[:, 0:1], 0.0).then_inc(xT_ready, 2)
                with dve.Fori(0, STEPS // 2) as i:
                    for w in range(2):
                        dve.wait_ge(T_moved, 2 * i + w + 3)
                        nc.vector.tensor_copy(xT[:, w, :], bank[w][:, :]).then_inc(xT_ready, 1)
                steps = [0]

                def then(ins):
                    steps[0] += 1
                    ins.then_inc(step, 1)
                    dve.wait_ge(step, steps[0])

                def over(t, axis):
                    return t.rearrange("p (a e) -> p a e", a=1).broadcast_to([P, B, E]) if axis == 1 else \
                        t.rearrange("p (b a) -> p b a", a=1).broadcast_to([P, B, E])

                dve.wait_ge(routed, STEPS)
                dve.wait_ge(primed, 10)
                logits = bank[4][:, 0:BE].rearrange("p (b e) -> p b e", b=B)
                then(nc.vector.tensor_reduce(best[:, :], logits, AX.X, ALU.max))
                then(nc.vector.tensor_tensor(equal[:, :, :], logits, over(best[:, :], 2), ALU.is_equal))
                then(nc.vector.tensor_tensor(place[:, :, :], equal[:, :, :], over(less8[:, :], 1), ALU.mult))
                then(nc.vector.tensor_reduce(first[:, :], place[:, :, :], AX.X, ALU.min))
                nc.vector.tensor_tensor(onehot[:, :, :], over(less8[:, :], 1), over(first[:, :], 2), ALU.is_equal).then_inc(chose, 1)
                dve.wait_ge(ranked, 2)
                dve.wait_ge(chose, 1)
                nc.vector.tensor_copy(totals[:, :, :], bank[3][:, 0:BE].rearrange("p (b e) -> p b e", b=B)).then_inc(chose, 1)
                then(nc.vector.tensor_copy(runs[:, 0, 16:16 + B, :], bank[3][:, 0:BE].rearrange("p (b e) -> p b e", b=B)))
                for n in range(5):
                    old, new, d = runs[:, n % 2], runs[:, 1 - n % 2], 2 ** n
                    then(nc.vector.tensor_tensor(new[:, 16:16 + B, :], old[:, 16:16 + B, :], old[:, 16 - d:16 - d + B, :], ALU.add))
                run = runs[:, 1]
                then(nc.vector.tensor_scalar(tiles_i[:, :], run[:, 16 + B - 1, :], float(P - 1), None, ALU.add))
                then(nc.vector.tensor_scalar(tiles_i[:, :], tiles_i[:, :], 7, None, ALU.arith_shift_right))
                then(nc.vector.tensor_copy(tiles[:, :], tiles_i[:, :]))
                then(nc.vector.tensor_copy(ends[:, 0, 4:4 + E], tiles[:, :]))
                for n in range(3):
                    old, new, d = ends[:, n % 2], ends[:, 1 - n % 2], 2 ** n
                    then(nc.vector.tensor_tensor(new[:, 4:4 + E], old[:, 4:4 + E], old[:, 4 - d:4 - d + E], ALU.add))
                end = ends[:, 1, 4:4 + E]
                then(nc.vector.tensor_tensor(tiles[:, :], end, tiles[:, :], ALU.subtract))
                then(nc.vector.tensor_scalar(tiles[:, :], tiles[:, :], float(P), None, ALU.mult))
                then(nc.vector.tensor_tensor(totals[:, :, :], run[:, 16:16 + B, :], totals[:, :, :], ALU.subtract))
                then(nc.vector.tensor_tensor(place[:, :, :], totals[:, :, :], over(tiles[:, :], 1), ALU.add))
                then(nc.vector.tensor_tensor(place[:, :, :], bank[2][:, 0:BE].rearrange("p (b e) -> p b e", b=B), place[:, :, :], ALU.add))
                then(nc.vector.tensor_tensor(place[:, :, :], place[:, :, :], onehot[:, :, :], ALU.mult))
                then(nc.vector.tensor_reduce(slot[:, :], place[:, :, :], AX.X, ALU.add))
                nc.vector.tensor_copy(slot_i[:, :], slot[:, :]).then_inc(slots_ready, 1)
                then(nc.vector.tensor_copy(tile_no[:, :, :], tile_no_i[:, :, :]))
                ends_all = end[0:1, :].rearrange("p (a e) -> p a e", a=1).broadcast_to([1, TILES, E])
                then(nc.vector.tensor_tensor(passed[:, :, :], ends_all, tile_no[:, :, :], ALU.is_le))
                then(nc.vector.tensor_reduce(owner[:, :], passed[:, :, :], AX.X, ALU.add))
                then(nc.vector.tensor_scalar(k.tile_expert[:, :], owner[:, :], float(E - 1), None, ALU.min))


def second_ffn(nc, k, out):
    U = 3
    STEPS = TILES // U
    IP = 3 * P
    with ExitStack() as ctx:
        def sb(name, shape, dt=F32):
            return ctx.enter_context(nc.sbuf_tensor("f1_" + name, shape, dt))

        def sem(name):
            return ctx.enter_context(nc.semaphore("f1_" + name))

        rows = sb("rows", [P, TILES + U, ROW])
        carrier = sb("carrier", [P, 3])
        bn = sb("bn", [P, U, 6])
        stats = sb("stats", [P, U, 2])
        var = sb("var", [P, U])
        half = sb("half", [P, U])
        rstd = sb("rstd", [P, U])
        hn = sb("hn", [P, U, P])
        hT = sb("hT", [P, U * P])
        silu = sb("silu", [P, U, I1])
        hid = sb("hid", [P, U, IP])
        hidT = sb("hidT", [P, U, IP])
        result = sb("result", [P, U, P])
        taker = sb("taker", [P, 3])
        token = sb("token", [P, U], mybir.dt.uint32)
        bank = [ctx.enter_context(nc.psum_tensor(f"f1_bank{n}", [P, 512], F32)) for n in range(8)]
        names = ("primed landed bn_done var_ready rstd_ready hn_ready T_moved hT_ready gate_done up_done silu_ready hid_ready "
                 "hidT_moved hidT_ready down_done result_ready result_free stored").split()
        (primed, landed, bn_done, var_ready, rstd_ready, hn_ready, T_moved, hT_ready, gate_done, up_done, silu_ready, hid_ready,
         hidT_moved, hidT_ready, down_done, result_ready, result_free, stored) = map(sem, names)

        with nc.Block() as block:
            @block.sync
            def _(sp):
                with sp.Fori(0, STEPS + 1) as i:
                    sp.wait_ge(landed, 16 * (i + 1))
                    sp.dma_start(rows[:, bass.ts(i, U), :],
                                 k.sorted_rows[bass.ts(i, U * P), :].rearrange("(j p) w -> p j w", p=P)).then_inc(landed, 16)

            @block.vector
            def _(dve):
                nc.vector.memset(hn[:, :, :], 0.0).then_inc(primed, 1)
                nc.vector.memset(carrier[:, 0:2], 0.0).then_inc(primed, 1)
                nc.vector.memset(var[:, :], 1.0).then_inc(landed, 16)
                nc.vector.memset(half[:, :], -0.5).then_inc(result_ready, 2 * U)
                nc.vector.memset(hid[:, :, I1:IP], 0.0).then_inc(primed, 1)
                dve.wait_ge(primed, 3)

                def statistics(i):
                    dve.wait_ge(landed, 16 * (i + 2))
                    for v in range(U):
                        nc.vector.bn_stats(bn[:, v, :], rows[:, bass.ds(U * i + v, 1), 0:P]).then_inc(bn_done, 1)
                    alone(nc, dve, carrier, bn_done, U * i + U)
                    for v in range(U):
                        nc.vector.bn_aggr(stats[:, v, :], bn[:, v, :]).then_inc(var_ready, 1)
                    dve.wait_ge(var_ready, (U + 1) * i + U)
                    nc.vector.tensor_scalar(var[:, :], stats[:, :, 1], EPS, None, ALU.add).then_inc(var_ready, 1)

                def normalised(i):
                    dve.wait_ge(rstd_ready, i + 1)
                    for v in range(U):
                        nc.vector.tensor_scalar(hn[:, v, :], rows[:, bass.ds(U * i + v, 1), 0:P].rearrange("p a n -> p (a n)"),
                                                stats[:, v, 0:1], rstd[:, v:v + 1], ALU.subtract, ALU.mult).then_inc(hn_ready, 1)

                statistics(0)
                normalised(0)
                with dve.Fori(0, STEPS) as i:
                    dve.wait_ge(T_moved, i + 1)
                    nc.vector.tensor_copy(hT[:, :], bank[0][:, 0:U * P]).then_inc(hT_ready, 1)
                    statistics(i + 1)
                    for v in range(U):
                        dve.wait_ge(silu_ready, U * i + v + 1)
                        dve.wait_ge(up_done, U * i + v + 1)
                        nc.vector.tensor_tensor(hid[:, v, 0:I1], bank[2 + 2 * v][:, 0:I1], silu[:, v, :], ALU.mult).then_inc(hid_ready, 1)
                    normalised(i + 1)
                    dve.wait_ge(result_free, i + 1)
                    for v in range(U):
                        dve.wait_ge(down_done, U * i + v + 1)
                        nc.vector.tensor_copy(token[:, v:v + 1], rows[:, bass.ds(U * i + v, 1), P]).then_inc(result_ready, 1)
                        nc.vector.scalar_tensor_tensor(out=result[:, v, :], in0=bank[2 + 2 * v][:, 0:P], scalar=k.tg[:, 3:4],
                                                       in1=rows[:, bass.ds(U * i + v, 1), 0:P].rearrange("p a n -> p (a n)"),
                                                       op0=ALU.mult, op1=ALU.add).then_inc(result_ready, 1)

            @block.gpsimd
            def _(pool):
                pool.wait_ge(primed, 3)
                nc.gpsimd.memset(taker[:, :], 0.0).then_inc(result_free, 1)
                last_row = pool.to_reg(B * P - 1)
                pool.wait_ge(result_free, 1)

                def deviation(i):
                    pool.wait_ge(var_ready, (U + 1) * (i + 1))
                    nc.gpsimd.tensor_tensor(rstd[:, :], var[:, :], half[:, :], ALU.pow).then_inc(rstd_ready, 1)

                pool.wait_ge(result_ready, 2 * U)
                deviation(0)
                with pool.Fori(0, STEPS) as i:
                    deviation(i + 1)
                    pool.wait_ge(result_ready, 2 * U * (i + 2))
                    nc.gpsimd.tensor_tensor(taker[:, 1:2], taker[:, 0:1], taker[:, 0:1], ALU.add)
                    for v in range(U):
                        nc.gpsimd.indirect_dma_start(out, bass.IndirectOffsetOnAxis(token[:, v:v + 1], 0), result[:, v, :], None,
                                                     bounds_check=last_row, oob_is_err=False).then_inc(stored, 16)
                    pool.wait_ge(stored, 16 * U * (i + 1))
                    nc.gpsimd.tensor_tensor(taker[:, 2:3], taker[:, 0:1], taker[:, 0:1], ALU.add).then_inc(result_free, 1)
                pool.wait_ge(stored, 16 * TILES)

            @block.scalar
            def _(act):
                act.wait_ge(primed, 3)
                nc.scalar.activation(carrier[:, 2:3], carrier[:, 0:1], ACT.Silu)
                with act.Fori(0, STEPS) as i:
                    for v in range(U):
                        act.wait_ge(gate_done, U * i + v + 1)
                        nc.scalar.activation(silu[:, v, :], bank[1 + 2 * v][:, 0:I1], ACT.Silu).then_inc(silu_ready, 1)
                    for v in range(U):
                        act.wait_ge(hidT_moved, U * i + v + 1)
                        nc.scalar.activation(hidT[:, v, :], bank[1 + 2 * v][:, 0:IP], ACT.Copy).then_inc(hidT_ready, 1)

            @block.tensor
            def _(pe):
                pe.wait_ge(primed, 3)
                with pe.Fori(0, STEPS) as i:
                    experts = [pe.value_load(k.tile_expert[0:1, bass.ds(U * i + v, 1)], min_val=0, max_val=E - 1) for v in range(U)]
                    pe.wait_ge(hn_ready, U * (i + 1))
                    for v in range(U):
                        last = nc.tensor.transpose(bank[0][:, v * P:v * P + P], hn[:, v, :], k.ident[:, :])
                    last.then_inc(T_moved, 1)
                    pe.wait_ge(hT_ready, i + 1)
                    for v in range(U):
                        for w, base, done in ((k.gateT, 1, gate_done), (k.upT, 2, up_done)):
                            if w is k.upT:
                                pe.wait_ge(result_ready, 2 * (U * i + v + 1))
                            nc.tensor.matmul(bank[base + 2 * v][:, 0:I1], hT[:, v * P:v * P + P],
                                             w[:, bass.ds(experts[v], 1), :].rearrange("p a n -> p (a n)"),
                                             start=True, stop=True).then_inc(done, 1)
                    for v in range(U):
                        pe.wait_ge(hid_ready, U * i + v + 1)
                        for c in range(3):
                            last = nc.tensor.transpose(bank[1 + 2 * v][:, c * P:c * P + P], hid[:, v, c * P:c * P + P], k.ident[:, :])
                        last.then_inc(hidT_moved, 1)
                    for v in range(U):
                        pe.wait_ge(hidT_ready, U * i + v + 1)
                        for c in range(3):
                            last = nc.tensor.matmul(bank[2 + 2 * v][:, 0:P], hidT[:, v, c * P:c * P + P],
                                                    k.downT[:, c, bass.ds(experts[v], 1), :].rearrange("p a n -> p (a n)"),
                                                    start=c == 0, stop=c == 2)
                        last.then_inc(down_done, 1)


def build(nc, A, out):
    with ExitStack() as ctx:
        k = Setup()
        load_and_prepare(nc, ctx, A, k)
        first_attention(nc, k)
        first_ffn(nc, k)
        second_attention(nc, k)
        route(nc, k)
        second_ffn(nc, k, out.rearrange("b t d -> (b t) d"))


_NAMES = ['x', 'ctx_1024', 'g_xattn', 'g_ffn', 'L0_xattn_Wq', 'L0_xattn_bq', 'L0_xattn_Wk', 'L0_xattn_bk', 'L0_xattn_Wv',
          'L0_xattn_bv', 'L0_xattn_Wo', 'L0_xattn_bo', 'L0_ffn_ln_scale', 'L0_ffn_ln_bias', 'L0_ffn_attn_w', 'L0_ffn_attn_b',
          'L0_ffn_w1', 'L0_ffn_b1', 'L0_ffn_w2', 'L0_ffn_b2', 'L0_ffn_next_w', 'L0_ffn_next_b', 'L1_xattn_Wq', 'L1_xattn_Wk',
          'L1_xattn_Wv', 'L1_xattn_Wo', 'L1_xattn_bo', 'L1_ffn_router_w', 'L1_ffn_gate_w', 'L1_ffn_up_w', 'L1_ffn_down_w']


def kernel(**inputs):
    import concourse.bacc as bacc
    from concourse.bass_utils import run_bass_kernel_spmd

    nc = bacc.Bacc("TRN2", target_bir_lowering=False, num_devices=1)
    arrays, A = {}, {}
    for name in _NAMES:
        a = np.ascontiguousarray(inputs[name])
        arrays["in_" + name] = a
        A[name] = nc.dram_tensor("in_" + name, a.shape, mybir.dt.from_np(a.dtype), kind="ExternalInput").ap()
    out = nc.dram_tensor("out", (B, P, P), F32, kind="ExternalOutput").ap()
    build(nc, A, out)
    r = run_bass_kernel_spmd(nc, [arrays], core_ids=[0])
    return r.results[0]["out"]
```

```python
from contextlib import ExitStack
import numpy as np
import concourse.bass as bass
from concourse import mybir

ALU = mybir.AluOpType
ACT = mybir.ActivationFunctionType
F32 = mybir.dt.float32
F16 = mybir.dt.float16
BF16 = mybir.dt.bfloat16
I32 = mybir.dt.int32
AX = mybir.AxisListType

P = 128
B = 32
PAIRS = B // 2
H = 16
D0 = P // H
G = 32
HD1 = 64
E = 8
H0 = 4
I1 = 352
CHUNKS = ((0, 128), (128, 128), (256, 96))
EPS = 1e-5
TILES = B + E - 1
AHEAD = 8
TILES_STEP = 3
LISTED = TILES + 2 * TILES_STEP
REGION = B * P + P
CONSTS = 3 + 3 * E + TILES_STEP
ROW = P + 4


def both_products(nc, out, pairs, start=True, stop=True):
    last = None
    for n, (lhsT, rhs) in enumerate(pairs):
        last = nc.tensor.matmul(out, lhsT, rhs, start=start and n == 0, stop=stop and n == len(pairs) - 1,
                                skip_group_check=True)
    return last


class Setup:
    pass


def prepare(nc, ctx, raw, A, k):
    def sb(name, shape, dt=F32):
        return ctx.enter_context(nc.sbuf_tensor(name, shape, dt))

    k.x_sb = sb("x_sb", [P, B + AHEAD, ROW])
    k.ctx_sb = sb("ctx_sb", [P, B + 3, P])
    k.cT = sb("cT", [P, 2, B + 2, P], F16)
    k.cT_hi, k.cT_lo = k.cT[:, 0], k.cT[:, 1]
    k.ident = sb("ident", [P, P])
    k.gates = sb("gates", [P, 4])
    k.tg = sb("tg", [P, 4])
    k.pick_head = sb("pick_head", [P, H, P], BF16)
    k.stack_sel = sb("stack_sel", [P, 4, H, 4, D0], F16)
    k.w0T_hi = sb("w0T_hi", [P, 3, P], F16)
    k.w0T_lo = sb("w0T_lo", [P, 3, P], F16)
    k.wo0 = sb("wo0", [P, P])
    k.bias0 = sb("bias0", [P, 3])
    k.bv0 = sb("bv0", [P, P])
    k.bo = sb("bo", [P, 2, P])
    k.attn_wT = sb("attn_wT", [P, P])
    k.next_wT = sb("next_wT", [P, P])
    k.ffn_cols = sb("ffn_cols", [P, 4])
    k.b1 = sb("b1", [P, E, H0])
    k.b2 = sb("b2", [P, E])
    k.w1 = sb("w1", [P, E, H0 * P])
    k.w2 = sb("w2", [P, E, H0, P])
    k.AM = sb("AM", [P, 4, H, P], F16)
    k.A_hi, k.A_lo = k.AM[:, 0], k.AM[:, 1]
    k.M_hi, k.M_lo = k.AM[:, 2], k.AM[:, 3]
    k.gate_hi = sb("gate_hi", [P, E, I1], F16)
    k.gate_lo = sb("gate_lo", [P, E, I1], F16)
    k.up_hi = sb("up_hi", [P, E, I1], F16)
    k.up_lo = sb("up_lo", [P, E, I1], F16)
    k.downT = sb("downT", [P, 3, E, P])
    k.routerT = sb("routerT", [P, E])
    k.tile_expert = sb("tile_expert", [1, TILES // TILES_STEP], I32)
    k.tile_row = sb("tile_row", [1, LISTED], I32)
    k.empty_row = sb("empty_row", [P, ROW])
    k.expert_rows = nc.dram_tensor("expert_rows", (E * REGION + (LISTED - B) * P, ROW), F32, kind="Internal").ap()
    k.rows_cleared = ctx.enter_context(nc.semaphore("rows_cleared"))
    k.x_landed = ctx.enter_context(nc.semaphore("x_landed"))
    k.ffn0_landed = ctx.enter_context(nc.semaphore("ffn0_landed"))

    k.big = raw.enter_context(nc.sbuf_tensor("big", [P, 3, H * HD1], F32))
    k.big_out = raw.enter_context(nc.sbuf_tensor("big_out", [P, 8, P], F32))
    k.gu = raw.enter_context(nc.sbuf_tensor("gu", [P, 2, 3, E, P], F32))
    k.down = k.AM[:, :, :, :].rearrange("p a h n -> p (a h n)").bitcast(F32)[:, 0:E * I1].rearrange("p (e i) -> p e i", e=E)
    k.late_landed = ctx.enter_context(nc.semaphore("late_landed"))

    with ExitStack() as tmp:
        def tb(name, shape, dt=F32):
            return tmp.enter_context(nc.sbuf_tensor(name, shape, dt))

        def sem(name):
            return tmp.enter_context(nc.semaphore(name))

        small = tb("small", [P, 6, P])
        numbers = tb("numbers", [P, B], I32)
        router = tb("router", [E, P])
        router_c = tb("router_c", [E, P])
        router_bn = tb("router_bn", [E, 8])
        banks = [tmp.enter_context(nc.psum_tensor(f"setup_bank{n}", [P, 512], F32)) for n in range(7)]
        names = "small_landed g_landed tg_ready zeroed const_ready moved_ready split_hi numbered centred".split()
        small_landed, g_landed, tg_ready, zeroed, const_ready, moved_ready, split_hi, numbered, centred = map(sem, names)

        with nc.Block() as block:
            @block.sync
            def _(sp):
                for g, name in enumerate(("g_xattn", "g_ffn")):
                    sp.dma_start(k.gates[:, 2 * g:2 * g + 2], on_all(A[name])).then_inc(g_landed, 16)
                for n, name in enumerate(("L0_xattn_Wq", "L0_xattn_Wk", "L0_xattn_Wv", "L0_xattn_Wo",
                                          "L0_ffn_attn_w", "L0_ffn_next_w")):
                    sp.dma_start(small[:, n, :], A[name]).then_inc(small_landed, 16)
                sp.dma_start(router[:, :], A["L1_ffn_router_w"]).then_inc(small_landed, 16)
                load_tokens(sp, A, k, 0, k.x_landed)
                for n, name in enumerate(("L0_xattn_bq", "L0_xattn_bk")):
                    sp.dma_start(k.bias0[:, n:n + 1], column(A[name])).then_inc(k.x_landed, 16)
                sp.dma_start(k.bv0[:, :], on_all(A["L0_xattn_bv"])).then_inc(k.x_landed, 16)
                for n, name in enumerate(("L0_xattn_bo", "L1_xattn_bo")):
                    sp.dma_start(k.bo[:, n, :], on_all(A[name])).then_inc(k.x_landed, 16)
                sp.wait_ge(zeroed, 8)
                sp.dma_start(k.expert_rows[E * REGION:, :].rearrange("(j p) w -> p j w", p=P),
                             k.empty_row[:, :].rearrange("p (a w) -> p a w", a=1).broadcast_to([P, LISTED - B, ROW])).then_inc(k.rows_cleared, 16)

            @block.gpsimd
            def _(pool):
                nc.gpsimd.memset(k.ident[:, :], 0.0).then_inc(const_ready, 1)
                nc.gpsimd.iota(numbers[:, :], pattern=[[P, B]], base=0, channel_multiplier=1).then_inc(numbered, 1)
                pool.wait_ge(const_ready, 1)
                nc.gpsimd.affine_select(out=k.ident[:, :], in_=k.ident[:, :], compare_op=ALU.not_equal, fill=1.0,
                                        base=0, pattern=[[-1, P]], channel_multiplier=1).then_inc(const_ready, 1)
                pool.wait_ge(zeroed, 2)
                for n, copies in enumerate((slice(0, 4, 2), slice(1, 4, 2), slice(0, 2), slice(2, 4))):
                    part = k.stack_sel[:, n, :, copies, :]
                    nc.gpsimd.affine_select(out=part, in_=part, compare_op=ALU.not_equal, fill=1.0, base=0,
                                            pattern=[[-D0, H], [0, 2], [-1, D0]], channel_multiplier=1)\
                        .then_inc(const_ready, 1)
                nc.gpsimd.affine_select(out=k.pick_head[:, :, :], in_=k.pick_head[:, :, :], compare_op=ALU.not_equal,
                                        fill=1.0, base=0, pattern=[[-1, H], [0, P]], channel_multiplier=1)\
                    .then_inc(const_ready, 1)
                pool.wait_ge(const_ready, 7)

            @block.scalar
            def _(act):
                act.wait_ge(g_landed, 32)
                nc.scalar.activation(k.tg[:, :], k.gates[:, :], ACT.Tanh).then_inc(tg_ready, 1)

            @block.tensor
            def _(pe):
                pe.wait_ge(const_ready, 2)
                pe.wait_ge(small_landed, 16 * 7)
                for n in range(6):
                    nc.tensor.transpose(banks[n][:, 0:P], small[:, n, :], k.ident[:, :]).then_inc(moved_ready, 1)
                pe.wait_ge(centred, 3)
                nc.tensor.transpose(banks[6][:, 0:E], router_c[:, :], k.ident[0:E, 0:E]).then_inc(moved_ready, 1)

            @block.vector
            def _(dve):
                nc.vector.memset(k.stack_sel[:, :, :, :, :], 0.0).then_inc(zeroed, 1)
                nc.vector.memset(k.pick_head[:, :, :], 0.0).then_inc(zeroed, 1)
                nc.vector.memset(k.x_sb[:, B:B + AHEAD, :], 0.0).then_inc(zeroed, 1)
                nc.vector.memset(k.x_sb[:, 0:B, P:ROW], 0.0).then_inc(zeroed, 1)
                nc.vector.memset(k.empty_row[:, 0:P], 0.0).then_inc(zeroed, 1)
                nc.vector.memset(k.empty_row[:, P:ROW], float(B * P)).then_inc(zeroed, 1)
                nc.vector.memset(k.ctx_sb[:, B:B + 3, :], 0.0).then_inc(zeroed, 1)
                dve.wait_ge(numbered, 1)
                dve.wait_ge(zeroed, 7)
                nc.vector.tensor_copy(k.x_sb[:, 0:B, P], numbers[:, :]).then_inc(zeroed, 1)
                dve.wait_ge(small_landed, 16 * 7)
                nc.vector.bn_stats(router_bn[:, 0:6], router[:, :]).then_inc(centred, 1)
                dve.wait_ge(centred, 1)
                nc.vector.bn_aggr(router_bn[:, 6:8], router_bn[:, 0:6]).then_inc(centred, 1)
                dve.wait_ge(centred, 2)
                nc.vector.tensor_scalar(router_c[:, :], router[:, :], router_bn[:, 6:7], None, ALU.subtract).then_inc(centred, 1)
                for n in range(3):
                    dve.wait_ge(moved_ready, n + 1)
                    nc.vector.tensor_copy(k.w0T_hi[:, n, :], banks[n][:, 0:P]).then_inc(split_hi, 1)
                for n in range(3):
                    dve.wait_ge(split_hi, n + 1)
                    nc.vector.tensor_tensor(k.w0T_lo[:, n, :], banks[n][:, 0:P], k.w0T_hi[:, n, :], ALU.subtract).then_inc(split_hi, 1)
                dve.wait_ge(moved_ready, 7)
                dve.wait_ge(tg_ready, 1)
                nc.vector.tensor_scalar(k.wo0[:, :], banks[3][:, 0:P], k.tg[:, 0:1], None, ALU.mult).then_inc(split_hi, 1)
                nc.vector.tensor_copy(k.attn_wT[:, :], banks[4][:, 0:P]).then_inc(split_hi, 1)
                nc.vector.tensor_copy(k.next_wT[:, :], banks[5][:, 0:P]).then_inc(split_hi, 1)
                nc.vector.tensor_copy(k.routerT[:, :], banks[6][:, 0:E]).then_inc(split_hi, 1)
                dve.wait_ge(split_hi, 10)
                dve.wait_ge(zeroed, 8)


def on_all(v):
    return v.rearrange("(a n) -> a n", a=1).broadcast_to([P, v.shape[0]])


def column(v):
    return v.rearrange("(p a) -> p a", a=1)


LOADS = 4
FIRST_LOADS = 16 * (2 + 5)
TOKEN_LOADS = 16 * 2 * (LOADS - 1)


def load_tokens(sp, A, k, n, landed):
    some = slice(n * (B // LOADS), (n + 1) * (B // LOADS))
    sp.dma_start(k.x_sb[:, some, 0:P], A["x"][some].rearrange("b t d -> t b d")).then_inc(landed, 16)
    sp.dma_start(k.ctx_sb[:, some, :], A["ctx_1024"][some].rearrange("b t d -> t b d")).then_inc(landed, 16)


def load_weights(nc, sp, A, k):
    late, ffn0 = 0, 0
    for n, name in enumerate(("L1_xattn_Wq", "L1_xattn_Wk", "L1_xattn_Wv")):
        sp.dma_start(k.big[:, n, :], A[name]).then_inc(k.late_landed, 16)
        late += 16
    sp.dma_start(k.big_out[:, :, :], A["L1_xattn_Wo"].rearrange("(j p) n -> p j n", p=P)).then_inc(k.late_landed, 16)
    for w, name in enumerate(("L1_ffn_gate_w", "L1_ffn_up_w")):
        for c, (c0, rows) in enumerate(CHUNKS):
            sp.dma_start(k.gu[0:rows, w, c, :, :], A[name][:, c0:c0 + rows, :].rearrange("e i h -> i e h")).then_inc(k.late_landed, 16)
            late += 16
    sp.dma_start(k.down, A["L1_ffn_down_w"].rearrange("e h i -> h e i")).then_inc(k.late_landed, 16)
    late += 32
    for n, name in enumerate(("L0_ffn_ln_scale", "L0_ffn_ln_bias", "L0_ffn_attn_b", "L0_ffn_next_b")):
        sp.dma_start(k.ffn_cols[:, n:n + 1], column(A[name])).then_inc(k.ffn0_landed, 16)
        ffn0 += 16
    sp.dma_start(k.w1[:, :, :], A["L0_ffn_w1"].rearrange("e d h -> d e h")).then_inc(k.ffn0_landed, 16)
    sp.dma_start(k.w2[:, :, :, :].rearrange("p e c n -> p (e c) n"),
                 A["L0_ffn_w2"].rearrange("e (c p) n -> p (e c) n", p=P)).then_inc(k.ffn0_landed, 16)
    with nc.allow_non_contiguous_dma(reason="small bias columns"):
        sp.dma_start(k.b1[:, :, :].rearrange("p e c -> p (e c)"),
                     A["L0_ffn_b1"].rearrange("e (c p) -> p (e c)", p=P)).then_inc(k.ffn0_landed, 16)
        sp.dma_start(k.b2[:, :], A["L0_ffn_b2"].rearrange("e p -> p e")).then_inc(k.ffn0_landed, 16)
    return late, ffn0 + 64


def prepare_second_layer(nc, k):
    with ExitStack() as ctx:
        def sem(name):
            return ctx.enter_context(nc.semaphore("w_" + name))

        bigT = ctx.enter_context(nc.sbuf_tensor("w_bigT", [P, 3, 8, P], F32))
        banks = [ctx.enter_context(nc.psum_tensor(f"w_bank{n}", [P, 512], F32)) for n in range(8)]
        moved, split_hi, dve_out, act_out = map(sem, "moved split_hi dve_out act_out".split())

        jobs = []
        for w in range(3):
            for q in range(2):
                jobs.append(("t", [(k.big[:, w, (4 * q + n) * P:(4 * q + n + 1) * P], P, P) for n in range(4)],
                             ("act" if q else "dve", bigT[:, w, 4 * q:4 * q + 4, :].rearrange("p a n -> p (a n)"))))
        BIG = len(jobs)
        for w, (hi, lo) in enumerate(((k.gate_hi, k.gate_lo), (k.up_hi, k.up_lo))):
            for e in range(E):
                jobs.append(("t", [(k.gu[0:rows, w, c, e, :], P, rows) for c, (_, rows) in enumerate(CHUNKS)],
                             (1.0, hi[:, e, :], lo[:, e, :])))
        for c, (c0, rows) in enumerate(CHUNKS):
            for q in range(2):
                jobs.append(("t", [(k.down[:, 4 * q + n, c0:c0 + rows], rows, P) for n in range(4)],
                             ("act" if c else "dve", k.downT[0:rows, c, 4 * q:4 * q + 4, :].rearrange("p a n -> p (a n)"))))
        for q in range(4):
            heads = range(8 * (q // 2) + q % 2, 8 * (q // 2) + 8, 2)
            half = lambda t, w, h: t[HD1 * (h % 2):HD1 * (h % 2) + HD1, w, h // 2, :]
            there = slice(heads[0], heads[0] + 7, 2)
            jobs.append(("m", [(half(bigT, 0, h), half(bigT, 1, h)) for h in heads],
                         (float(HD1) ** -0.5, k.A_hi[:, there, :], k.A_lo[:, there, :])))
            jobs.append(("m", [(half(bigT, 2, h), k.big_out[HD1 * (h % 2):HD1 * (h % 2) + HD1, h // 2, :]) for h in heads],
                         (k.tg[:, 1:2], k.M_hi[:, there, :], k.M_lo[:, there, :])))

        def outs(n, engine):
            return sum(1 for _, _, target in jobs[:n] if (target[0] == "act") == (engine == "act"))

        def source(n):
            kind, _, target = jobs[n]
            dst = target[1]
            width = dst.shape[1] * (P if kind == "m" else 1)
            src = banks[n % 8][0:dst.shape[0], 0:width]
            return src.rearrange("p (a n) -> p a n", n=P) if kind == "m" else src

        with nc.Block() as block:
            @block.tensor
            def _(pe):
                pe.wait_ge(k.late_landed, k.late_total)
                for n, (kind, parts, _) in enumerate(jobs):
                    first = max(n - 7, BIG if kind == "m" else 0)
                    if first > 0:
                        if jobs[first - 1][2][0] == "act" or kind == "m":
                            pe.wait_ge(act_out, outs(first, "act"))
                        if jobs[first - 1][2][0] != "act" or kind == "m":
                            pe.wait_ge(dve_out, outs(first, "dve"))
                    at = 0
                    for part in parts:
                        if kind == "t":
                            src, rows, width = part
                            last = nc.tensor.transpose(banks[n % 8][0:rows, at:at + width], src, k.ident[0:width, 0:width])
                            at += width
                        else:
                            last = nc.tensor.matmul(banks[n % 8][:, at:at + P], part[0], part[1], start=True, stop=True)
                            at += P
                    last.then_inc(moved, 1)

            @block.scalar
            def _(act):
                for n, (_, _, target) in enumerate(jobs):
                    if target[0] == "act":
                        act.wait_ge(moved, n + 1)
                        nc.scalar.activation(target[1], source(n), ACT.Copy).then_inc(act_out, 1)
                    elif target[0] != "dve":
                        act.wait_ge(moved, n + 1)
                        nc.scalar.activation(target[1], source(n), ACT.Identity, scale=target[0]).then_inc(split_hi, 1)

            @block.vector
            def _(dve):
                splits = 0
                for n, (_, _, target) in enumerate(jobs):
                    if target[0] == "dve":
                        dve.wait_ge(moved, n + 1)
                        nc.vector.tensor_copy(target[1], source(n)).then_inc(dve_out, 1)
                    elif target[0] != "act":
                        splits += 1
                        dve.wait_ge(split_hi, splits)
                        nc.vector.scalar_tensor_tensor(out=target[2], in0=source(n), scalar=target[0], in1=target[1],
                                                       op0=ALU.mult, op1=ALU.subtract).then_inc(dve_out, 1)


def alone(nc, dve, carrier, semaphore, value):
    dve.wait_ge(semaphore, value)
    nc.vector.tensor_copy(carrier[:, 1:2], carrier[:, 0:1])


def normalise(nc, pool, stats, x_b, out, work, s, count):
    nc.gpsimd.tensor_tensor(work[:, 0:1], stats[:, 1:2], work[:, 3:4], ALU.add).then_inc(s, 1)
    nc.gpsimd.tensor_tensor(out, x_b, stats[:, 0:1].broadcast_to([P, P]), ALU.subtract).then_inc(s, 1)
    pool.wait_ge(s, count + 2)
    nc.gpsimd.tensor_tensor(work[:, 1:2], work[:, 0:1], work[:, 2:3], ALU.pow).then_inc(s, 1)
    pool.wait_ge(s, count + 3)
    return nc.gpsimd.tensor_tensor(out, out, work[:, 1:2].broadcast_to([P, P]), ALU.mult)


def first_attention(nc, A, k):
    R = 4
    with ExitStack() as ctx:
        def sb(name, shape, dt=F32):
            return ctx.enter_context(nc.sbuf_tensor("l0_" + name, shape, dt))

        def sem(name):
            return ctx.enter_context(nc.semaphore("l0_" + name))

        carrier = sb("carrier", [P, 3])
        taker = sb("taker", [P, 2])
        bn = sb("bn", [P, 2, 6])
        stats = sb("stats", [P, 2, 2])
        work = sb("work", [P, 2, 4])
        xn = sb("xn", [P, 2, 2, P])
        bias_row = sb("bias_row", [P, P])
        T_hi = sb("T_hi", [P, P], F16)
        T_lo = sb("T_lo", [P, P], F16)
        qk_hi = sb("qk_hi", [P, 2, P], F16)
        qk_lo = sb("qk_lo", [P, 2, P], F16)
        stack = sb("stack", [P, 2, 2, 4, P], F16)
        V = sb("V", [P, 2, H, G])
        neg_max = sb("neg_max", [P, H])
        neg_maxT = sb("neg_maxT", [P, P], BF16)
        probs = k.downT[:, 0:2].rearrange("p c e n -> p (c e n)").rearrange("p (r n) -> p r n", r=R)
        sums = k.downT[:, 2].rearrange("p e n -> p (e n)")[:, 0:4 * P]
        inv = sb("inv", [P, H])
        heads_out = sb("heads_out", [P, P])
        headsT = sb("headsT", [P, P])
        score_bank = [ctx.enter_context(nc.psum_tensor(f"l0_score{n}", [P, 512], F32)) for n in range(R)]
        front_bank, stack_bank, misc_bank, sum_bank = (
            ctx.enter_context(nc.psum_tensor(f"l0_{name}", [P, 512], F32)) for name in ("front", "stack_bank", "misc", "sum_bank"))
        names = ("primed bn_done stats_ready norm_step xn_ready bias_added T_moved T_hi_ready T_lo_ready qk_done qk_hi_ready "
                 "qk_lo_ready v_done V_ready q_stacked k_stacked stack_q stack_k scored max_ready maxT_moved maxT_ready shifted "
                 "exp_done pv_done sums_ready sums_moved inv_ready heads_ready heads_moved headsT_ready projected x_done tokens_landed").split()
        (primed, bn_done, stats_ready, norm_step, xn_ready, bias_added, T_moved, T_hi_ready, T_lo_ready, qk_done, qk_hi_ready,
         qk_lo_ready, v_done, V_ready, q_stacked, k_stacked, stack_q, stack_k, scored, max_ready, maxT_moved, maxT_ready, shifted,
         exp_done, pv_done, sums_ready, sums_moved, inv_ready, heads_ready, heads_moved, headsT_ready, projected, x_done, tokens_landed) = map(sem, names)

        def row(t, n):
            return t[:, bass.ds(n, 1), 0:P].rearrange("p a n -> p (a n)")

        with nc.Block() as block:
            @block.sync
            def _(sp):
                for n in range(1, LOADS):
                    load_tokens(sp, A, k, n, tokens_landed)
                k.late_total, k.ffn0_total = load_weights(nc, sp, A, k)

            @block.vector
            def _(dve):
                nc.vector.memset(V[:, :, :, :], 1.0).then_inc(primed, 1)
                nc.vector.memset(neg_maxT[:, :], 0.0).then_inc(primed, 1)
                nc.vector.memset(taker[:, :], 0.0).then_inc(primed, 1)
                nc.vector.memset(work[:, :, 2:3], -0.5).then_inc(primed, 1)
                nc.vector.memset(carrier[:, 0:2], 0.0).then_inc(primed, 1)
                nc.vector.memset(work[:, :, 3:4], EPS).then_inc(primed, 1)
                dve.wait_ge(k.x_landed, FIRST_LOADS)
                nc.vector.tensor_scalar(bias_row[:, :], k.bo[:, 0, :], k.tg[:, 0:1], None, ALU.mult).then_inc(primed, 1)
                dve.wait_ge(primed, 7)

                def statistics(n, w):
                    nc.vector.bn_stats(bn[:, w, :], row(k.x_sb, n)).then_inc(bn_done, 1)
                    alone(nc, dve, carrier, bn_done, n + 1)
                    nc.vector.bn_aggr(stats[:, w, :], bn[:, w, :]).then_inc(stats_ready, 1)

                def transposed_lo(n):
                    dve.wait_ge(T_hi_ready, 2 * n + 2)
                    nc.vector.tensor_tensor(T_lo[:, :], front_bank[:, 0:P], T_hi[:, :], ALU.subtract).then_inc(T_lo_ready, 1)
                    nc.vector.tensor_tensor(row(k.cT_lo, n), front_bank[:, P:2 * P], row(k.cT_hi, n), ALU.subtract).then_inc(T_lo_ready, 1)

                def projected_lo(n):
                    dve.wait_ge(qk_hi_ready, 2 * n + 2)
                    for m in range(2):
                        nc.vector.scalar_tensor_tensor(out=qk_lo[:, m, :], in0=front_bank[:, (2 + m) * P:(3 + m) * P],
                                                       scalar=k.bias0[:, m:m + 1], in1=qk_hi[:, m, :],
                                                       op0=ALU.add, op1=ALU.subtract).then_inc(qk_lo_ready, 1)

                def values(n, w):
                    dve.wait_ge(v_done, n + 1)
                    nc.vector.tensor_tensor(V[:, w, :, 0:D0], misc_bank[:, 0:P].rearrange("p (h d) -> p h d", h=H),
                                            k.bv0[:, :].rearrange("p (h d) -> p h d", h=H), ALU.add).then_inc(V_ready, 1)

                def stacked_q(n, w):
                    dve.wait_ge(q_stacked, n + 1)
                    nc.vector.tensor_copy(stack[:, w, 0].rearrange("p j n -> p (j n)"), stack_bank[:, :]).then_inc(stack_q, 1)

                def maxima(n, r):
                    dve.wait_ge(scored, R * n + r + 1)
                    nc.vector.tensor_reduce(neg_max[:, 4 * r:4 * r + 4], score_bank[r][:, :].rearrange("p (j n) -> p j n", j=4),
                                            AX.X, ALU.max, negate=True).then_inc(max_ready, 1)

                def maxima_out(n):
                    dve.wait_ge(maxT_moved, n + 1)
                    nc.vector.tensor_copy(neg_maxT[0:H, :], misc_bank[0:H, P:2 * P]).then_inc(maxT_ready, 1)

                def divide(n):
                    O = sum_bank[:, :].rearrange("p (h g) -> p h g", g=G)
                    dve.wait_ge(sums_moved, n + 1)
                    nc.vector.reciprocal(inv[:, :], O[:, :, D0]).then_inc(inv_ready, 1)
                    dve.wait_ge(inv_ready, n + 1)
                    nc.vector.tensor_tensor(heads_out[:, :].rearrange("p (h d) -> p h d", h=H), O[:, :, 0:D0],
                                            inv[:, :].rearrange("p (h a) -> p h a", a=1).broadcast_to([P, H, D0]), ALU.mult)\
                        .then_inc(heads_ready, 1)

                def heads_transposed(n):
                    dve.wait_ge(heads_moved, n + 1)
                    nc.vector.tensor_copy(headsT[:, :], misc_bank[:, 2 * P:3 * P]).then_inc(headsT_ready, 1)

                def add_to_x(n):
                    dve.wait_ge(projected, n + 1)
                    dve.wait_ge(bias_added, n + 1)
                    nc.vector.tensor_tensor(row(k.x_sb, n), misc_bank[:, 3 * P:4 * P], row(k.x_sb, n), ALU.add).then_inc(x_done, 1)

                def step(n, w, first=False):
                    maxima_out(n)
                    stacked_q(n + 1, 1 - w)
                    transposed_lo(n + 2)
                    if not first:
                        divide(n - 1)
                    values(n + 1, 1 - w)
                    dve.wait_ge(xn_ready, 2 * n + 4)
                    statistics(n + 3, 1 - w)
                    if not first:
                        heads_transposed(n - 1)
                    for r in range(R):
                        maxima(n + 1, r)
                        if r == 0:
                            projected_lo(n + 2)
                        if r == 1 and not first:
                            add_to_x(n - 1)

                for n in range(3):
                    if n == 2:
                        dve.wait_ge(xn_ready, 2)
                    statistics(n, n % 2)
                transposed_lo(0)
                projected_lo(0)
                values(0, 0)
                transposed_lo(1)
                stacked_q(0, 0)
                projected_lo(1)
                for r in range(R):
                    maxima(0, r)
                step(0, 0, first=True)
                step(1, 1)
                dve.wait_ge(tokens_landed, TOKEN_LOADS)
                with dve.Fori(1, PAIRS) as i:
                    for w in range(2):
                        step(2 * i + w, w)
                divide(B - 1)
                heads_transposed(B - 1)
                add_to_x(B - 1)

            @block.gpsimd
            def _(pool):
                pool.wait_ge(primed, 7)
                pool.wait_ge(k.x_landed, FIRST_LOADS)

                def normal(n, w, free=True):
                    pool.wait_ge(stats_ready, n + 1)
                    if free:
                        pool.wait_ge(T_moved, n - 1)
                    normalise(nc, pool, stats[:, w, :], row(k.x_sb, n), xn[:, w, 0, :], work[:, w, :], norm_step, 3 * n).then_inc(xn_ready, 1)
                    nc.gpsimd.tensor_copy(xn[:, w, 1, :], row(k.ctx_sb, n)).then_inc(xn_ready, 1)
                    pool.wait_ge(xn_ready, 2 * n + 2)
                    nc.gpsimd.tensor_tensor(taker[:, 1:2], taker[:, 0:1], taker[:, 0:1], ALU.add)
                    nc.gpsimd.tensor_tensor(row(k.x_sb, n), row(k.x_sb, n), bias_row[:, :], ALU.add).then_inc(bias_added, 1)

                normal(0, 0, free=False)
                normal(1, 1, free=False)
                normal(2, 0)
                normal(3, 1)
                normal(4, 0)
                pool.wait_ge(tokens_landed, TOKEN_LOADS)
                with pool.Fori(1, PAIRS) as i:
                    for w in range(2):
                        normal(2 * i + w + 3, 1 - w)

            @block.scalar
            def _(act):
                act.wait_ge(primed, 7)
                nc.scalar.activation(carrier[:, 2:3], carrier[:, 0:1], ACT.Exp).then_inc(exp_done, R)

                def transposed_hi(n):
                    act.wait_ge(T_moved, n + 1)
                    nc.scalar.activation(T_hi[:, :], front_bank[:, 0:P], ACT.Copy).then_inc(T_hi_ready, 1)
                    nc.scalar.activation(row(k.cT_hi, n), front_bank[:, P:2 * P], ACT.Copy).then_inc(T_hi_ready, 1)

                def projected_hi(n):
                    act.wait_ge(qk_done, n + 1)
                    for m in range(2):
                        nc.scalar.activation(qk_hi[:, m, :], front_bank[:, (2 + m) * P:(3 + m) * P], ACT.Identity,
                                             bias=k.bias0[:, m:m + 1]).then_inc(qk_hi_ready, 1)

                def stacked_k(n, w):
                    act.wait_ge(k_stacked, n + 1)
                    nc.scalar.activation(stack[:, w, 1].rearrange("p j n -> p (j n)"), stack_bank[:, :], ACT.Copy).then_inc(stack_k, 1)

                def exponentials(n, r):
                    act.wait_ge(shifted, R * n + r + 1)
                    nc.scalar.activation(probs[:, r, :], score_bank[r][:, :], ACT.Exp, scale=float(D0) ** -0.5).then_inc(exp_done, 1)

                def sums_out(n):
                    act.wait_ge(pv_done, n + 1)
                    nc.scalar.activation(sums[:, :], sum_bank[:, :], ACT.Copy).then_inc(sums_ready, 1)

                def step(n, w, first=False):
                    if not first:
                        sums_out(n - 1)
                    transposed_hi(n + 2)
                    exponentials(n, 0)
                    stacked_k(n + 1, 1 - w)
                    exponentials(n, 1)
                    projected_hi(n + 2)
                    exponentials(n, 2)
                    exponentials(n, 3)

                transposed_hi(0)
                projected_hi(0)
                transposed_hi(1)
                stacked_k(0, 0)
                projected_hi(1)
                step(0, 0, first=True)
                step(1, 1)
                with act.Fori(1, PAIRS) as i:
                    for w in range(2):
                        step(2 * i + w, w)
                sums_out(B - 1)

            @block.tensor
            def _(pe):
                pe.wait_ge(primed, 7)

                def transpose(n, w, first=False):
                    pe.wait_ge(xn_ready, 2 * n + 2)
                    if not first:
                        pe.wait_ge(qk_lo_ready, 2 * n)
                    for m in range(2):
                        last = nc.tensor.transpose(front_bank[:, m * P:m * P + P], xn[:, w, m, :], k.ident[:, :])
                    last.then_inc(T_moved, 1)

                def project(n, first=False):
                    pe.wait_ge(T_lo_ready, 2 * n + 2)
                    for m, (hi, lo) in enumerate(((T_hi[:, :], T_lo[:, :]), (row(k.cT_hi, n), row(k.cT_lo, n)))):
                        last = both_products(nc, front_bank[:, (2 + m) * P:(3 + m) * P],
                                             [(v[:, m, :], t) for v, t in ((k.w0T_hi, hi), (k.w0T_lo, hi), (k.w0T_hi, lo))])
                    last.then_inc(qk_done, 1)

                def project_values(n, first=False):
                    if not first:
                        pe.wait_ge(maxT_ready, n)
                    last = both_products(nc, misc_bank[:, 0:P], [(row(t, n), v[:, 2, :]) for v, t in
                                                                 ((k.w0T_hi, k.cT_hi), (k.w0T_lo, k.cT_hi), (k.w0T_hi, k.cT_lo))])
                    last.then_inc(v_done, 1)

                def stack_up(n, m, done, first=False):
                    if m == 0:
                        pe.wait_ge(qk_lo_ready, 2 * n + 2)
                        if not first:
                            pe.wait_ge(stack_k, n)
                    else:
                        pe.wait_ge(stack_q, n + 1)
                    for j in range(4):
                        sel = [k.stack_sel[:, 2 * m + part, 4 * j:4 * j + 4].rearrange("p h c d -> p (h c d)") for part in range(2)]
                        last = both_products(nc, stack_bank[:, j * P:j * P + P], [(sel[0], qk_hi[:, m, :]), (sel[1], qk_lo[:, m, :])])
                    last.then_inc(done, 1)

                def score_by_query(n, w, r):
                    pe.wait_ge(stack_k, n + 1)
                    pe.wait_ge(exp_done, R * n + r + 1)
                    rows = slice(G * r, G * r + G)
                    for j in range(4):
                        last = nc.tensor.matmul(score_bank[r][:, j * P:j * P + P], stack[rows, w, 0, j, :], stack[rows, w, 1, j, :],
                                                start=True, stop=True, tile_position=(G * r, 0))
                    last.then_inc(scored, 1)

                def transpose_maxima(n, back=True):
                    pe.wait_ge(max_ready, R * n + R)
                    pe.wait_ge(V_ready, n + 1)
                    if back:
                        pe.wait_ge(x_done, n - 1)
                    nc.tensor.transpose(misc_bank[0:H, P:2 * P], neg_max[:, :], k.ident[:, :]).then_inc(maxT_moved, 1)

                def score_by_key(n, w, r):
                    if r == 0:
                        pe.wait_ge(maxT_ready, n + 1)
                    rows = slice(G * r, G * r + G)
                    for j in range(4):
                        nc.tensor.matmul(score_bank[r][:, j * P:j * P + P], k.pick_head[:, 4 * r + j, :], neg_maxT[:, :],
                                         start=j == 0, stop=False, skip_group_check=True)
                    for j in range(4):
                        last = nc.tensor.matmul(score_bank[r][:, j * P:j * P + P], stack[rows, w, 1, j, :], stack[rows, w, 0, j, :],
                                                start=False, stop=j == 3, tile_position=(G * r, 0), skip_group_check=True)
                    last.then_inc(shifted, 1)

                def weigh(n, w, r, first=False):
                    pe.wait_ge(exp_done, R * n + r + R + 1)
                    if r == 0:
                        pe.wait_ge(V_ready, n + 1)
                        if not first:
                            pe.wait_ge(heads_ready, n)
                    for j in range(4):
                        last = nc.tensor.matmul(sum_bank[G * r:G * r + G, j * P:j * P + P], V[:, w, 4 * j + r, :],
                                                probs[:, r, j * P:j * P + P], start=True, stop=True, tile_position=(0, G * r))
                    if r == R - 1:
                        last.then_inc(pv_done, 1)

                def transpose_sums(n):
                    pe.wait_ge(sums_ready, n + 1)
                    for j in range(4):
                        last = nc.tensor.transpose(sum_bank[:, j * P:j * P + P], sums[:, j * P:j * P + P], k.ident[:, :])
                    last.then_inc(sums_moved, 1)

                def transpose_heads(n, values=None):
                    pe.wait_ge(heads_ready, n + 1)
                    if values is not None:
                        pe.wait_ge(V_ready, values + 1)
                    nc.tensor.transpose(misc_bank[:, 2 * P:3 * P], heads_out[:, :], k.ident[:, :]).then_inc(heads_moved, 1)

                def project_heads(n):
                    pe.wait_ge(headsT_ready, n + 1)
                    nc.tensor.matmul(misc_bank[:, 3 * P:4 * P], headsT[:, :], k.wo0[:, :], start=True, stop=True).then_inc(projected, 1)

                def step(n, w, first=False, back=True):
                    transpose(n + 2, w)
                    stack_up(n + 1, 0, q_stacked)
                    transpose_maxima(n, back)
                    if not first:
                        transpose_sums(n - 1)
                    score_by_key(n, w, 0)
                    project_values(n + 1)
                    stack_up(n + 1, 1, k_stacked)
                    score_by_key(n, w, 1)
                    project(n + 2)
                    score_by_key(n, w, 2)
                    if not first:
                        transpose_heads(n - 1, n + 1)
                    score_by_query(n + 1, 1 - w, 0)
                    score_by_key(n, w, 3)
                    if not first:
                        project_heads(n - 1)
                    score_by_query(n + 1, 1 - w, 1)
                    score_by_query(n + 1, 1 - w, 2)
                    weigh(n, w, 0, first)
                    score_by_query(n + 1, 1 - w, 3)
                    for r in range(1, R):
                        weigh(n, w, r)

                transpose(0, 0, first=True)
                project(0)
                project_values(0, first=True)
                transpose(1, 1)
                stack_up(0, 0, q_stacked, first=True)
                stack_up(0, 1, k_stacked)
                project(1)
                for r in range(R):
                    score_by_query(0, 0, r)
                step(0, 0, first=True, back=False)
                step(1, 1, back=False)
                with pe.Fori(1, PAIRS) as i:
                    for w in range(2):
                        step(2 * i + w, w)
                transpose_sums(B - 1)
                transpose_heads(B - 1)
                project_heads(B - 1)


def first_ffn(nc, k):
    with ExitStack() as ctx:
        def sb(name, shape, dt=F32):
            return ctx.enter_context(nc.sbuf_tensor("f0_" + name, shape, dt))

        def sem(name):
            return ctx.enter_context(nc.semaphore("f0_" + name))

        carrier = sb("carrier", [P, 3])
        half = sb("half", [P, 2])
        bn = sb("bn", [P, 2, 2, 6])
        stats = sb("stats", [P, 2, 2, 2])
        var = sb("var", [P, 2, 2])
        rstd = sb("rstd", [P, 2, 2])
        xn = sb("xn", [P, 2, 2, 2, P])
        znT = sb("znT", [P, 2, 2, 2 * P])
        xaT = sb("xaT", [P, 2 * P])
        hid = sb("hid", [P, H0, 2 * P])
        eoT = sb("eoT", [P, 2 * P])
        outT = sb("outT", [P, 2 * P])
        t_bank, attn_bank, *hid_bank, eo_bank, next_bank = (
            ctx.enter_context(nc.psum_tensor(f"f0_bank{n}", [P, 512], F32)) for n in range(8))
        names = ("primed bn_done stats_ready var_ready rstd_ready once_ready twice_ready T_moved T_ready attn_done xa_ready "
                 "hid_done hid_ready eo_done eo_ready next_done outT_ready back_done x_done").split()
        (primed, bn_done, stats_ready, var_ready, rstd_ready, once_ready, twice_ready, T_moved, T_ready, attn_done, xa_ready,
         hid_done, hid_ready, eo_done, eo_ready, next_done, outT_ready, back_done, x_done) = map(sem, names)

        def row(n):
            return k.x_sb[:, bass.ds(n, 1), 0:P].rearrange("p a n -> p (a n)")

        with nc.Block() as block:
            @block.vector
            def _(dve):
                nc.vector.memset(half[:, :], -0.5).then_inc(primed, 1)
                nc.vector.memset(carrier[:, 0:2], 0.0).then_inc(primed, 1)
                nc.vector.memset(var[:, :, :], 1.0).then_inc(x_done, 2)
                dve.wait_ge(k.ffn0_landed, k.ffn0_total)
                dve.wait_ge(primed, 2)
                dve.wait_ge(x_done, 2)

                def statistics(g, w, s):
                    if s == 1:
                        dve.wait_ge(once_ready, 2 * g + 2)
                    for u in range(2):
                        nc.vector.bn_stats(bn[:, s, u, :], xn[:, w, 0, u, :] if s else row(2 * g + u)).then_inc(bn_done, 1)
                    alone(nc, dve, carrier, bn_done, 4 * g + 2 * s + 2)
                    for u in range(2):
                        nc.vector.bn_aggr(stats[:, s, u, :], bn[:, s, u, :]).then_inc(stats_ready, 1)
                    dve.wait_ge(stats_ready, 4 * g + 2 * s + 2)
                    nc.vector.tensor_scalar(var[:, s, :], stats[:, s, :, 1], EPS, None, ALU.add).then_inc(var_ready, 1)

                def normalised(g, w, s):
                    dve.wait_ge(rstd_ready, 2 * g + s + 1)
                    for u in range(2):
                        nc.vector.tensor_scalar(xn[:, w, s, u, :], xn[:, w, 0, u, :] if s else row(2 * g + u), stats[:, s, u, 0:1],
                                                rstd[:, s, u:u + 1], ALU.subtract, ALU.mult).then_inc(twice_ready if s else once_ready, 1)

                def transposed(g, w):
                    dve.wait_ge(T_moved, g + 1)
                    nc.vector.tensor_copy(znT[:, w, 0, :], t_bank[:, 0:2 * P]).then_inc(T_ready, 1)
                    nc.vector.tensor_scalar(znT[:, w, 1, :], t_bank[:, 2 * P:4 * P], k.ffn_cols[:, 0:1], k.ffn_cols[:, 1:2],
                                            ALU.mult, ALU.add).then_inc(T_ready, 1)

                def attended(g, w):
                    dve.wait_ge(T_ready, 2 * g + 1)
                    dve.wait_ge(attn_done, g + 1)
                    nc.vector.scalar_tensor_tensor(out=xaT[:, :], in0=attn_bank[:, 0:2 * P], scalar=k.ffn_cols[:, 2:3],
                                                   in1=znT[:, w, 0, :], op0=ALU.add, op1=ALU.add).then_inc(xa_ready, 1)

                def add_to_x(g):
                    dve.wait_ge(back_done, g + 1)
                    for u in range(2):
                        nc.vector.scalar_tensor_tensor(out=row(2 * g + u), in0=attn_bank[:, (2 + u) * P:(3 + u) * P], scalar=k.tg[:, 2:3],
                                                       in1=row(2 * g + u), op0=ALU.mult, op1=ALU.add).then_inc(x_done, 1)

                for g in range(2):
                    for s in range(2):
                        statistics(g, g, s)
                        normalised(g, g, s)
                    if g == 0:
                        transposed(0, 0)
                        attended(0, 0)
                transposed(1, 1)
                for s in range(2):
                    statistics(2, 0, s)
                    normalised(2, 0, s)
                statistics(3, 1, 0)
                with dve.Fori(0, 2) as m:
                    for e in range(E):
                        g, w = m * E + e, 1 - e % 2
                        normalised(g + 3, w, 0)
                        statistics(g + 3, w, 1)
                        attended(g + 1, w)
                        transposed(g + 2, 1 - w)
                        normalised(g + 3, w, 1)
                        statistics(g + 4, 1 - w, 0)
                        add_to_x(g)

            @block.gpsimd
            def _(pool):
                pool.wait_ge(primed, 2)

                def deviations(g, s):
                    pool.wait_ge(var_ready, 2 * g + s + 1)
                    nc.gpsimd.tensor_tensor(rstd[:, s, :], var[:, s, :], half[:, :], ALU.pow).then_inc(rstd_ready, 1)

                for g in range(3):
                    for s in range(2):
                        deviations(g, s)
                deviations(3, 0)
                with pool.Fori(0, 2) as m:
                    for e in range(E):
                        g = m * E + e
                        deviations(g + 3, 1)
                        deviations(g + 4, 0)

            @block.scalar
            def _(act):
                act.wait_ge(primed, 2)
                nc.scalar.activation(carrier[:, 2:3], carrier[:, 0:1], ACT.Gelu)
                act.wait_ge(k.ffn0_landed, k.ffn0_total)

                def hidden(g, e):
                    for c in range(H0):
                        act.wait_ge(hid_done, H0 * g + c + 1)
                        nc.scalar.activation(hid[:, c, :], hid_bank[c][:, 0:2 * P], ACT.Gelu, bias=k.b1[:, e, c:c + 1])\
                            .then_inc(hid_ready, 1)

                hidden(0, 0)
                with act.Fori(0, 2) as m:
                    for e in range(E):
                        g = m * E + e
                        act.wait_ge(eo_done, g + 1)
                        nc.scalar.activation(eoT[:, :], eo_bank[:, 0:2 * P], ACT.Identity, bias=k.b2[:, e:e + 1]).then_inc(eo_ready, 1)
                        act.wait_ge(next_done, g + 1)
                        nc.scalar.activation(outT[:, :], next_bank[:, 0:2 * P], ACT.Gelu, bias=k.ffn_cols[:, 3:4]).then_inc(outT_ready, 1)
                        hidden(g + 1, (e + 1) % E)

            @block.tensor
            def _(pe):
                pe.wait_ge(k.ffn0_landed, k.ffn0_total)

                def transpose(g, w):
                    pe.wait_ge(twice_ready, 2 * g + 2)
                    for s in range(2):
                        for u in range(2):
                            last = nc.tensor.transpose(t_bank[:, (2 * s + u) * P:(2 * s + u + 1) * P], xn[:, w, s, u, :], k.ident[:, :])
                    last.then_inc(T_moved, 1)

                def attend(g, w, back=True):
                    pe.wait_ge(T_ready, 2 * g + 2)
                    if back:
                        pe.wait_ge(x_done, 2 * g)
                    nc.tensor.matmul(attn_bank[:, 0:2 * P], k.attn_wT[:, :], znT[:, w, 1, :], start=True, stop=True).then_inc(attn_done, 1)

                def first_product(g, e):
                    pe.wait_ge(xa_ready, g + 1)
                    for c in range(H0):
                        nc.tensor.matmul(hid_bank[c][:, 0:2 * P], k.w1[:, e, c * P:c * P + P], xaT[:, :],
                                         start=True, stop=True).then_inc(hid_done, 1)

                transpose(0, 0)
                attend(0, 0, back=False)
                transpose(1, 1)
                first_product(0, 0)
                with pe.Fori(0, 2) as m:
                    for e in range(E):
                        g = m * E + e
                        for c in range(H0):
                            pe.wait_ge(hid_ready, H0 * g + c + 1)
                            last = nc.tensor.matmul(eo_bank[:, 0:2 * P], k.w2[:, e, c, :], hid[:, c, :], start=c == 0, stop=c == H0 - 1)
                        last.then_inc(eo_done, 1)
                        attend(g + 1, 1 - e % 2)
                        transpose(g + 2, e % 2)
                        pe.wait_ge(eo_ready, g + 1)
                        nc.tensor.matmul(next_bank[:, 0:2 * P], k.next_wT[:, :], eoT[:, :], start=True, stop=True).then_inc(next_done, 1)
                        first_product(g + 1, (e + 1) % E)
                        pe.wait_ge(outT_ready, g + 1)
                        for u in range(2):
                            last = nc.tensor.transpose(attn_bank[:, (2 + u) * P:(3 + u) * P], outT[:, u * P:u * P + P], k.ident[:, :])
                        last.then_inc(back_done, 1)


def second_attention(nc, k):
    Q = 4
    with ExitStack() as ctx:
        def sb(name, shape, dt=F32):
            return ctx.enter_context(nc.sbuf_tensor("l1_" + name, shape, dt))

        def sem(name):
            return ctx.enter_context(nc.semaphore("l1_" + name))

        carrier = sb("carrier", [P, 3])
        taker = sb("taker", [P, 8])
        bn = sb("bn", [P, 2, 6])
        stats = sb("stats", [P, 2, 2])
        work = sb("work", [P, 2, 4])
        xn = sb("xn", [P, 2, P])
        bias_row = sb("bias_row", [P, P])
        T_hi = sb("T_hi", [P, P], F16)
        T_lo = sb("T_lo", [P, P], F16)
        Y_hi = sb("Y_hi", [P, 2, H, P], F16)
        Y_lo = sb("Y_lo", [P, 2, H, P], F16)
        Z = sb("Z", [P, 2, H, P + 1])
        neg_max = sb("neg_max", [P, H])
        neg_maxT = sb("neg_maxT", [P, P], BF16)
        probs = sb("probs", [P, H, P])
        inv = sb("inv", [P, H])
        acc = sb("acc", [P, 2, ROW])
        rows = sb("rows", [P, 2, ROW])
        rowsT = sb("rowsT", [P, 2, P])
        logits = sb("logits", [P, 2, E])
        best = sb("best", [P, 2])
        equal = sb("equal", [P, 2, E])
        less8 = sb("less8", [P, E])
        first = sb("first", [P, 2])
        onehot = sb("onehot", [P, 2, E], BF16)
        before = sb("before", [P, P], BF16)
        ones = sb("ones", [P, P], BF16)
        ranks = sb("ranks", [P, 3, E])
        place = sb("place", [P, 2, E])
        slot = sb("slot", [P, 2])
        slot_i = sb("slot_i", [P, 2], mybir.dt.uint32)
        region = sb("region", [P, E])
        ends = sb("ends", [P, E])
        tiles_i = sb("tiles_i", [1, E], I32)
        tiles = sb("tiles", [1, E])
        upto = sb("upto", [1, 2, 4 + E])
        skip = sb("skip", [1, E])
        tile_no_i = sb("tile_no_i", [1, LISTED, E], I32)
        tile_no = sb("tile_no", [1, LISTED, E])
        passed = sb("passed", [1, LISTED, E])
        skipped = sb("skipped", [1, LISTED, E])
        owner = sb("owner", [1, LISTED])
        offset = sb("offset", [1, LISTED])
        digit = sb("digit", [1, TILES_STEP])
        digits = sb("digits", [1, LISTED // TILES_STEP, TILES_STEP])
        code = sb("code", [1, LISTED // TILES_STEP])
        ends_i = sb("ends_i", [1, E], I32)
        tz_bank, y_bank = (ctx.enter_context(nc.psum_tensor(f"l1_{name}", [P, 512], F32)) for name in ("tz", "y"))
        a_bank, b_bank, pv_bank = (
            [ctx.enter_context(nc.psum_tensor(f"l1_{name}{n}", [P, 512], F32)) for n in range(2)]
            for name in ("a", "b", "pv"))
        names = ("primed bn_done stats_ready norm_step xn_ready bias_added T_moved T_hi_ready T_lo_ready y_done Y_hi_ready "
                 "Y_lo_ready z_done Z_ready scored max_ready maxT_moved maxT_ready shifted exp_done pv_done inv_ready "
                 "summed x_done consts ones_ready rowsT_moved rowsT_ready routed chosen chose ranked placing slots_ready scattered "
                 "tiling ends_ready filled").split()
        (primed, bn_done, stats_ready, norm_step, xn_ready, bias_added, T_moved, T_hi_ready, T_lo_ready, y_done, Y_hi_ready,
         Y_lo_ready, z_done, Z_ready, scored, max_ready, maxT_moved, maxT_ready, shifted, exp_done, pv_done, inv_ready,
         summed, x_done, consts, ones_ready, rowsT_moved, rowsT_ready, routed, chosen, chose, ranked, placing, slots_ready, scattered,
         tiling, ends_ready, filled) = map(sem, names)
        SIDE = 2 * (P + 1)
        def a_ring(w, unit):
            return a_bank[(w * (Q + 1) + unit) % 2]

        def row(t, n):
            return t[:, bass.ds(n, 1), 0:P].rearrange("p a n -> p (a n)")

        with nc.Block() as block:
            @block.vector
            def _(dve):
                nc.vector.memset(Z[:, :, :, P:P + 1], 1.0).then_inc(primed, 1)
                nc.vector.memset(neg_maxT[:, :], 0.0).then_inc(primed, 1)
                nc.vector.memset(work[:, :, 2:3], -0.5).then_inc(primed, 1)
                nc.vector.memset(carrier[:, 0:2], 0.0).then_inc(primed, 1)
                nc.vector.memset(work[:, :, 3:4], EPS).then_inc(primed, 1)
                nc.vector.tensor_scalar(bias_row[:, :], k.bo[:, 1, :], k.tg[:, 1:2], None, ALU.mult).then_inc(primed, 1)
                nc.vector.memset(taker[:, :], 0.0).then_inc(summed, 4)
                nc.vector.memset(acc[:, :, :], 0.0).then_inc(x_done, 2)
                dve.wait_ge(primed, 6)
                dve.wait_ge(summed, 4)
                dve.wait_ge(x_done, 2)
                nc.vector.memset(ones[:, :], 1.0).then_inc(consts, 1)
                nc.vector.memset(upto[:, :, 0:4], 0.0).then_inc(consts, 1)
                for e in range(E):
                    nc.vector.memset(less8[:, e:e + 1], float(e - E)).then_inc(consts, 1)
                    nc.vector.memset(region[:, e:e + 1], float(e * REGION)).then_inc(consts, 1)
                    nc.vector.memset(ends[:, e:e + 1], float(e * REGION)).then_inc(consts, 1)
                for n in range(TILES_STEP):
                    nc.vector.memset(digit[:, n:n + 1], float(E ** n)).then_inc(consts, 1)
                dve.wait_ge(consts, CONSTS)

                def statistics(n, w):
                    nc.vector.bn_stats(bn[:, w, :], row(k.x_sb, n)).then_inc(bn_done, 1)
                    alone(nc, dve, carrier, bn_done, n + 1)
                    nc.vector.bn_aggr(stats[:, w, :], bn[:, w, :]).then_inc(stats_ready, 1)

                def transposed_lo(n):
                    dve.wait_ge(T_hi_ready, n + 1)
                    nc.vector.tensor_tensor(T_lo[:, :], tz_bank[:, 0:P], T_hi[:, :], ALU.subtract).then_inc(T_lo_ready, 1)

                def y_lo(n, w, q):
                    dve.wait_ge(Y_hi_ready, Q * n + q + 1)
                    nc.vector.tensor_tensor(Y_lo[:, w, Q * q:Q * q + Q].rearrange("p h n -> p (h n)"), y_bank[:, :],
                                            Y_hi[:, w, Q * q:Q * q + Q].rearrange("p h n -> p (h n)"), ALU.subtract)\
                        .then_inc(Y_lo_ready, 1)

                def maxima(n, w, q):
                    dve.wait_ge(scored, Q * n + q + 1)
                    nc.vector.tensor_reduce(neg_max[:, Q * q:Q * q + Q], a_ring(w, q)[:, :].rearrange("p (h n) -> p h n", h=Q),
                                            AX.X, ALU.max, negate=True).then_inc(max_ready, 1)

                def maxima_out(n, w):
                    dve.wait_ge(maxT_moved, n + 1)
                    nc.vector.tensor_copy(neg_maxT[0:H, :], a_ring(w, Q)[0:H, 0:P]).then_inc(maxT_ready, 1)

                def sums(n, w, m):
                    O = pv_bank[m % 2][:, 0:2 * (P + 1)].rearrange("p (h n) -> p h n", h=2)
                    dve.wait_ge(pv_done, 8 * n + m + 1)
                    nc.vector.reciprocal(inv[:, 2 * m:2 * m + 2], O[:, :, P]).then_inc(inv_ready, 1)
                    if m == 0:
                        dve.wait_ge(bias_added, n + 1)
                    dve.wait_ge(inv_ready, 8 * n + m + 1)
                    for h, total in enumerate((row(k.x_sb, n), acc[:, w, 0:P])):
                        j = 2 * m + h
                        if m == 0 and h == 1:
                            dve.wait_ge(x_done, n + 1)
                            nc.vector.tensor_scalar(total, O[:, h, 0:P], inv[:, j:j + 1], None, ALU.mult).then_inc(summed, 1)
                            continue
                        if m:
                            dve.wait_ge(summed, 16 * n + j + 3)
                        nc.vector.scalar_tensor_tensor(out=total, in0=O[:, h, 0:P], scalar=inv[:, j:j + 1], in1=total,
                                                       op0=ALU.mult, op1=ALU.add).then_inc(summed, 1)

                def rows_transposed(j, v, sums=None):
                    dve.wait_ge(rowsT_moved, 2 * j + v + 1)
                    if sums is not None:
                        dve.wait_ge(pv_done, sums)
                    nc.vector.tensor_copy(rowsT[:, v, :], pv_bank[v][:, SIDE:SIDE + P]).then_inc(rowsT_ready, 1)

                def logits_out(j, sums=None):
                    dve.wait_ge(routed, j + 1)
                    if sums is not None:
                        dve.wait_ge(pv_done, sums)
                    nc.vector.tensor_copy(logits[:, :, :].rearrange("p v e -> p (v e)"), pv_bank[0][:, SIDE:SIDE + 2 * E]).then_inc(chosen, 1)

                def each(t):
                    return t.rearrange("p (v a) -> p v a", a=1).broadcast_to([P, 2, E])

                def both(t):
                    return t.rearrange("p (a e) -> p a e", a=1).broadcast_to([P, 2, E])

                def choose(j, part):
                    dve.wait_ge(chosen, 4 * j + part + 1)
                    if part == 0:
                        nc.vector.tensor_reduce(best[:, :], logits[:, :, :], AX.X, ALU.max).then_inc(chosen, 1)
                    elif part == 1:
                        nc.vector.tensor_tensor(equal[:, :, :], logits[:, :, :], each(best[:, :]), ALU.is_equal).then_inc(chosen, 1)
                    elif part == 2:
                        nc.vector.tensor_tensor(equal[:, :, :], equal[:, :, :], both(less8[:, :]), ALU.mult).then_inc(chosen, 1)

                def chosen_out(j, part):
                    if part == 0:
                        dve.wait_ge(chosen, 4 * j + 4)
                        nc.vector.tensor_reduce(first[:, :], equal[:, :, :], AX.X, ALU.min).then_inc(chose, 1)
                    else:
                        dve.wait_ge(chose, 2 * j + 1)
                        nc.vector.tensor_tensor(onehot[:, :, :], both(less8[:, :]), each(first[:, :]), ALU.is_equal).then_inc(chose, 1)

                def ranks_out(j, sums=None):
                    dve.wait_ge(ranked, j + 1)
                    if sums is not None:
                        dve.wait_ge(pv_done, sums)
                    nc.vector.tensor_copy(ranks[:, :, :].rearrange("p v e -> p (v e)"), pv_bank[0][:, SIDE:SIDE + 3 * E]).then_inc(placing, 1)

                def put(j, part):
                    dve.wait_ge(placing, 5 * j + part + 1)
                    if part == 0:
                        nc.vector.tensor_tensor(place[:, :, :], ranks[:, 0:2, :], both(ends[:, :]), ALU.add).then_inc(placing, 1)
                    elif part == 1:
                        nc.vector.tensor_tensor(place[:, :, :], place[:, :, :], onehot[:, :, :], ALU.mult).then_inc(placing, 1)
                    elif part == 2:
                        nc.vector.tensor_reduce(slot[:, :], place[:, :, :], AX.X, ALU.add).then_inc(placing, 1)
                    elif part == 3:
                        nc.vector.tensor_copy(slot_i[:, :], slot[:, :]).then_inc(slots_ready, 1)
                        nc.vector.tensor_tensor(ends[:, :], ends[:, :], ranks[:, 2, :], ALU.add).then_inc(placing, 1)

                statistics(0, 0)
                statistics(1, 1)
                transposed_lo(0)
                for q in range(Q):
                    y_lo(0, 0, q)
                    maxima(0, 0, q)
                maxima_out(0, 0)
                transposed_lo(1)
                def step(n, u, route=None):
                    f, w, j = n + 1, 1 - u, route
                    for q in range(Q):
                        y_lo(f, w, q)
                        if q:
                            for h in range(2):
                                if j is not None and u == 0:
                                    if q == 1:
                                        rows_transposed(j, h, 8 * n + h + 1)
                                    elif (q, h) == (2, 0):
                                        logits_out(j, 8 * n + 3)
                                    elif q == 2:
                                        choose(j, 0)
                                    else:
                                        choose(j, 1 + h)
                                elif j is not None:
                                    if (q, h) == (1, 0):
                                        ranks_out(j, 8 * n + 1)
                                    elif q == 1:
                                        put(j, 0)
                                    elif q == 2:
                                        put(j, 1 + h)
                                    elif h == 0:
                                        put(j, 3)
                                sums(n, u, 2 * q - 2 + h)
                        else:
                            dve.wait_ge(xn_ready, n + 1)
                            statistics(n + 2, u)
                        maxima(f, w, q)
                    transposed_lo(f + 1)
                    maxima_out(f, w)
                    if j is not None and u == 0:
                        chosen_out(j, 0)
                    sums(n, u, 2 * Q - 2)
                    if j is not None and u == 0:
                        chosen_out(j, 1)
                    sums(n, u, 2 * Q - 1)

                step(0, 0)
                step(1, 1)
                with dve.Fori(1, PAIRS) as i:
                    for u in range(2):
                        step(2 * i + u, u, i - 1)
                j = PAIRS - 1
                for v in range(2):
                    rows_transposed(j, v)
                logits_out(j)
                for part in range(3):
                    choose(j, part)
                for part in range(2):
                    chosen_out(j, part)
                ranks_out(j)
                for part in range(4):
                    put(j, part)

                done = [0]

                def then(ins):
                    done[0] += 1
                    ins.then_inc(tiling, 1)
                    dve.wait_ge(tiling, done[0])

                dve.wait_ge(placing, 5 * PAIRS)
                nc.vector.tensor_copy(ends_i[:, :], ends[0:1, :]).then_inc(ends_ready, 1)
                then(nc.vector.scalar_tensor_tensor(out=tiles_i[:, :], in0=ends[0:1, :], scalar=float(P - 1), in1=region[0:1, :],
                                                    op0=ALU.add, op1=ALU.subtract))
                then(nc.vector.tensor_scalar(tiles_i[:, :], tiles_i[:, :], 7, None, ALU.arith_shift_right))
                then(nc.vector.tensor_copy(tiles[:, :], tiles_i[:, :]))
                nc.vector.tensor_copy(tile_no[:, :, :], tile_no_i[:, :, :]).then_inc(ends_ready, 1)
                nc.vector.tensor_scalar(skip[:, :], tiles[:, :], float(-P), float(REGION), ALU.mult, ALU.add).then_inc(ends_ready, 1)
                then(nc.vector.tensor_copy(upto[:, 0, 4:4 + E], tiles[:, :]))
                for n in range(3):
                    old, new, d = upto[:, n % 2], upto[:, 1 - n % 2], 2 ** n
                    then(nc.vector.tensor_tensor(new[:, 4:4 + E], old[:, 4:4 + E], old[:, 4 - d:4 - d + E], ALU.add))
                over_tiles = lambda t: t.rearrange("p (a e) -> p a e", a=1).broadcast_to([1, LISTED, E])
                dve.wait_ge(ends_ready, 3)
                then(nc.vector.tensor_tensor(passed[:, :, :], over_tiles(upto[:, 1, 4:4 + E]), tile_no[:, :, :], ALU.is_le))
                nc.vector.tensor_tensor(skipped[:, :, :], passed[:, :, :], over_tiles(skip[:, :]), ALU.mult).then_inc(ends_ready, 1)
                then(nc.vector.tensor_reduce(owner[:, :], passed[:, :, :], AX.X, ALU.add))
                dve.wait_ge(ends_ready, 4)
                nc.vector.tensor_reduce(offset[:, :], skipped[:, :, :], AX.X, ALU.add).then_inc(ends_ready, 1)
                then(nc.vector.scalar_tensor_tensor(out=digits[:, :, :], in0=owner[:, :].rearrange("p (s n) -> p s n", n=TILES_STEP), scalar=float(E - 1),
                                                    in1=digit[:, :].rearrange("p (a n) -> p a n", a=1).broadcast_to([1, LISTED // TILES_STEP, TILES_STEP]),
                                                    op0=ALU.min, op1=ALU.mult))
                dve.wait_ge(ends_ready, 5)
                nc.vector.scalar_tensor_tensor(out=k.tile_row[:, :], in0=tile_no[:, :, 0], scalar=float(P), in1=offset[:, :],
                                               op0=ALU.mult, op1=ALU.add).then_inc(ends_ready, 1)
                then(nc.vector.tensor_reduce(code[:, :], digits[:, :, :], AX.X, ALU.add))
                then(nc.vector.scalar_tensor_tensor(out=k.tile_expert[:, :], in0=code[:, 1:TILES // TILES_STEP + 1], scalar=float(E ** TILES_STEP),
                                                    in1=code[:, 0:TILES // TILES_STEP], op0=ALU.mult, op1=ALU.add))
                dve.wait_ge(ends_ready, 6)

            @block.sync
            def _(sp):
                sp.wait_ge(ends_ready, 1)
                _, rows_from = nc.values_load_multi_w_load_instructions(ends_i[:, :], [mybir.EngineType.SP], min_val=0,
                                                                        max_val=(E - 1) * REGION + B * P)
                for start in rows_from:
                    sp.dma_start(k.expert_rows[bass.ds(start, P), :], k.empty_row[:, :]).then_inc(filled, 16)
                sp.wait_ge(filled, 16 * E)

            @block.gpsimd
            def _(pool):
                pool.wait_ge(primed, 6)
                pool.wait_ge(summed, 4)

                def normal(n, w):
                    pool.wait_ge(stats_ready, n + 1)
                    normalise(nc, pool, stats[:, w, :], row(k.x_sb, n), xn[:, w, :], work[:, w, :], norm_step, 3 * n).then_inc(xn_ready, 1)

                nc.gpsimd.memset(before[:, :], 1.0).then_inc(ones_ready, 1)
                nc.gpsimd.iota(tile_no_i[:, :, :], pattern=[[1, LISTED], [0, E]], base=0, channel_multiplier=0).then_inc(consts, 1)
                pool.wait_ge(ones_ready, 1)
                nc.gpsimd.affine_select(out=before[:, :], in_=before[:, :], compare_op=ALU.is_gt, fill=0.0, base=0,
                                        pattern=[[1, P]], channel_multiplier=-1).then_inc(ones_ready, 1)

                def take(column, semaphore, value):
                    pool.wait_ge(semaphore, value)
                    nc.gpsimd.tensor_tensor(taker[:, column:column + 1], taker[:, 0:1], taker[:, 0:1], ALU.add)

                def bias(n, column):
                    take(column, xn_ready, n + 1)
                    nc.gpsimd.tensor_tensor(row(k.x_sb, n), row(k.x_sb, n), bias_row[:, :], ALU.add).then_inc(bias_added, 1)

                def scatter(j):
                    take(1, slots_ready, j + 1)
                    for v in range(2):
                        nc.gpsimd.indirect_dma_start(k.expert_rows[:, :], bass.IndirectOffsetOnAxis(slot_i[:, v:v + 1], 0),
                                                     rows[:, v, :], None).then_inc(scattered, 16)

                def rows_out(n, u, j=None):
                    if j is not None:
                        take(2, scattered, 32 * j + 32)
                    take(6 + u, summed, 16 * n + 20)
                    nc.gpsimd.tensor_tensor(rows[:, u, :].rearrange("p (a n) -> p a n", a=1), k.x_sb[:, bass.ds(n, 1), :],
                                            acc[:, u, :].rearrange("p (a n) -> p a n", a=1), ALU.add).then_inc(x_done, 1)

                def pair(i, j=None):
                    bias(2 * i, 4)
                    pool.wait_ge(T_moved, 2 * i + 1)
                    normal(2 * i + 2, 0)
                    bias(2 * i + 1, 5)
                    pool.wait_ge(T_moved, 2 * i + 2)
                    normal(2 * i + 3, 1)
                    if j is not None:
                        scatter(j)
                    rows_out(2 * i, 0, j)
                    rows_out(2 * i + 1, 1)

                normal(0, 0)
                normal(1, 1)
                pair(0)
                pool.wait_ge(k.rows_cleared, 16)
                with pool.Fori(1, PAIRS) as i:
                    pair(i, i - 1)
                scatter(PAIRS - 1)
                pool.wait_ge(scattered, 16 * B)

            @block.scalar
            def _(act):
                act.wait_ge(primed, 6)
                nc.scalar.activation(carrier[:, 2:3], carrier[:, 0:1], ACT.Exp).then_inc(exp_done, 2)

                def transposed_hi(n):
                    act.wait_ge(T_moved, n + 1)
                    nc.scalar.activation(T_hi[:, :], tz_bank[:, 0:P], ACT.Copy).then_inc(T_hi_ready, 1)

                def y_hi(n, w, q):
                    act.wait_ge(y_done, Q * n + q + 1)
                    nc.scalar.activation(Y_hi[:, w, Q * q:Q * q + Q].rearrange("p h n -> p (h n)"), y_bank[:, :], ACT.Copy)\
                        .then_inc(Y_hi_ready, 1)

                def z_out(n, w, q):
                    act.wait_ge(z_done, Q * n + q + 1)
                    nc.scalar.activation(Z[:, w, Q * q:Q * q + Q, 0:P], tz_bank[:, :].rearrange("p (h n) -> p h n", h=Q), ACT.Copy)\
                        .then_inc(Z_ready, 1)

                transposed_hi(0)
                for q in range(Q):
                    y_hi(0, 0, q)
                    z_out(0, 0, q)
                transposed_hi(1)
                with act.Fori(0, PAIRS) as i:
                    for u in range(2):
                        n, f, w = 2 * i + u, 2 * i + u + 1, 1 - u
                        for q in range(Q):
                            y_hi(f, w, q)
                            act.wait_ge(shifted, Q * n + q + 1)
                            nc.scalar.activation(probs[:, Q * q:Q * q + Q, :].rearrange("p h n -> p (h n)"), b_bank[q % 2][:, :], ACT.Exp)\
                                .then_inc(exp_done, 1)
                            z_out(f, w, q)
                        transposed_hi(f + 1)

            @block.tensor
            def _(pe):
                pe.wait_ge(primed, 6)

                def transpose(n, w, wait=True):
                    pe.wait_ge(xn_ready, n + 1)
                    if wait:
                        pe.wait_ge(Z_ready, Q * n)
                    nc.tensor.transpose(tz_bank[:, 0:P], xn[:, w, :], k.ident[:, :]).then_inc(T_moved, 1)

                def project_x(n, w, q, wait=True):
                    if q == 0:
                        pe.wait_ge(T_lo_ready, n + 1)
                    if q or wait:
                        pe.wait_ge(Y_lo_ready, Q * n + q)
                    for h in range(Q):
                        last = both_products(nc, y_bank[:, h * P:h * P + P],
                                             [(m[:, Q * q + h, :], t[:, :]) for m, t in ((k.A_hi, T_hi), (k.A_lo, T_hi), (k.A_hi, T_lo))])
                    last.then_inc(y_done, 1)

                def project_context(n, w, q):
                    if q:
                        pe.wait_ge(Z_ready, Q * n + q)
                    else:
                        pe.wait_ge(T_lo_ready, n + 1)
                    last = both_products(nc, tz_bank[:, :],
                                         [(row(c, n), m[:, Q * q:Q * q + Q, :].rearrange("p h n -> p (h n)"))
                                          for c, m in ((k.cT_hi, k.M_hi), (k.cT_hi, k.M_lo), (k.cT_lo, k.M_hi))])
                    last.then_inc(z_done, 1)

                def score_by_query(n, w, q, wait=True):
                    pe.wait_ge(Y_hi_ready, Q * n + q + 1)
                    if q == 1 and wait:
                        pe.wait_ge(maxT_ready, n)
                    elif q >= 2:
                        pe.wait_ge(max_ready, Q * n + q - 1)
                    for h in range(Q):
                        last = nc.tensor.matmul(a_ring(w, q)[:, h * P:h * P + P], Y_hi[:, w, Q * q + h, :], row(k.cT_hi, n),
                                                start=True, stop=True)
                    last.then_inc(scored, 1)

                def transpose_maxima(n, w):
                    pe.wait_ge(max_ready, Q * n + Q)
                    nc.tensor.transpose(a_ring(w, Q)[0:H, 0:P], neg_max[:, :], k.ident[:, :]).then_inc(maxT_moved, 1)

                def score_by_key(n, w, q):
                    out = b_bank[q % 2]
                    if q == 0:
                        pe.wait_ge(maxT_ready, n + 1)
                    pe.wait_ge(exp_done, Q * n + q + 1)
                    for h in range(Q):
                        nc.tensor.matmul(out[:, h * P:h * P + P], k.pick_head[:, Q * q + h, :], neg_maxT[:, :],
                                         start=h == 0, stop=False, skip_group_check=True)
                    last = both_products(nc, out[:, :], [(row(c, n), y[:, w, Q * q:Q * q + Q, :].rearrange("p h n -> p (h n)"))
                                                         for c, y in ((k.cT_hi, Y_hi), (k.cT_hi, Y_lo), (k.cT_lo, Y_hi))], start=False)
                    last.then_inc(shifted, 1)

                def route_transpose(j, v):
                    pe.wait_ge(x_done, 2 * j + v + 3)
                    nc.tensor.transpose(pv_bank[v][:, SIDE:SIDE + P], rows[:, v, 0:P], k.ident[:, :]).then_inc(rowsT_moved, 1)

                def route_logits(j):
                    pe.wait_ge(rowsT_ready, 2 * j + 2)
                    for v in range(2):
                        last = nc.tensor.matmul(pv_bank[0][:, SIDE + v * E:SIDE + v * E + E], rowsT[:, v, :], k.routerT[:, :], start=True, stop=True)
                    last.then_inc(routed, 1)

                def route_ranks(j):
                    pe.wait_ge(chose, 2 * j + 2)
                    for v, parts in enumerate(([(before, 0)], [(before, 1), (ones, 0)], [(ones, 0), (ones, 1)])):
                        last = both_products(nc, pv_bank[0][:, SIDE + v * E:SIDE + v * E + E], [(t[:, :], onehot[:, u, :]) for t, u in parts])
                    last.then_inc(ranked, 1)

                def weigh(n, w, m, route=None):
                    if m % 2 == 0:
                        pe.wait_ge(exp_done, Q * n + m // 2 + 3)
                    pe.wait_ge(summed, 16 * n + 2 * m + 2)
                    if route is not None:
                        if w == 0 and m < 2:
                            route_transpose(route, m)
                        elif w == 0 and m == 2:
                            route_logits(route)
                        elif w == 1 and m == 0:
                            route_ranks(route)
                    for h in range(2):
                        last = nc.tensor.matmul(pv_bank[m % 2][:, h * (P + 1):(h + 1) * (P + 1)], probs[:, 2 * m + h, :],
                                                Z[:, w, 2 * m + h, :], start=True, stop=True)
                    last.then_inc(pv_done, 1)

                transpose(0, 0, wait=False)
                for q in range(Q):
                    project_x(0, 0, q, wait=False)
                    project_context(0, 0, q)
                    score_by_query(0, 0, q, wait=False)
                transpose_maxima(0, 0)
                transpose(1, 1)
                def step(n, u, route=None):
                    f, w = n + 1, 1 - u
                    for q in range(Q):
                        project_x(f, w, q)
                        score_by_key(n, u, q)
                        if q == 1:
                            pe.wait_ge(Z_ready, Q * n + Q)
                        if q:
                            weigh(n, u, 2 * q - 2, route)
                        project_context(f, w, q)
                        if q:
                            weigh(n, u, 2 * q - 1, route)
                        score_by_query(f, w, q)
                    transpose(f + 1, u)
                    weigh(n, u, 2 * Q - 2)
                    weigh(n, u, 2 * Q - 1)
                    transpose_maxima(f, w)

                step(0, 0)
                step(1, 1)
                pe.wait_ge(consts, CONSTS)
                pe.wait_ge(ones_ready, 2)
                with pe.Fori(1, PAIRS) as i:
                    for u in range(2):
                        step(2 * i + u, u, i - 1)
                pe.wait_ge(x_done, B + 2)
                for v in range(2):
                    route_transpose(PAIRS - 1, v)
                route_logits(PAIRS - 1)
                route_ranks(PAIRS - 1)


def second_ffn(nc, k, out):
    U = TILES_STEP
    STEPS = TILES // U
    with ExitStack() as ctx:
        def sb(name, shape, dt=F32):
            return ctx.enter_context(nc.sbuf_tensor("f1_" + name, shape, dt))

        def sem(name):
            return ctx.enter_context(nc.semaphore("f1_" + name))

        rows = sb("rows", [P, TILES + 2 * U, ROW])
        carrier = sb("carrier", [P, 3])
        bn = sb("bn", [P, U, 6])
        stats = sb("stats", [P, U, 2])
        var = sb("var", [P, U])
        half = sb("half", [P, U])
        rstd = sb("rstd", [P, U])
        hn = sb("hn", [P, U, P])
        T_hi = sb("T_hi", [P, U * P], F16)
        T_lo = sb("T_lo", [P, U * P], F16)
        silu = sb("silu", [P, U, I1])
        hid = sb("hid", [P, U, I1])
        hidT = sb("hidT", [P, U, len(CHUNKS), P])
        result = sb("result", [P, U, P])
        taker = sb("taker", [P, 2 + U])
        token = sb("token", [P, U], mybir.dt.uint32)
        t_bank, *bank = [ctx.enter_context(nc.psum_tensor(f"f1_bank{n}", [P, 512], F32)) for n in range(1 + 2 * U)]
        gate_bank, up_bank = bank[:U], bank[U:]
        names = ("primed landed bn_done stats_ready var_ready rstd_ready hn_ready T_moved T_hi_ready T_lo_ready gate_done up_done "
                 "silu_ready hid_ready hidT_moved hidT_ready down_done token_ready result_ready result_free stored").split()
        (primed, landed, bn_done, stats_ready, var_ready, rstd_ready, hn_ready, T_moved, T_hi_ready, T_lo_ready, gate_done, up_done,
         silu_ready, hid_ready, hidT_moved, hidT_ready, down_done, token_ready, result_ready, result_free, stored) = map(sem, names)
        PIECES = ((P, slice(0, 2)), (CHUNKS[2][1], slice(2, 3)))

        def row(n):
            return rows[:, bass.ds(n, 1), 0:P].rearrange("p a n -> p (a n)")

        with nc.Block() as block:
            @block.sync
            def _(sp):
                with sp.Fori(0, STEPS + 2) as i:
                    _, starts = nc.values_load_multi_w_load_instructions(k.tile_row[0:1, bass.ts(i, U)], [mybir.EngineType.SP], min_val=0,
                                                                         max_val=E * REGION + (LISTED - B - 1) * P)
                    sp.wait_ge(landed, 16 * U * (i + 1))
                    for v in range(U):
                        sp.dma_start(rows[:, bass.ds(U * i + v, 1), :].rearrange("p a w -> p (a w)"),
                                     k.expert_rows[bass.ds(starts[v], P), :]).then_inc(landed, 16)

            @block.vector
            def _(dve):
                nc.vector.memset(carrier[:, 0:2], 0.0).then_inc(primed, 1)
                nc.vector.memset(var[:, :], 1.0).then_inc(landed, 16 * U)
                nc.vector.memset(half[:, :], -0.5).then_inc(result_ready, U)
                dve.wait_ge(primed, 1)
                dve.wait_ge(landed, 16 * U)

                def statistics(i):
                    dve.wait_ge(landed, 16 * U * (i + 2))
                    for v in range(U):
                        nc.vector.bn_stats(bn[:, v, :], row(U * i + v)).then_inc(bn_done, 1)
                    alone(nc, dve, carrier, bn_done, U * i + U)
                    for v in range(U):
                        nc.vector.bn_aggr(stats[:, v, :], bn[:, v, :]).then_inc(stats_ready, 1)
                    dve.wait_ge(stats_ready, U * i + U)
                    nc.vector.tensor_scalar(var[:, :], stats[:, :, 1], EPS, None, ALU.add).then_inc(var_ready, 1)

                def normalised(i):
                    dve.wait_ge(rstd_ready, i + 1)
                    for v in range(U):
                        nc.vector.tensor_scalar(hn[:, v, :], row(U * i + v), stats[:, v, 0:1], rstd[:, v:v + 1],
                                                ALU.subtract, ALU.mult).then_inc(hn_ready, 1)

                def transposed_lo(i):
                    dve.wait_ge(T_hi_ready, i + 1)
                    nc.vector.tensor_tensor(T_lo[:, :], t_bank[:, 0:U * P], T_hi[:, :], ALU.subtract).then_inc(T_lo_ready, 1)

                def hidden(i, v):
                    dve.wait_ge(up_done, U * i + v + 1)
                    dve.wait_ge(silu_ready, U * i + v + 1)
                    nc.vector.tensor_tensor(hid[:, v, :], up_bank[v][:, 0:I1], silu[:, v, :], ALU.mult).then_inc(hid_ready, 1)

                statistics(0)
                normalised(0)
                statistics(1)
                transposed_lo(0)
                normalised(1)
                for v in range(U):
                    hidden(0, v)
                with dve.Fori(0, STEPS) as i:
                    transposed_lo(i + 1)
                    statistics(i + 2)
                    dve.wait_ge(result_free, i + 1)
                    nc.vector.tensor_copy(token[:, :], rows[:, bass.ts(i, U), P]).then_inc(token_ready, 1)
                    for v in range(U):
                        dve.wait_ge(down_done, U * i + v + 1)
                        nc.vector.scalar_tensor_tensor(out=result[:, v, :], in0=up_bank[v][:, 0:P], scalar=k.tg[:, 3:4],
                                                       in1=row(U * i + v), op0=ALU.mult, op1=ALU.add).then_inc(result_ready, 1)
                    normalised(i + 2)
                    for v in range(U):
                        hidden(i + 1, v)

            @block.gpsimd
            def _(pool):
                pool.wait_ge(primed, 1)
                nc.gpsimd.memset(taker[:, :], 0.0).then_inc(result_free, 1)
                last_row = pool.to_reg(B * P - 1)
                pool.wait_ge(result_free, 1)

                def deviation(i):
                    pool.wait_ge(var_ready, i + 1)
                    nc.gpsimd.tensor_tensor(rstd[:, :], var[:, :], half[:, :], ALU.pow).then_inc(rstd_ready, 1)

                pool.wait_ge(result_ready, U)
                for i in range(2):
                    deviation(i)
                with pool.Fori(0, STEPS) as i:
                    deviation(i + 2)
                    pool.wait_ge(token_ready, i + 1)
                    for v in range(U):
                        pool.wait_ge(result_ready, U * (i + 1) + v + 1)
                        nc.gpsimd.tensor_tensor(taker[:, 1 + v:2 + v], taker[:, 0:1], taker[:, 0:1], ALU.add)
                        nc.gpsimd.indirect_dma_start(out, bass.IndirectOffsetOnAxis(token[:, v:v + 1], 0), result[:, v, :], None,
                                                     bounds_check=last_row, oob_is_err=False).then_inc(stored, 16)
                    pool.wait_ge(stored, 16 * U * (i + 1))
                    nc.gpsimd.tensor_tensor(taker[:, 1 + U:2 + U], taker[:, 0:1], taker[:, 0:1], ALU.add).then_inc(result_free, 1)
                pool.wait_ge(stored, 16 * TILES)

            @block.scalar
            def _(act):
                act.wait_ge(primed, 1)
                nc.scalar.activation(carrier[:, 2:3], carrier[:, 0:1], ACT.Silu)

                def transposed_hi(i):
                    act.wait_ge(T_moved, i + 1)
                    nc.scalar.activation(T_hi[:, :], t_bank[:, 0:U * P], ACT.Copy).then_inc(T_hi_ready, 1)

                def gated(i, v):
                    act.wait_ge(gate_done, U * i + v + 1)
                    nc.scalar.activation(silu[:, v, :], gate_bank[v][:, 0:I1], ACT.Silu).then_inc(silu_ready, 1)

                def hidden_transposed(i, v):
                    act.wait_ge(hidT_moved, U * i + v + 1)
                    for height, c in PIECES:
                        nc.scalar.activation(hidT[0:height, v, c, :], gate_bank[v][0:height, 0:len(CHUNKS) * P].rearrange("p (c n) -> p c n", n=P)[:, c, :],
                                             ACT.Copy).then_inc(hidT_ready, 1)

                transposed_hi(0)
                for v in range(U):
                    gated(0, v)
                with act.Fori(0, STEPS) as i:
                    transposed_hi(i + 1)
                    for v in range(U):
                        hidden_transposed(i, v)
                    for v in range(U):
                        gated(i + 1, v)

            @block.tensor
            def _(pe):
                def experts(i):
                    packed = pe.value_load(k.tile_expert[0:1, bass.ds(i, 1)], min_val=0, max_val=E ** (2 * U) - 1)
                    values = [pe.snap((packed >> (3 * n)) & (E - 1)) for n in range(2 * U)]
                    return values[:U], values[U:]

                def transpose(i):
                    pe.wait_ge(hn_ready, U * i + U)
                    for v in range(U):
                        last = nc.tensor.transpose(t_bank[:, v * P:v * P + P], hn[:, v, :], k.ident[:, :])
                    last.then_inc(T_moved, 1)

                def first_products(i, v, e):
                    if v == 0:
                        pe.wait_ge(T_lo_ready, i + 1)
                    T = [t[:, v * P:v * P + P] for t in (T_hi, T_lo)]
                    for hi, lo, bank, done in ((k.gate_hi, k.gate_lo, gate_bank, gate_done), (k.up_hi, k.up_lo, up_bank, up_done)):
                        if bank is up_bank:
                            pe.wait_ge(result_ready, U * i + v + 1)
                        weights = [w[:, bass.ds(e, 1), :].rearrange("p a n -> p (a n)") for w in (hi, lo)]
                        both_products(nc, bank[v][:, 0:I1], [(T[0], weights[0]), (T[0], weights[1]), (T[1], weights[0])]).then_inc(done, 1)

                def transpose_hidden(i, v):
                    pe.wait_ge(hid_ready, U * i + v + 1)
                    for c, (c0, height) in enumerate(CHUNKS):
                        last = nc.tensor.transpose(gate_bank[v][0:height, c * P:c * P + P], hid[:, v, c0:c0 + height], k.ident[:, :])
                    last.then_inc(hidT_moved, 1)

                def second_product(i, v, e):
                    pe.wait_ge(hidT_ready, 2 * (U * i + v) + 2)
                    for c, (_, height) in enumerate(CHUNKS):
                        last = nc.tensor.matmul(up_bank[v][:, 0:P], hidT[0:height, v, c, :],
                                                k.downT[0:height, c, bass.ds(e, 1), :].rearrange("p a n -> p (a n)"),
                                                start=c == 0, stop=c == len(CHUNKS) - 1)
                    last.then_inc(down_done, 1)

                now, _ = experts(0)
                transpose(0)
                for v in range(U):
                    first_products(0, v, now[v])
                with pe.Fori(0, STEPS) as i:
                    now, coming = experts(i)
                    transpose(i + 1)
                    for v in range(U):
                        transpose_hidden(i, v)
                    for v in range(U):
                        second_product(i, v, now[v])
                    for v in range(U):
                        first_products(i + 1, v, coming[v])


def build(nc, A, out):
    with ExitStack() as ctx:
        k = Setup()
        with ExitStack() as raw:
            prepare(nc, ctx, raw, A, k)
            first_attention(nc, A, k)
            prepare_second_layer(nc, k)
        first_ffn(nc, k)
        second_attention(nc, k)
        second_ffn(nc, k, out.rearrange("b t d -> (b t) d"))


_NAMES = ['x', 'ctx_1024', 'g_xattn', 'g_ffn', 'L0_xattn_Wq', 'L0_xattn_bq', 'L0_xattn_Wk', 'L0_xattn_bk', 'L0_xattn_Wv',
          'L0_xattn_bv', 'L0_xattn_Wo', 'L0_xattn_bo', 'L0_ffn_ln_scale', 'L0_ffn_ln_bias', 'L0_ffn_attn_w', 'L0_ffn_attn_b',
          'L0_ffn_w1', 'L0_ffn_b1', 'L0_ffn_w2', 'L0_ffn_b2', 'L0_ffn_next_w', 'L0_ffn_next_b', 'L1_xattn_Wq', 'L1_xattn_Wk',
          'L1_xattn_Wv', 'L1_xattn_Wo', 'L1_xattn_bo', 'L1_ffn_router_w', 'L1_ffn_gate_w', 'L1_ffn_up_w', 'L1_ffn_down_w']


def kernel(**inputs):
    import concourse.bacc as bacc
    from concourse.bass_utils import run_bass_kernel_spmd

    nc = bacc.Bacc("TRN2", target_bir_lowering=False, num_devices=1)
    arrays, A = {}, {}
    for name in _NAMES:
        a = np.ascontiguousarray(inputs[name])
        arrays["in_" + name] = a
        A[name] = nc.dram_tensor("in_" + name, a.shape, mybir.dt.from_np(a.dtype), kind="ExternalInput").ap()
    out = nc.dram_tensor("out", (B, P, P), F32, kind="ExternalOutput").ap()
    build(nc, A, out)
    r = run_bass_kernel_spmd(nc, [arrays], core_ids=[0])
    return r.results[0]["out"]
```
